# Optimizing a Trainium2 kernel written in Bass

```python
import numpy as np
import jax
import jax.numpy as jnp

def _softmax(x, axis=-1):
    return jax.nn.softmax(x, axis=axis)

def _gelu(x):
    return jax.nn.gelu(x, approximate=True)

def _silu(x):
    return jax.nn.silu(x)

def _sigmoid(x):
    return jax.nn.sigmoid(x)

def _layernorm(x, axis=-1, eps=1e-05):
    m = jnp.mean(x, axis=axis, keepdims=True)
    v = jnp.var(x, axis=axis, keepdims=True)
    return (x - m) / jnp.sqrt(v + eps)

def _scatter_add(tgt, idx, src, axis=0):
    return tgt.at[idx].add(src)

def _segment_sum(src, seg, n):
    return jax.ops.segment_sum(src, seg, n)
kernel_name = 'mk_decoder_postln_d2_seqx_r8_7f5523'

def setup_inputs(seed: int=0):
    np.random.seed(seed)
    _w = jnp.asarray

    def _rec_inputs():
        import jax
        import jax.numpy as jnp
        _rk = jax.random.key(seed)
        x = -0.0002928 + 1 * jax.random.normal(jax.random.fold_in(_rk, 1), (16, 256, 128), jnp.float32)
        _lenS = 256 - jax.random.randint(jax.random.fold_in(_rk, 7), (16,), 0, max(1, 256 // 4) + 1, jnp.int32)
        _lenS2 = 1601 - jax.random.randint(jax.random.fold_in(_rk, 8), (16,), 0, max(1, 1601 // 4) + 1, jnp.int32)
        _ctx_768P = jax.random.normal(jax.random.fold_in(_rk, 11), (16, 16, 96), jnp.float32)
        _ctx_768c = jax.random.dirichlet(jax.random.fold_in(_rk, 511), 0.3 * jnp.ones((16,), jnp.float32), (16, 1601))
        _ctx_768t = jnp.einsum('bsk,bkd->bsd', _ctx_768c, _ctx_768P)
        _ctx_768t = _ctx_768t * jax.lax.rsqrt(jnp.mean(jnp.square(_ctx_768t)) + 1e-12) * 0.953939
        ctx_768 = 2.09791e-05 + 1.00001 * (_ctx_768t + 0.3 * jax.random.normal(jax.random.fold_in(_rk, 611), (16, 1601, 96), jnp.float32))
        return (x, ctx_768)
    x, ctx_768 = _rec_inputs()

    def _L0_attn_setup():
        import jax, jax.numpy as jnp
        import numpy as np
        import math
        INPUT_DIM = 128
        EMBED_DIM = 128
        NUM_HEADS = 16
        HEAD_DIM = EMBED_DIM // NUM_HEADS
        key = jax.random.key(seed)
        k_x, k_qkv, k_out_w, k_out_b = jax.random.split(key, 4)
        x = jax.random.normal(k_x, (1, 512, INPUT_DIM), dtype=jnp.float32)
        s1 = 1.0 / math.sqrt(INPUT_DIM)
        s2 = 1.0 / math.sqrt(EMBED_DIM)
        qkv_w = jax.random.uniform(k_qkv, (3 * EMBED_DIM, INPUT_DIM), jnp.float32, -s1, s1)
        out_w = jax.random.uniform(k_out_w, (EMBED_DIM, EMBED_DIM), jnp.float32, -s2, s2)
        out_b = jax.random.uniform(k_out_b, (EMBED_DIM,), jnp.float32, -s2, s2)
        return {'x': x, 'qkv_w': qkv_w, 'out_w': out_w, 'out_b': out_b}
    _L0_attn_all = _L0_attn_setup()
    _L0_attn_in = {k: v for k, v in _L0_attn_all.items() if k in ('qkv_w', 'out_w', 'out_b')}
    del _L0_attn_all

    def _L0_xattn_setup():
        import jax, jax.numpy as jnp
        import numpy as np
        N_HEADS = 16
        DIMS = 128
        D_CTX = 96
        HEAD = DIMS // N_HEADS
        key = jax.random.key(seed)
        ks = jax.random.split(key, 10)
        s_q = 1.0 / np.sqrt(DIMS)
        s_c = 1.0 / np.sqrt(D_CTX)
        return {'x': jax.random.normal(ks[0], (2, 256, DIMS), jnp.float32), 'context': jax.random.normal(ks[1], (2, 256, D_CTX), jnp.float32), 'w_q': jax.random.normal(ks[2], (DIMS, DIMS), jnp.float32) * s_q, 'b_q': jax.random.normal(ks[3], (DIMS,), jnp.float32) * 0.01, 'w_k': jax.random.normal(ks[4], (D_CTX, DIMS), jnp.float32) * s_c, 'b_k': jax.random.normal(ks[5], (DIMS,), jnp.float32) * 0.01, 'w_v': jax.random.normal(ks[6], (D_CTX, DIMS), jnp.float32) * s_c, 'b_v': jax.random.normal(ks[7], (DIMS,), jnp.float32) * 0.01, 'w_o': jax.random.normal(ks[8], (DIMS, DIMS), jnp.float32) * s_q, 'b_o': jax.random.normal(ks[9], (DIMS,), jnp.float32) * 0.01}
    _L0_xattn_all = _L0_xattn_setup()
    _L0_xattn_in = {k: v for k, v in _L0_xattn_all.items() if k in ('w_q', 'b_q', 'w_k', 'b_k', 'w_v', 'b_v', 'w_o', 'b_o')}
    del _L0_xattn_all

    def _L0_ffn_setup():
        import jax, jax.numpy as jnp
        import numpy as np
        HIDDEN = 128
        MOE_INTER = 64
        SHARED_INTER = 256
        N_EXPERTS = 32
        TOP_K = 6
        N_GROUP = 8
        TOPK_GROUP = 4
        ROUTED_SCALE = 2.5

        def _relu2(x):
            return jnp.square(jax.nn.relu(x))

        def _router(x, gate_w, e_bias):
            T = x.shape[0]
            logits = x.astype(jnp.float32) @ gate_w.astype(jnp.float32).T
            scores = jax.nn.sigmoid(logits)
            sc = scores + e_bias[None, :]
            g = sc.reshape(T, N_GROUP, N_EXPERTS // N_GROUP)
            group_scores = jax.lax.top_k(g, 2)[0].sum(-1)
            group_idx = jax.lax.top_k(group_scores, TOPK_GROUP)[1]
            group_mask = jnp.zeros_like(group_scores).at[jnp.arange(T)[:, None], group_idx].set(1.0)
            score_mask = jnp.repeat(group_mask, N_EXPERTS // N_GROUP, axis=1)
            masked = jnp.where(score_mask > 0, sc, 0.0)
            topk_idx = jax.lax.stop_gradient(jax.lax.top_k(masked, TOP_K)[1])
            topk_w = jnp.take_along_axis(scores, topk_idx, axis=1)
            topk_w = topk_w / (topk_w.sum(-1, keepdims=True) + 1e-20)
            topk_w = topk_w * ROUTED_SCALE
            return (topk_idx, topk_w)
        if __name__ == '__main__':
            out = reference(**setup_inputs())
            print(out.shape, out.dtype)
        key = jax.random.key(seed)
        ks = jax.random.split(key, 6)
        s = 0.02
        return {'hidden_states': jax.random.normal(ks[0], (2, 128, HIDDEN), jnp.float32), 'gate_w': jax.random.normal(ks[1], (N_EXPERTS, HIDDEN), jnp.float32) * s, 'e_bias': jnp.zeros((N_EXPERTS,), jnp.float32), 'up_w': jax.random.normal(ks[2], (N_EXPERTS, MOE_INTER, HIDDEN), jnp.float32) * s, 'down_w': jax.random.normal(ks[3], (N_EXPERTS, HIDDEN, MOE_INTER), jnp.float32) * s, 'shared_up_w': jax.random.normal(ks[4], (SHARED_INTER, HIDDEN), jnp.float32) * s, 'shared_down_w': jax.random.normal(ks[5], (HIDDEN, SHARED_INTER), jnp.float32) * s}
    _L0_ffn_all = _L0_ffn_setup()
    _L0_ffn_in = {k: v for k, v in _L0_ffn_all.items() if k in ('gate_w', 'e_bias', 'up_w', 'down_w', 'shared_up_w', 'shared_down_w')}
    del _L0_ffn_all

    def _L1_attn_setup():
        import jax, jax.numpy as jnp
        import numpy as np
        B, T, H, N = (4, 256, 128, 16)
        DT_MIN, DT_MAX = (0.001, 0.1)
        A_INIT_MIN, A_INIT_MAX = (0.5, 2.0)

        def _inv_softplus(x):
            return x + jnp.log(-jnp.expm1(-x))

        def _reference_tuple_inner(x, A_log, B_mat, C_mat, D_vec, W_dt, b_dt):
            u = x
            A = -jnp.exp(A_log)
            dt = jax.nn.softplus(jnp.einsum('bth,gh->btg', u, W_dt) + b_dt)
            state0 = jnp.zeros((u.shape[0], A_log.shape[0], A_log.shape[1]), dtype=u.dtype)

            def step(state, inp):
                dt_t, u_t = inp
                dtA = dt_t[..., None]
                A_bar = jnp.exp(dtA * A)
                state = A_bar * state + dtA * B_mat * u_t[..., None]
                y_t = jnp.einsum('bhn,hn->bh', state, C_mat) + D_vec * u_t
                return (state, y_t)
            state_final, ys = jax.lax.scan(step, state0, (dt.transpose(1, 0, 2), u.transpose(1, 0, 2)))
            out = ys.transpose(1, 0, 2)
            return (out, state_final)
        key = jax.random.key(seed)
        kx, ka, kb, kc, kw, kdt = jax.random.split(key, 6)
        x = jax.random.normal(kx, (B, T, H), dtype=jnp.float32)
        A_log = jax.random.uniform(ka, (H, N), minval=np.log(A_INIT_MIN), maxval=np.log(A_INIT_MAX), dtype=jnp.float32)
        B_mat = 0.02 * jax.random.normal(kb, (H, N), dtype=jnp.float32)
        C_mat = 0.02 * jax.random.normal(kc, (H, N), dtype=jnp.float32)
        D_vec = jnp.ones((H,), dtype=jnp.float32)
        W_dt = 0.02 * jax.random.normal(kw, (H, H), dtype=jnp.float32)
        b_dt = _inv_softplus(jax.random.uniform(kdt, (H,), minval=DT_MIN, maxval=DT_MAX, dtype=jnp.float32))
        return {'x': x, 'A_log': A_log, 'B_mat': B_mat, 'C_mat': C_mat, 'D_vec': D_vec, 'W_dt': W_dt, 'b_dt': b_dt}
    _L1_attn_all = _L1_attn_setup()
    _L1_attn_in = {k: v for k, v in _L1_attn_all.items() if k in ('A_log', 'B_mat', 'C_mat', 'D_vec', 'W_dt', 'b_dt')}
    del _L1_attn_all

    def _L1_xattn_setup():
        import jax, jax.numpy as jnp
        import numpy as np
        N_HEADS = 16
        key = jax.random.key(seed)
        ks = jax.random.split(key, 8)
        b, l, m = (8, 128, 128)
        d_embed, d_cross = (128, 96)
        s_q = 1.0 / np.sqrt(d_embed)
        s_kv = 1.0 / np.sqrt(d_cross)
        return {'x': jax.random.normal(ks[0], (b, l, d_embed), jnp.float32), 'y': jax.random.normal(ks[1], (b, m, d_cross), jnp.float32), 'Wq': jax.random.normal(ks[2], (d_embed, d_embed), jnp.float32) * s_q, 'bq': jax.random.normal(ks[3], (d_embed,), jnp.float32) * 0.01, 'Wkv': jax.random.normal(ks[4], (2 * d_embed, d_cross), jnp.float32) * s_kv, 'bkv': jax.random.normal(ks[5], (2 * d_embed,), jnp.float32) * 0.01, 'Wo': jax.random.normal(ks[6], (d_embed, d_embed), jnp.float32) * s_q, 'bo': jax.random.normal(ks[7], (d_embed,), jnp.float32) * 0.01}
    _L1_xattn_all = _L1_xattn_setup()
    _L1_xattn_in = {k: v for k, v in _L1_xattn_all.items() if k in ('Wq', 'bq', 'Wkv', 'bkv', 'Wo', 'bo')}
    del _L1_xattn_all

    def _L1_ffn_setup():
        import jax, jax.numpy as jnp
        import numpy as np
        BITS = 8
        LORA_RANK = 16
        LORA_ALPHA = 32
        SCALING = LORA_ALPHA / LORA_RANK

        def fake_quant_weight(w, bits=BITS):
            qmax = 2.0 ** (bits - 1) - 1
            scale = jnp.max(jnp.abs(w)) / qmax
            wq = jnp.clip(jnp.round(w / scale), -qmax - 1, qmax) * scale
            return w + jax.lax.stop_gradient(wq - w)

        def qat_lora_linear(x, W, b, A, B):
            Wq = fake_quant_weight(W)
            base = jnp.einsum('bsi,oi->bso', x, Wq) + b
            lora = jnp.einsum('bsr,or->bso', jnp.einsum('bsi,ri->bsr', x, A), B)
            return base + SCALING * lora
        key = jax.random.key(seed)
        ks = jax.random.split(key, 9)
        d, f = (128, 512)
        s_in = 1.0 / np.sqrt(d)
        s_ff = 1.0 / np.sqrt(f)
        return {'hidden_states': jax.random.normal(ks[0], (4, 256, d), jnp.float32), 'W_fc': jax.random.normal(ks[1], (f, d), jnp.float32) * s_in, 'b_fc': jnp.zeros((f,), jnp.float32), 'A_fc': jax.random.normal(ks[2], (LORA_RANK, d), jnp.float32) * s_in, 'B_fc': jnp.zeros((f, LORA_RANK), jnp.float32), 'W_proj': jax.random.normal(ks[3], (d, f), jnp.float32) * s_ff, 'b_proj': jnp.zeros((d,), jnp.float32), 'A_proj': jax.random.normal(ks[4], (LORA_RANK, f), jnp.float32) * s_ff, 'B_proj': jnp.zeros((d, LORA_RANK), jnp.float32)}
    _L1_ffn_all = _L1_ffn_setup()
    _L1_ffn_in = {k: v for k, v in _L1_ffn_all.items() if k in ('W_fc', 'b_fc', 'A_fc', 'B_fc', 'W_proj', 'b_proj', 'A_proj', 'B_proj')}
    del _L1_ffn_all
    return {'x': x, 'ctx_768': ctx_768, 'L0_attn_qkv_w': _L0_attn_in['qkv_w'], 'L0_attn_out_w': _L0_attn_in['out_w'], 'L0_attn_out_b': _L0_attn_in['out_b'], 'L0_xattn_w_q': _L0_xattn_in['w_q'], 'L0_xattn_b_q': _L0_xattn_in['b_q'], 'L0_xattn_w_k': _L0_xattn_in['w_k'], 'L0_xattn_b_k': _L0_xattn_in['b_k'], 'L0_xattn_w_v': _L0_xattn_in['w_v'], 'L0_xattn_b_v': _L0_xattn_in['b_v'], 'L0_xattn_w_o': _L0_xattn_in['w_o'], 'L0_xattn_b_o': _L0_xattn_in['b_o'], 'L0_ffn_gate_w': _L0_ffn_in['gate_w'], 'L0_ffn_e_bias': _L0_ffn_in['e_bias'], 'L0_ffn_up_w': _L0_ffn_in['up_w'], 'L0_ffn_down_w': _L0_ffn_in['down_w'], 'L0_ffn_shared_up_w': _L0_ffn_in['shared_up_w'], 'L0_ffn_shared_down_w': _L0_ffn_in['shared_down_w'], 'L1_attn_A_log': _L1_attn_in['A_log'], 'L1_attn_B_mat': _L1_attn_in['B_mat'], 'L1_attn_C_mat': _L1_attn_in['C_mat'], 'L1_attn_D_vec': _L1_attn_in['D_vec'], 'L1_attn_W_dt': _L1_attn_in['W_dt'], 'L1_attn_b_dt': _L1_attn_in['b_dt'], 'L1_xattn_Wq': _L1_xattn_in['Wq'], 'L1_xattn_bq': _L1_xattn_in['bq'], 'L1_xattn_Wkv': _L1_xattn_in['Wkv'], 'L1_xattn_bkv': _L1_xattn_in['bkv'], 'L1_xattn_Wo': _L1_xattn_in['Wo'], 'L1_xattn_bo': _L1_xattn_in['bo'], 'L1_ffn_W_fc': _L1_ffn_in['W_fc'], 'L1_ffn_b_fc': _L1_ffn_in['b_fc'], 'L1_ffn_A_fc': _L1_ffn_in['A_fc'], 'L1_ffn_B_fc': _L1_ffn_in['B_fc'], 'L1_ffn_W_proj': _L1_ffn_in['W_proj'], 'L1_ffn_b_proj': _L1_ffn_in['b_proj'], 'L1_ffn_A_proj': _L1_ffn_in['A_proj'], 'L1_ffn_B_proj': _L1_ffn_in['B_proj']}

def reference(x, ctx_768, L0_attn_qkv_w, L0_attn_out_w, L0_attn_out_b, L0_xattn_w_q, L0_xattn_b_q, L0_xattn_w_k, L0_xattn_b_k, L0_xattn_w_v, L0_xattn_b_v, L0_xattn_w_o, L0_xattn_b_o, L0_ffn_gate_w, L0_ffn_e_bias, L0_ffn_up_w, L0_ffn_down_w, L0_ffn_shared_up_w, L0_ffn_shared_down_w, L1_attn_A_log, L1_attn_B_mat, L1_attn_C_mat, L1_attn_D_vec, L1_attn_W_dt, L1_attn_b_dt, L1_xattn_Wq, L1_xattn_bq, L1_xattn_Wkv, L1_xattn_bkv, L1_xattn_Wo, L1_xattn_bo, L1_ffn_W_fc, L1_ffn_b_fc, L1_ffn_A_fc, L1_ffn_B_fc, L1_ffn_W_proj, L1_ffn_b_proj, L1_ffn_A_proj, L1_ffn_B_proj):
    import jax
    import jax.numpy as jnp

    def _L0_attn_ref(x, qkv_w, out_w, out_b):
        import jax, jax.numpy as jnp
        import numpy as np
        import math
        INPUT_DIM = 128
        EMBED_DIM = 128
        NUM_HEADS = 16
        HEAD_DIM = EMBED_DIM // NUM_HEADS
        B, N, C = x.shape
        qkv = jnp.einsum('bnc,ec->bne', x, qkv_w)
        q = qkv[:, :, 0:EMBED_DIM].reshape(B, N, NUM_HEADS, HEAD_DIM)
        k = qkv[:, :, EMBED_DIM:2 * EMBED_DIM].reshape(B, N, NUM_HEADS, HEAD_DIM)
        v = qkv[:, :, 2 * EMBED_DIM:].reshape(B, N, NUM_HEADS, HEAD_DIM)
        scores = jnp.einsum('bihd,bjhd->bhij', q, k) / jnp.sqrt(jnp.float32(HEAD_DIM))
        attn = jax.nn.softmax(scores, axis=-1)
        out = jnp.einsum('bhik,bkhd->bhid', attn, v)
        out = out.transpose(0, 2, 1, 3).reshape(B, N, EMBED_DIM)
        return jnp.einsum('bne,fe->bnf', out, out_w) + out_b

    def _L0_xattn_ref(x, context, w_q, b_q, w_k, b_k, w_v, b_v, w_o, b_o):
        import jax, jax.numpy as jnp
        import numpy as np
        N_HEADS = 16
        DIMS = 128
        D_CTX = 96
        HEAD = DIMS // N_HEADS
        B, Lq, D = x.shape
        q = x @ w_q + b_q
        k = context @ w_k + b_k
        v = context @ w_v + b_v
        q = q.reshape(B, Lq, N_HEADS, HEAD)
        k = k.reshape(B, -1, N_HEADS, HEAD)
        v = v.reshape(B, -1, N_HEADS, HEAD)
        scale = 1.0 / np.sqrt(HEAD).astype(np.float32)
        scores = jnp.einsum('bqhd,bkhd->bhqk', q, k) * scale
        weights = jax.nn.softmax(scores, axis=-1)
        out = jnp.einsum('bhqk,bkhd->bqhd', weights, v).reshape(B, Lq, D)
        return out @ w_o + b_o

    def _L0_ffn_ref(hidden_states, gate_w, e_bias, up_w, down_w, shared_up_w, shared_down_w):
        import jax, jax.numpy as jnp
        import numpy as np
        HIDDEN = 128
        MOE_INTER = 64
        SHARED_INTER = 256
        N_EXPERTS = 32
        TOP_K = 6
        N_GROUP = 8
        TOPK_GROUP = 4
        ROUTED_SCALE = 2.5

        def _relu2(x):
            return jnp.square(jax.nn.relu(x))

        def _router(x, gate_w, e_bias):
            T = x.shape[0]
            logits = x.astype(jnp.float32) @ gate_w.astype(jnp.float32).T
            scores = jax.nn.sigmoid(logits)
            sc = scores + e_bias[None, :]
            g = sc.reshape(T, N_GROUP, N_EXPERTS // N_GROUP)
            group_scores = jax.lax.top_k(g, 2)[0].sum(-1)
            group_idx = jax.lax.top_k(group_scores, TOPK_GROUP)[1]
            group_mask = jnp.zeros_like(group_scores).at[jnp.arange(T)[:, None], group_idx].set(1.0)
            score_mask = jnp.repeat(group_mask, N_EXPERTS // N_GROUP, axis=1)
            masked = jnp.where(score_mask > 0, sc, 0.0)
            topk_idx = jax.lax.stop_gradient(jax.lax.top_k(masked, TOP_K)[1])
            topk_w = jnp.take_along_axis(scores, topk_idx, axis=1)
            topk_w = topk_w / (topk_w.sum(-1, keepdims=True) + 1e-20)
            topk_w = topk_w * ROUTED_SCALE
            return (topk_idx, topk_w)
        if __name__ == '__main__':
            out = reference(**setup_inputs())
            print(out.shape, out.dtype)
        B, S, H = hidden_states.shape
        x = hidden_states.reshape(-1, H)
        T = x.shape[0]
        topk_idx, topk_w = _router(x, gate_w, e_bias)
        combine = jnp.zeros((T, N_EXPERTS), topk_w.dtype).at[jnp.arange(T)[:, None], topk_idx].add(topk_w)
        h = _relu2(jnp.einsum('th,eih->tei', x, up_w))
        h = h * combine[:, :, None]
        moe_out = jnp.einsum('tei,ehi->th', h, down_w)
        shared = _relu2(x @ shared_up_w.T) @ shared_down_w.T
        return (moe_out + shared).reshape(B, S, H)

    def _L1_attn_ref(x, A_log, B_mat, C_mat, D_vec, W_dt, b_dt):
        import jax, jax.numpy as jnp
        import numpy as np
        B, T, H, N = (4, 256, 128, 16)
        DT_MIN, DT_MAX = (0.001, 0.1)
        A_INIT_MIN, A_INIT_MAX = (0.5, 2.0)

        def _inv_softplus(x):
            return x + jnp.log(-jnp.expm1(-x))

        def _reference_tuple_inner(x, A_log, B_mat, C_mat, D_vec, W_dt, b_dt):
            u = x
            A = -jnp.exp(A_log)
            dt = jax.nn.softplus(jnp.einsum('bth,gh->btg', u, W_dt) + b_dt)
            state0 = jnp.zeros((u.shape[0], A_log.shape[0], A_log.shape[1]), dtype=u.dtype)

            def step(state, inp):
                dt_t, u_t = inp
                dtA = dt_t[..., None]
                A_bar = jnp.exp(dtA * A)
                state = A_bar * state + dtA * B_mat * u_t[..., None]
                y_t = jnp.einsum('bhn,hn->bh', state, C_mat) + D_vec * u_t
                return (state, y_t)
            state_final, ys = jax.lax.scan(step, state0, (dt.transpose(1, 0, 2), u.transpose(1, 0, 2)))
            out = ys.transpose(1, 0, 2)
            return (out, state_final)
        return _reference_tuple_inner(x, A_log, B_mat, C_mat, D_vec, W_dt, b_dt)[0]

    def _L1_xattn_ref(x, y, Wq, bq, Wkv, bkv, Wo, bo):
        import jax, jax.numpy as jnp
        import numpy as np
        N_HEADS = 16
        b, l, d = x.shape
        m = y.shape[1]
        h = N_HEADS
        dh = d // h
        q = (jnp.einsum('bld,ed->ble', x, Wq) + bq).reshape(b, l, h, dh)
        kv = (jnp.einsum('bmc,ec->bme', y, Wkv) + bkv).reshape(b, m, h, 2 * dh)
        k, v = (kv[..., :dh], kv[..., dh:])
        scale = 1.0 / jnp.sqrt(jnp.asarray(dh, x.dtype))
        att = jax.nn.softmax(jnp.einsum('blhd,bmhd->blmh', q, k) * scale, axis=2)
        out = jnp.einsum('blmh,bmhd->blhd', att, v).reshape(b, l, d)
        return jnp.einsum('bld,ed->ble', out, Wo) + bo

    def _L1_ffn_ref(hidden_states, W_fc, b_fc, A_fc, B_fc, W_proj, b_proj, A_proj, B_proj):
        import jax, jax.numpy as jnp
        import numpy as np
        BITS = 8
        LORA_RANK = 16
        LORA_ALPHA = 32
        SCALING = LORA_ALPHA / LORA_RANK

        def fake_quant_weight(w, bits=BITS):
            qmax = 2.0 ** (bits - 1) - 1
            scale = jnp.max(jnp.abs(w)) / qmax
            wq = jnp.clip(jnp.round(w / scale), -qmax - 1, qmax) * scale
            return w + jax.lax.stop_gradient(wq - w)

        def qat_lora_linear(x, W, b, A, B):
            Wq = fake_quant_weight(W)
            base = jnp.einsum('bsi,oi->bso', x, Wq) + b
            lora = jnp.einsum('bsr,or->bso', jnp.einsum('bsi,ri->bsr', x, A), B)
            return base + SCALING * lora
        h = qat_lora_linear(hidden_states, W_fc, b_fc, A_fc, B_fc)
        h = jax.nn.gelu(h, approximate=False)
        h = qat_lora_linear(h, W_proj, b_proj, A_proj, B_proj)
        return h
    x = _layernorm(x + _L0_attn_ref(x, L0_attn_qkv_w, L0_attn_out_w, L0_attn_out_b), axis=-1)
    x = _layernorm(x + _L0_xattn_ref(x, ctx_768, L0_xattn_w_q, L0_xattn_b_q, L0_xattn_w_k, L0_xattn_b_k, L0_xattn_w_v, L0_xattn_b_v, L0_xattn_w_o, L0_xattn_b_o), axis=-1)
    x = _layernorm(x + _L0_ffn_ref(x, L0_ffn_gate_w, L0_ffn_e_bias, L0_ffn_up_w, L0_ffn_down_w, L0_ffn_shared_up_w, L0_ffn_shared_down_w), axis=-1)
    x = _layernorm(x + _L1_attn_ref(x, L1_attn_A_log, L1_attn_B_mat, L1_attn_C_mat, L1_attn_D_vec, L1_attn_W_dt, L1_attn_b_dt), axis=-1)
    x = _layernorm(x + _L1_xattn_ref(x, ctx_768, L1_xattn_Wq, L1_xattn_bq, L1_xattn_Wkv, L1_xattn_bkv, L1_xattn_Wo, L1_xattn_bo), axis=-1)
    x = _layernorm(x + _L1_ffn_ref(x, L1_ffn_W_fc, L1_ffn_b_fc, L1_ffn_A_fc, L1_ffn_B_fc, L1_ffn_W_proj, L1_ffn_b_proj, L1_ffn_A_proj, L1_ffn_B_proj), axis=-1)
    return x

_drawn_inputs = setup_inputs


def setup_inputs(seed=0):
    import zlib

    import numpy as np

    out = dict(_drawn_inputs(seed))
    spreads = {'L0_ffn_e_bias': (0.0, 0.8),
     'L1_attn_D_vec': (1.0, 0.2),
     'L1_ffn_b_fc': (0.0, 0.1),
     'L1_ffn_B_fc': (0.0, 0.1),
     'L1_ffn_b_proj': (0.0, 0.1),
     'L1_ffn_B_proj': (0.0, 0.1)}
    factors = {'L0_xattn_b_q': 8.0,
     'L0_xattn_b_k': 64.0,
     'L0_xattn_b_v': 7.206,
     'L0_xattn_b_o': 6.304,
     'L0_ffn_gate_w': 8.0,
     'L0_ffn_up_w': 6.831,
     'L0_ffn_down_w': 6.142,
     'L0_ffn_shared_up_w': 3.428,
     'L0_ffn_shared_down_w': 3.017,
     'L1_attn_A_log': 64.0,
     'L1_attn_B_mat': 64.0,
     'L1_attn_C_mat': 64.0,
     'L1_attn_W_dt': 64.0,
     'L1_attn_b_dt': 64.0,
     'L1_xattn_bq': 26.798,
     'L1_xattn_bkv': 6.087,
     'L1_xattn_bo': 6.412}
    for name, (base, spread) in spreads.items():
        noise = np.random.default_rng([zlib.crc32(name.encode()), seed]).standard_normal(out[name].shape)
        drawn = base * np.exp(spread * noise) if base else spread * noise
        out[name] = jnp.asarray(drawn.astype(out[name].dtype))
    for name, factor in factors.items():
        out[name] = (out[name] * factor).astype(out[name].dtype)
    return out
```

```python
from contextlib import ExitStack

import numpy as np

import concourse.bass as bass
from concourse import mybir

F32 = mybir.dt.float32
BF16 = mybir.dt.bfloat16
ALU = mybir.AluOpType
ACT = mybir.ActivationFunctionType
AX = mybir.AxisListType

P = 128
B, S, D = 16, 256, 128
H, DH = 16, 8
NKV, DC = 1601, 96
QT = S // P
NT = B * QT
EPS = 1e-5
SCALE = 1.0 / float(np.sqrt(np.float32(DH)))
PARTS = 3
STACK = PARTS * PARTS * DH
MROW = 96
KROWS = MROW + PARTS
GROUPS = 2
GH = H // GROUPS
GP = GH * DH


def heads_to_groups(ap):
    return ap.rearrange("p (g l d) -> p g d l", g=GROUPS, l=GH, d=DH)


def as_groups(ap):
    return ap.rearrange("p (g d l) -> p g d l", g=GROUPS, l=GH, d=DH)


class Attention:

    def __init__(self, name, keys):
        self.name = name
        self.keys = keys
        self.cross = keys != S
        self.chunks = [(s, min(P, keys - s)) for s in range(0, keys, P)]
        self.nch = len(self.chunks)
        self.units = (self.nch + 1) // 2
        self.nb = H * self.units
        self.quads = min(4, self.nch)
        if self.cross:
            self.block = (keys + 3) // 4
            self.block_step = (keys - 1) // 4
            self.max_units = QT * 2
            self.ahead, self.ahead_rows = 2, 1
            assert 3 * self.block_step + self.block == keys
            self.ksplit = [(400 * j, 400 if j < 3 else keys - 1200) for j in range(4)]
        else:
            self.block = keys
            self.max_units = 1
            self.ahead, self.ahead_rows = 4, 2
            self.ksplit = [(0, keys)]
        self.prep = ["XT"] + (["CT0", "CT1"] if self.cross else []) + ["Q", "K0"] + (["K1"] if self.cross else [])
        self.values = ["V0", "V1"] if self.cross else ["V0"]
        self.reader = {"A": "dve", "XT": "act", "CT0": "dve", "CT1": "dve", "Q": "dve", "K0": "act",
                       "K1": "act", "V0": "dve", "V1": "dve", "ONT": "act", "OUT": "dve"}
        self.pro = self._prologue()
        self.loop = self._iteration(True)
        self.last = self._iteration(False)
        self.ring = {p: [e for slot in plan for e in slot if e[0] in self.reader]
                     for p, plan in (("pro", self.pro), ("loop", self.loop), ("last", self.last))}
        self.n_pro = len(self.ring["pro"])
        self.n_loop = len(self.ring["loop"])
        assert self.n_loop % 2 == 0

    def _prologue(self):
        slots = [[(k, 0)] for k in self.prep[:-1] if k not in ("K0", "K1")]
        slots += [[("SPLIT_Q", 0)]]
        slots += [[(k, 0)] for k in self.prep if k in ("K0", "K1")]
        slots += [[("SPLIT_K", 0, j)] for j in range(len(self.ksplit))]
        slots += [[(k, 0)] for k in self.values]
        slots += [[("VX", 0)]]
        slots += [[("A", h, k, 0)] for h in range(self.ahead) for k in range(self.max_units)]
        slots += [[("MT", h, 0)] for h in range(self.ahead_rows)]
        return slots

    def _iteration(self, has_next):
        n, u = self.nb, self.units
        slots = [[] for _ in range(n + 7)]
        for g in range(n):
            slots[g].append(("B", g))
        for h in range(H):
            slots[(h + 1) * u + 3].append(("FOLD", h))
            if has_next or h + 1 < H:
                slots[h * u].append(("VX", (h + 1) % H))
        if has_next:
            nxt = 1
            if self.cross:
                at = {"XT": 1, "CT0": 3, "CT1": 5, "Q": 8, "K0": 10, "K1": 12,
                      "V0": 15 * u + 1, "V1": 15 * u + 3}
                slots[9].append(("SPLIT_Q", nxt))
                for j in range(4):
                    slots[(2 + j) * u + 1].append(("SPLIT_K", nxt, j))
            else:
                at = {"XT": 0, "Q": 1, "K0": 2, "V0": 15}
                slots[2].append(("SPLIT_Q", nxt))
                slots[3].append(("SPLIT_K", nxt, 0))
            for k, s in at.items():
                slots[s].append((k, nxt))
        for h in range(H):
            ha, hm = h + self.ahead, h + self.ahead_rows
            for k in range(self.max_units):
                if has_next or ha < H:
                    slots[h * u + 2 * k].append(("A", ha % H, k, ha // H))
            if has_next or hm < H:
                slots[h * u + (3 if self.cross else 0)].append(("MT", hm % H, hm // H))
        for g in range(n):
            slots[g + 2].append(("PV", g))
        for h in range(H):
            slots[(h + 1) * u + 1].append(("EV", h))
        slots[-3].append(("ON",))
        slots[-2].append(("ONT",))
        slots[-1].append(("OUT",))
        return slots

    def ring_at(self, part, k, i):
        return k if part == "pro" else self.n_pro + self.n_loop * i + k

    def ring_slot(self, part, k):
        return k % 2 if part == "pro" else (self.n_pro + k) % 2

    def released(self, part, k, i, who):
        count = lambda units: sum(self.reader[e[0]] == who for e in units)
        if part == "pro":
            return count(self.ring["pro"][:k])
        return count(self.ring["pro"]) + i * count(self.ring["loop"]) + count(self.ring[part][:k])


def attention(nc, top, cfg, X, ident_f, ident_b, ones_row, fold, ctx_dram, wts):
    n = cfg.name
    with ExitStack() as ctx:
        def sb(name, shape, dt):
            return ctx.enter_context(nc.sbuf_tensor(f"{n}_{name}", shape, dt))

        def pb(name, shape, dt):
            return ctx.enter_context(nc.psum_tensor(f"{n}_{name}", shape, dt))

        def sem(name):
            return top.enter_context(nc.semaphore(f"{n}_{name}"))

        NK, U, NB = cfg.keys, cfg.units, cfg.nb
        NKP = NK + NK % 2
        KD = DC + 1 if cfg.cross else D
        wq = sb("wq", [D, D], F32)
        wk = sb("wk", [KD, D], F32)
        wv = sb("wv", [KD, D], F32)
        wo = sb("wo", [D, D], F32)
        bq = sb("bq", [D, 1], F32)
        bo = sb("bo", [1, D], F32)
        raw = sb("raw", [P, 4, D], F32)
        raw_k = sb("raw_k", [P, 2, DC + 1], F32)
        xs = sb("xs", [P, QT, D], F32)
        xT = sb("xT", [D, S], F32)
        C = sb("C", [P, cfg.nch, DC], F32) if cfg.cross else None
        cT = sb("cT", [DC + 1, NK], F32) if cfg.cross else xT
        qf = sb("qf", [D, S], F32)
        kf = sb("kf", [D, NK], F32)
        res = sb("res", [D, 512], F32)
        qparts = sb("qparts", [D, PARTS, S], BF16)
        kparts = sb("kparts", [D, PARTS, NKP], BF16)
        Q = sb("Q", [KROWS, H, S], BF16)
        K = sb("K", [KROWS, H, NKP], BF16)
        Vf = sb("Vf", [P, cfg.nch, H, DH], F32)
        V32 = sb("V32", [P, 2, cfg.nch, 32], F32)
        nm4 = sb("nm4", [P, 2, QT, 2], F32)
        nm = sb("nm", [P, 2, QT], F32)
        mres = sb("mres", [P, 2, QT], F32)
        mp = sb("mp", [P, 2, QT, PARTS + 1], BF16)
        Pr = sb("Pr", [P, 4, 2 * S], F32)
        OTs = sb("OTs", [32 * cfg.quads, 2, S], F32)
        rden = sb("rden", [P, QT * H], F32)
        On = sb("On", [P, QT, D], F32)
        OnT = sb("OnT", [D, S], F32)
        y = sb("y", [P, QT, D], F32)
        stats = sb("stats", [P, QT, 6], F32)
        mv = sb("mv", [P, QT, 2], F32)
        rstd = sb("rstd", [P, QT], F32)
        half_neg = sb("half_neg", [P, QT], F32)
        eps = sb("eps", [P, QT], F32)
        one = sb("one", [P, 1], F32)
        seen = sb("seen", [P, 1], F32)

        ring = pb("ring", [P, 2, 1024], F32)
        sT = pb("sT", [P, 2, 512], F32)
        oT = pb("oT", [P, S], F32)
        pm = pb("pm", [P, 512], F32)
        om = pm[:, 0:QT * H * (DH + 1)].rearrange("p (t h r) -> p t h r", t=QT, h=H)
        mrow = pm[:, 384:512].bitcast(BF16)

        w_loaded = sem("w_loaded")
        w_turned = sem("w_turned")
        w_ready = sem("w_ready")
        ctx_in = sem("ctx_in")
        xs_ready = sem("xs_ready")
        filled = sem("filled")
        by = {"dve": sem("ring_dve"), "act": sem("ring_act")}
        split_q = sem("split_q")
        split_k = sem("split_k")
        stacked = [sem(f"stacked{g}") for g in range(GROUPS)]
        max_done = sem("max_done")
        max_split = sem("max_split")
        max_turned = sem("max_turned")
        max_rows = sem("max_rows")
        scored = sem("scored")
        exped = sem("exped")
        v_ready = sem("v_ready")
        weighed = sem("weighed")
        o_out = sem("o_out")
        folded = sem("folded")
        recips = sem("recips")
        on_ready = sem("on_ready")
        ln_dve = sem("ln_dve")
        ln_pool = sem("ln_pool")

        tensors = dict(wq=wq, wk=wk, wv=wv, wo=wo, bq=bq, bo=bo, raw=raw, raw_k=raw_k)
        READY = wts.n_ready + 3 + (7 if cfg.cross else 5)
        SQ = 4 * 1
        SK = 4 * len(cfg.ksplit)
        STK = 16 * 18
        NVE = len(cfg.values)

        def fill_wait(pe, part, k, i):
            if part == "pro" or k >= 2:
                if k >= 2:
                    who = cfg.reader[cfg.ring[part][k - 2][0]]
                    pe.wait_ge(by[who], cfg.released(part, k - 1, i, who))
            elif k == 0:
                for who in by:
                    pe.wait_ge(by[who], cfg.released(part, 0, i, who))

        def parts_of(eng, body):
            body("pro", cfg.pro, 0)
            with eng.Fori(0, B - 1) as i:
                body("loop", cfg.loop, i)
            body("last", cfg.last, B - 1)

        def rows(c):
            return cfg.chunks[c][1]

        block = ctx.enter_context(nc.Block())

        @block.sync
        def _(sp):
            loads = wts.loads(tensors)
            for dst, src in loads:
                sp.dma_start(dst, src, allow_slow_non_contiguous=True).then_inc(w_loaded, 16)

            def load_x(b):
                src = X[:, QT * b:QT * (b + 1), :] if isinstance(b, int) else X[:, bass.ds(b * QT, QT), :]
                sp.dma_start(xs[:, :, :], src).then_inc(xs_ready, 16)

            def load_ctx(b):
                full = (NK // P) * P
                if isinstance(b, int):
                    src = ctx_dram[b:b + 1]
                else:
                    src = ctx_dram[bass.ds(b, 1)]
                sp.dma_start(C[:, 0:NK // P, :],
                             src[:, 0:full, :].rearrange("o (c p) f -> p (o c) f", p=P)).then_inc(ctx_in, 16)
                sp.dma_start(C[0:NK - full, NK // P, :],
                             src[:, full:NK, :].rearrange("o p f -> (o p) f")).then_inc(ctx_in, 16)

            def stack(g):
                for parts, dst, side, w in ((qparts, Q, 0, S), (kparts, K, 1, NK)):
                    for a in range(PARTS):
                        for b in range(PARTS):
                            r = (a * PARTS + b) * DH
                            sp.dma_start(dst[r:r + DH, g * GH:(g + 1) * GH, 0:w],
                                         parts[g * GP:(g + 1) * GP, a if side else b, 0:w])\
                              .then_inc(stacked[g], 16)

            load_x(0)
            if cfg.cross:
                load_ctx(0)
            sp.wait_ge(w_ready, READY)
            sp.wait_ge(split_q, SQ)
            sp.wait_ge(split_k, SK)
            stack(0)
            load_x(1)
            if cfg.cross:
                sp.wait_ge(filled, cfg.prep.index("CT1") + 1)
                load_ctx(1)
            stack(1)

            def body(i, has_next):
                sp.wait_ge(split_k, SK * (i + 2))
                if has_next:
                    load_x(i + 2)
                    if cfg.cross:
                        load_ctx(i + 2)
                sp.wait_ge(scored, NB * i + NB // GROUPS)
                stack(0)
                sp.wait_ge(scored, NB * i + NB)
                stack(1)

            with sp.Fori(0, B - 2) as i:
                body(i, True)
            body(B - 2, False)

        @block.gpsimd
        def _(pool):
            pool.memset(half_neg[:, :], -0.5).then_inc(w_ready, 1)
            pool.memset(eps[:, :], EPS).then_inc(w_ready, 1)
            pool.memset(one[:, :], 1.0).then_inc(w_ready, 1)
            if cfg.cross:
                pool.memset(Vf[:, cfg.nch - 1, :, :], 0.0).then_inc(w_ready, 1)
            pool.memset(V32[:, :, :, DH:DH + 1], 1.0).then_inc(w_ready, 1)
            pool.memset(V32[:, :, :, DH + 1:32], 0.0).then_inc(w_ready, 1)

            pool.wait_ge(w_ready, READY)

            def split(src, dst, sm, at):
                r = res[:, 0:src.shape[1]]
                ones = one[:, :].broadcast_to([P, src.shape[1]])
                pool.tensor_tensor(dst[0], src, ones, ALU.mult).then_inc(sm, 1)
                pool.wait_ge(sm, at + 1)
                pool.tensor_tensor(r, src, dst[0], ALU.subtract).then_inc(sm, 1)
                pool.wait_ge(sm, at + 2)
                pool.tensor_tensor(dst[1], r, ones, ALU.mult).then_inc(sm, 1)
                pool.wait_ge(sm, at + 3)
                pool.tensor_tensor(dst[2], r, dst[1], ALU.subtract).then_inc(sm, 1)

            def body(part, plan, i):
                k_ring = 0
                for slot in plan:
                    for e in slot:
                        ring_now = k_ring
                        if e[0] in cfg.reader:
                            k_ring += 1
                        nb = i if part == "pro" else i + 1
                        if e[0] == "SPLIT_Q":
                            qn = [j for j, x in enumerate(cfg.ring[part]) if x[0] == "Q"][0]
                            pool.wait_ge(by["dve"], cfg.released(part, qn + 1, i, "dve"))
                            if part != "pro":
                                for g in range(GROUPS):
                                    pool.wait_ge(stacked[g], STK * (i + 1))
                                pool.wait_ge(split_k, SK * nb)
                            split(qf[:, :], [qparts[:, a, :] for a in range(PARTS)], split_q, SQ * nb)
                        if e[0] == "SPLIT_K":
                            j = e[2]
                            if j == 0:
                                kn = max(m for m, x in enumerate(cfg.ring[part]) if x[0] in ("K0", "K1"))
                                pool.wait_ge(by["act"], cfg.released(part, kn + 1, i, "act"))
                                pool.wait_ge(split_q, SQ * (nb + 1))
                            else:
                                pool.wait_ge(split_k, SK * nb + 4 * j)
                            s, w = cfg.ksplit[j]
                            split(kf[:, s:s + w], [kparts[:, a, s:s + w] for a in range(PARTS)],
                                  split_k, SK * nb + 4 * j)
                        if e[0] == "VX":
                            h = e[1]
                            gh = nb * H if (h == 0 or part == "pro") else i * H + h
                            if h == 0 or part == "pro":
                                vn = max(m for m, x in enumerate(cfg.ring[part]) if x[0] in ("V0", "V1"))
                                pool.wait_ge(by["dve"], cfg.released(part, vn + 1, i, "dve"))
                            if part == "pro":
                                pool.wait_ge(w_ready, READY)
                            if h != 1 and part != "pro":
                                pool.wait_ge(weighed, (gh - 1) * U)
                            pool.tensor_tensor(V32[:, h % 2, :, 0:DH], Vf[:, :, h, :],
                                               one[:, :].unsqueeze(2).broadcast_to([P, cfg.nch, DH]), ALU.mult).then_inc(v_ready, 1)
                        if e[0] == "A" and e[2] == cfg.max_units - 1:
                            h = e[1]
                            gh = (i + e[3]) * H + h
                            sl = h % 2
                            ones = one[:, :].broadcast_to([P, QT])
                            if cfg.cross:
                                pool.wait_ge(max_done, gh + 1)
                            else:
                                pool.wait_ge(by["dve"], cfg.released(part, ring_now + 1, i, "dve"))
                            if not (part == "pro" and h < 2):
                                pool.wait_ge(max_turned, gh - 1)
                            pool.tensor_tensor(mp[:, sl, :, 0], nm[:, sl, :], ones, ALU.mult).then_inc(max_split, 1)
                            pool.wait_ge(max_split, 4 * gh + 1)
                            pool.tensor_tensor(mres[:, sl, :], nm[:, sl, :], mp[:, sl, :, 0],
                                               ALU.subtract).then_inc(max_split, 1)
                            pool.wait_ge(max_split, 4 * gh + 2)
                            pool.tensor_tensor(mp[:, sl, :, 1], mres[:, sl, :], ones,
                                               ALU.mult).then_inc(max_split, 1)
                            pool.wait_ge(max_split, 4 * gh + 3)
                            pool.tensor_tensor(mp[:, sl, :, 2], mres[:, sl, :], mp[:, sl, :, 1],
                                               ALU.subtract).then_inc(max_split, 1)
                        if e[0] == "OUT":
                            pool.wait_ge(ln_dve, 6 * i + 4)
                            pool.tensor_tensor(rstd[:, :], mv[:, :, 1], eps[:, :], ALU.add).then_inc(ln_pool, 1)
                            pool.wait_ge(ln_pool, 2 * i + 1)
                            pool.tensor_tensor(rstd[:, :], rstd[:, :], half_neg[:, :], ALU.pow)\
                                .then_inc(ln_pool, 1)

            parts_of(pool, body)

        @block.tensor
        def _(pe):
            wts.turn(pe, tensors, ring, w_loaded, w_turned, ident_f)
            pe.wait_ge(w_ready, READY)

            def body(part, plan, i):
                k = 0
                turned = 0
                for slot in plan:
                    for e in slot:
                        op = e[0]
                        if op in cfg.reader:
                            fill_wait(pe, part, k, i)
                            R = ring[:, cfg.ring_slot(part, k), :]
                            k += 1
                        nb = i if part == "pro" else i + 1
                        if op == "XT":
                            pe.wait_ge(xs_ready, 16 * (nb + 1))
                            for t in range(QT):
                                mm = pe.transpose(R[:, t * P:(t + 1) * P], xs[:, t, :], ident_f[:, :])
                            mm.then_inc(filled, 1)
                        elif op in ("CT0", "CT1"):
                            if op == "CT0":
                                pe.wait_ge(ctx_in, 32 * (nb + 1))
                            lo, hi = (0, 8) if op == "CT0" else (8, cfg.nch)
                            for c in range(lo, hi):
                                r = rows(c)
                                mm = pe.transpose(R[0:DC, (c - lo) * P:(c - lo) * P + r], C[0:r, c, :],
                                                  ident_f[0:r, 0:r])
                            mm.then_inc(filled, 1)
                        elif op == "Q":
                            pe.wait_ge(by["act"], cfg.released(part, 1 + [x[0] for x in cfg.ring[part]].index("XT"),
                                                               i, "act"))
                            pe.matmul(R[:, 0:S], wq[:, :], xT[:, :], start=True, stop=True).then_inc(filled, 1)
                        elif op in ("K0", "K1"):
                            names = [x[0] for x in cfg.ring[part]]
                            if op == "K0" and cfg.cross:
                                pe.wait_ge(by["dve"], cfg.released(part, 1 + names.index("CT1"), i, "dve"))
                            lo, hi = (0, min(1024, NK)) if op == "K0" else (1024, NK)
                            for s in range(lo, hi, 512):
                                w = min(512, hi - s)
                                mm = pe.matmul(R[:, s - lo:s - lo + w], wk[:, :], cT[0:KD, s:s + w],
                                               start=True, stop=True)
                            mm.then_inc(filled, 1)
                        elif op in ("V0", "V1"):
                            lo, hi = (0, min(8, cfg.nch)) if op == "V0" else (8, cfg.nch)
                            for c in range(lo, hi):
                                s, r = cfg.chunks[c]
                                mm = pe.matmul(R[0:r, (c - lo) * D:(c - lo + 1) * D], cT[0:KD, s:s + r], wv[:, :],
                                               start=True, stop=True)
                            mm.then_inc(filled, 1)
                        elif op == "A":
                            _, h, m, nxt = e
                            b = i + nxt
                            if m == 0 and h % GH == 0:
                                pe.wait_ge(stacked[h // GH], STK * (b + 1))
                            if cfg.cross:
                                t, half = m // 2, m % 2
                                for j in range(2):
                                    s = (2 * half + j) * cfg.block_step
                                    mm = pe.matmul(R[:, 512 * j:512 * j + cfg.block],
                                                   Q[0:STACK, h, t * P:(t + 1) * P],
                                                   K[0:STACK, h, s:s + cfg.block], start=True, stop=True)
                            else:
                                for t in range(QT):
                                    mm = pe.matmul(R[:, 512 * t:512 * t + NK], Q[0:STACK, h, t * P:(t + 1) * P],
                                                   K[0:STACK, h, 0:NK], start=True, stop=True)
                            mm.then_inc(filled, 1)
                        elif op == "MT":
                            _, h, nxt = e
                            gh = (i + nxt) * H + h
                            pe.wait_ge(max_split, 4 * (gh + 1))
                            if not (part == "pro" and h == 0):
                                pe.wait_ge(max_rows, gh)
                            for t in range(QT):
                                mm = pe.transpose(mrow[0:PARTS, t * P:(t + 1) * P], mp[:, h % 2, t, 0:PARTS],
                                                  ident_b[:, :])
                            mm.then_inc(max_turned, 1)
                            turned += 1
                        elif op == "B":
                            h, u = divmod(e[1], U)
                            if u == 0:
                                pe.wait_ge(max_rows, i * H + h + 1)
                            if e[1] >= 2:
                                pe.wait_ge(exped, i * NB + e[1] - 1)
                            for c in range(2 * u, min(2 * u + 2, cfg.nch)):
                                s, r = cfg.chunks[c]
                                mm = pe.matmul(sT[0:r, e[1] % 2, (c % 2) * S:(c % 2 + 1) * S],
                                               K[0:KROWS, h, s:s + r], Q[0:KROWS, h, :], start=True, stop=True)
                            mm.then_inc(scored, 1)
                        elif op == "PV":
                            h, u = divmod(e[1], U)
                            gh = i * H + h
                            pe.wait_ge(exped, i * NB + e[1] + 1)
                            if u == 0:
                                pe.wait_ge(v_ready, gh + 1)
                                if h >= 1:
                                    pe.wait_ge(o_out, gh)
                            for c in range(2 * u, min(2 * u + 2, cfg.nch)):
                                r = rows(c)
                                q = 32 * (c % 4)
                                mm = pe.matmul(oT[q:q + 32, :], V32[0:r, h % 2, c, :],
                                               Pr[0:r, e[1] % 4, (c % 2) * S:(c % 2 + 1) * S],
                                               start=(c < 4), stop=(c + 4 >= cfg.nch), tile_position=(0, q))
                            mm.then_inc(weighed, 1)
                        elif op == "FOLD":
                            h = e[1]
                            pe.wait_ge(o_out, i * H + h + 1)
                            pe.wait_ge(max_rows, cfg.ahead_rows + i * H + turned)
                            for t in range(QT):
                                mm = pe.matmul(om[:, t, h, :], OTs[:, h % 2, t * P:(t + 1) * P],
                                               fold[0:32 * cfg.quads, :], start=True, stop=True)
                            mm.then_inc(folded, 1)
                        elif op == "ONT":
                            pe.wait_ge(on_ready, i + 1)
                            for t in range(QT):
                                mm = pe.transpose(R[:, t * P:(t + 1) * P], On[:, t, :], ident_f[:, :])
                            mm.then_inc(filled, 1)
                        elif op == "OUT":
                            pe.wait_ge(by["act"], cfg.released(part, k - 1, i, "act"))
                            for t in range(QT):
                                pe.matmul(R[:, t * D:(t + 1) * D], OnT[:, t * P:(t + 1) * P], wo[:, :],
                                          start=(t == 0), stop=False, skip_group_check=True)
                                mm = pe.matmul(R[:, t * D:(t + 1) * D], ones_row[:, :], bo[:, :],
                                               start=False, stop=(t == QT - 1), skip_group_check=True)
                            mm.then_inc(filled, 1)

            parts_of(pe, body)

        @block.scalar
        def _(act):
            def body(part, plan, i):
                k = 0
                for slot in plan:
                    for e in slot:
                        op = e[0]
                        if op in cfg.reader:
                            R = ring[:, cfg.ring_slot(part, k), :]
                            if cfg.reader[op] == "act":
                                act.wait_ge(filled, cfg.ring_at(part, k, i) + 1)
                            k += 1
                        if op == "XT":
                            act.activation(xT[:, :], R[:, 0:S], ACT.Copy).then_inc(by["act"], 1)
                        elif op in ("K0", "K1"):
                            nb = i if part == "pro" else i + 1
                            if op == "K0" and part != "pro":
                                act.wait_ge(split_k, SK * nb)
                            lo, hi = (0, min(1024, NK)) if op == "K0" else (1024, NK)
                            act.activation(kf[:, lo:hi], R[:, 0:hi - lo], ACT.Copy).then_inc(by["act"], 1)
                        elif op == "MT":
                            _, h, nxt = e
                            gh = (i + nxt) * H + h
                            act.wait_ge(max_turned, gh + 1)
                            if part == "pro":
                                act.wait_ge(w_ready, READY)
                            act.activation(Q[MROW:KROWS, h, :], mrow[0:PARTS, :], ACT.Copy).then_inc(max_rows, 1)
                        elif op == "B":
                            g = e[1]
                            u = g % U
                            act.wait_ge(scored, i * NB + g + 1)
                            if g >= 4:
                                act.wait_ge(weighed, i * NB + g - 3)
                            nchunk = min(2, cfg.nch - 2 * u)
                            r = rows(2 * u)
                            act.activation(Pr[0:r, g % 4, 0:nchunk * S], sT[0:r, g % 2, 0:nchunk * S],
                                           ACT.Exp).then_inc(exped, 1)
                        elif op == "EV":
                            h = e[1]
                            gh = i * H + h
                            act.wait_ge(weighed, (gh + 1) * U)
                            if h >= 2:
                                act.wait_ge(folded, gh - 1)
                            act.activation(OTs[:, h % 2, :], oT[0:32 * cfg.quads, :],
                                           ACT.Copy).then_inc(o_out, 1)
                        elif op == "ONT":
                            act.activation(OnT[:, :], R[:, 0:S], ACT.Copy).then_inc(by["act"], 1)

            parts_of(act, body)

        @block.vector
        def _(dve):
            wts.place(dve, tensors, ring,
                         w_loaded, w_turned, w_ready)
            if cfg.cross:
                dve.memset(cT[DC:DC + 1, :], 1.0).then_inc(w_ready, 1)
            for T in (Q, K):
                dve.memset(T[64:MROW, :, :].rearrange("p h n -> p (h n)").bitcast(mybir.dt.uint32), 0)\
                   .then_inc(w_ready, 1)
            dve.memset(K[MROW:KROWS, :, :], 1.0).then_inc(w_ready, 1)

            def body(part, plan, i):
                k = 0
                for slot in plan:
                    for e in slot:
                        op = e[0]
                        if op in cfg.reader:
                            R = ring[:, cfg.ring_slot(part, k), :]
                            if cfg.reader[op] == "dve":
                                dve.wait_ge(filled, cfg.ring_at(part, k, i) + 1)
                            k += 1
                        nb = i if part == "pro" else i + 1
                        if op in ("CT0", "CT1"):
                            lo, hi = (0, 1024) if op == "CT0" else (1024, NK)
                            dve.tensor_copy(cT[0:DC, lo:hi], R[0:DC, 0:hi - lo]).then_inc(by["dve"], 1)
                        elif op == "Q":
                            if part != "pro":
                                dve.wait_ge(split_q, SQ * nb)
                            if part == "pro":
                                dve.wait_ge(w_ready, READY)
                            dve.tensor_scalar(qf[:, :], R[:, 0:S], bq[:, 0:1], SCALE, ALU.add, ALU.mult)\
                               .then_inc(by["dve"], 1)
                        elif op in ("V0", "V1"):
                            lo, hi = (0, min(8, cfg.nch)) if op == "V0" else (8, cfg.nch)
                            if part == "pro":
                                dve.wait_ge(w_ready, READY)
                            else:
                                dve.wait_ge(v_ready, (i + 1) * H)
                            full = hi if rows(hi - 1) == P else hi - 1
                            last = dve.tensor_copy(
                                Vf[:, lo:full, :, :],
                                R[:, 0:(full - lo) * D].rearrange("p (c h d) -> p c h d", h=H, d=DH))
                            if full < hi:
                                r = rows(full)
                                last = dve.tensor_copy(
                                    Vf[0:r, full, :, :],
                                    R[0:r, (full - lo) * D:(full - lo + 1) * D].rearrange("p (h d) -> p h d", d=DH))
                            last.then_inc(by["dve"], 1)
                        elif op == "A":
                            _, h, m, nxt = e
                            gh = (i + nxt) * H + h
                            sl = h % 2
                            if m == 0 and not (part == "pro" and h < 2):
                                dve.wait_ge(max_split, 4 * (gh - 1))
                            if cfg.cross:
                                t, half = m // 2, m % 2
                                dve.tensor_reduce(
                                    nm4[:, sl, t, half:half + 1],
                                    R.rearrange("p (j n) -> p j n", j=2)[:, :, 0:cfg.block],
                                    AX.XY, ALU.max, negate=True).then_inc(by["dve"], 1)
                                if m == cfg.max_units - 1:
                                    dve.wait_ge(by["dve"], cfg.released(part, k, i, "dve"))
                                    dve.tensor_tensor(nm[:, sl, :], nm4[:, sl, :, 0], nm4[:, sl, :, 1],
                                                      ALU.min).then_inc(max_done, 1)
                            else:
                                dve.tensor_reduce(
                                    nm[:, sl, :], R.rearrange("p (t n) -> p t n", t=2)[:, :, 0:NK],
                                    AX.X, ALU.max, negate=True).then_inc(by["dve"], 1)
                        elif op == "ON":
                            dve.wait_ge(folded, (i + 1) * H)
                            dve.reciprocal(rden[:, :].rearrange("p (t h) -> p t h", t=QT),
                                           om[:, :, :, DH]).then_inc(recips, 1)
                            dve.wait_ge(recips, i + 1)
                            dve.tensor_tensor(
                                On[:, :, :].rearrange("p t (h d) -> p (t h) d", d=DH),
                                om[:, :, :, 0:DH].rearrange("p t h d -> p (t h) d"),
                                rden[:, :].unsqueeze(2).broadcast_to([P, QT * H, DH]),
                                ALU.mult).then_inc(on_ready, 1)
                        elif op == "OUT":
                            xb = X[:, 2 * i:2 * i + 2, :] if isinstance(i, int) else X[:, bass.ds(i * 2, 2), :]
                            dve.tensor_tensor(y[:, :, :], R[:, 0:QT * D].rearrange("p (t f) -> p t f", t=QT),
                                              xb, ALU.add).then_inc(by["dve"], 1)
                            dve.wait_ge(by["dve"], cfg.released(part, k, i, "dve"))
                            for t in range(QT):
                                dve.bn_stats(stats[:, t, :], y[:, t, :]).then_inc(ln_dve, 1)
                            dve.wait_ge(ln_dve, 6 * i + 2)
                            dve.tensor_copy(seen[:, :], stats[:, 0, 0:1])
                            for t in range(QT):
                                dve.bn_aggr(mv[:, t, :], stats[:, t, :]).then_inc(ln_dve, 1)
                            dve.wait_ge(ln_pool, 2 * i + 2)
                            for t in range(QT):
                                xo = X[:, 2 * i + t, :] if isinstance(i, int) else X[:, bass.ds(i * 2 + t, 1), :]
                                dve.tensor_scalar(xo, y[:, t, :] if isinstance(i, int) else y[:, t:t + 1, :],
                                                  mv[:, t, 0:1], rstd[:, t:t + 1],
                                                  ALU.subtract, ALU.mult).then_inc(ln_dve, 1)

            parts_of(dve, body)


class SelfWeights:
    n_ready = 5

    def __init__(self, qkv_w, out_w, out_b):
        self.qkv_w, self.out_w, self.out_b = qkv_w, out_w, out_b

    def loads(self, t):
        return [(t["raw"][:, 0:3, :], self.qkv_w.rearrange("(j p) c -> p j c", p=P)),
                (t["raw"][:, 3, :], self.out_w),
                (t["bo"][:, :], self.out_b.rearrange("(o n) -> o n", o=1))]

    def turn(self, pe, t, ring, w_loaded, w_turned, ident_f):
        pe.wait_ge(w_loaded, 16 * 3)
        for j in range(4):
            mm = pe.transpose(ring[:, 0, j * D:(j + 1) * D], t["raw"][:, j, :], ident_f[:, :])
        mm.then_inc(w_turned, 1)

    def place(self, dve, t, ring, w_loaded, w_turned, w_ready):
        dve.wait_ge(w_turned, 1)
        for j, w in enumerate((t["wq"], t["wk"])):
            dve.tensor_copy(as_groups(w[:, :]), heads_to_groups(ring[:, 0, j * D:(j + 1) * D])).then_inc(w_ready, 1)
        for j, w in ((2, t["wv"]), (3, t["wo"])):
            dve.tensor_copy(w[:, :], ring[:, 0, j * D:(j + 1) * D]).then_inc(w_ready, 1)
        dve.memset(t["bq"][:, :], 0.0).then_inc(w_ready, 1)


class CrossWeightsIn:
    n_ready = 3

    def __init__(self, w_q, b_q, w_k, b_k, w_v, b_v, w_o, b_o):
        self.w_q, self.b_q, self.w_k, self.b_k = w_q, b_q, w_k, b_k
        self.w_v, self.b_v, self.w_o, self.b_o = w_v, b_v, w_o, b_o

    def loads(self, t):
        row = lambda v: v.rearrange("(o n) -> o n", o=1)
        return [(t["raw"][:, 0, :], self.w_q),
                (t["raw"][0:DC, 1, :], self.w_k), (t["raw"][DC:DC + 1, 1, :], row(self.b_k)),
                (t["raw"][0:DC, 2, :], self.w_v), (t["raw"][DC:DC + 1, 2, :], row(self.b_v)),
                (t["wo"][:, :], self.w_o), (t["bo"][:, :], row(self.b_o))] + bias_in_groups(t["bq"], self.b_q)

    def turn(self, pe, t, ring, w_loaded, w_turned, ident_f):
        pe.wait_ge(w_loaded, 16 * (7 + GROUPS))

    def place(self, dve, t, ring, w_loaded, w_turned, w_ready):
        dve.wait_ge(w_loaded, 16 * (7 + GROUPS))
        raw = t["raw"]
        dve.tensor_copy(as_groups(t["wq"][:, :]), heads_to_groups(raw[:, 0, :])).then_inc(w_ready, 1)
        dve.tensor_copy(as_groups(t["wk"][:, :]), heads_to_groups(raw[0:DC + 1, 1, :])).then_inc(w_ready, 1)
        dve.tensor_copy(t["wv"][:, :], raw[0:DC + 1, 2, :]).then_inc(w_ready, 1)


class CrossWeightsOut:
    n_ready = 4

    def __init__(self, Wq, bq, Wkv, bkv, Wo, bo):
        self.Wq, self.bq, self.Wkv, self.bkv, self.Wo, self.bo = Wq, bq, Wkv, bkv, Wo, bo

    def loads(self, t):
        return [(t["raw"][:, 0, :], self.Wq), (t["raw"][:, 1, :], self.Wo),
                (t["raw_k"][:, :, 0:DC], self.Wkv.rearrange("(j p) c -> p j c", p=P)),
                (t["raw_k"][:, :, DC], self.bkv.rearrange("(j p) -> p j", p=P)),
                (t["bo"][:, :], self.bo.rearrange("(o n) -> o n", o=1))] + bias_in_groups(t["bq"], self.bq)

    def turn(self, pe, t, ring, w_loaded, w_turned, ident_f):
        pe.wait_ge(w_loaded, 16 * (5 + GROUPS))
        for j in range(2):
            pe.transpose(ring[:, 0, j * D:(j + 1) * D], t["raw"][:, j, :], ident_f[:, :])
        for j in range(2):
            mm = pe.transpose(ring[0:DC + 1, 0, 512 + j * P:512 + (j + 1) * P], t["raw_k"][:, j, :], ident_f[:, :])
        mm.then_inc(w_turned, 1)

    def place(self, dve, t, ring, w_loaded, w_turned, w_ready):
        dve.wait_ge(w_turned, 1)
        dve.tensor_copy(as_groups(t["wq"][:, :]), heads_to_groups(ring[:, 0, 0:D])).then_inc(w_ready, 1)
        dve.tensor_copy(t["wo"][:, :], ring[:, 0, D:2 * D]).then_inc(w_ready, 1)
        kv = ring[0:DC + 1, 0, 512:512 + 2 * D].rearrange("p (g l s d) -> p s g d l", g=GROUPS, l=GH, s=2, d=DH)
        dve.tensor_copy(as_groups(t["wk"][:, :]), kv[:, 0]).then_inc(w_ready, 1)
        v = ring[0:DC + 1, 0, 512:512 + 2 * D].rearrange("p (h s d) -> p s h d", h=H, s=2)
        dve.tensor_copy(t["wv"][:, :].rearrange("p (h d) -> p h d", h=H), v[:, 1]).then_inc(w_ready, 1)


def bias_in_groups(dst, src):
    v = src.rearrange("(g l d o) -> g d l o", g=GROUPS, l=GH, d=DH, o=1)
    return [(dst[g * GP:(g + 1) * GP, :], v[g]) for g in range(GROUPS)]


def constants(nc, ctx, x_dram, X, ident_f, ident_b, ones_row, fold):
    x_in = ctx.enter_context(nc.semaphore("x_in"))
    set_ = ctx.enter_context(nc.semaphore("constants_set"))
    block = nc.Block()
    with block:
        @block.sync
        def _(sp):
            for q in range(4):
                n = NT // 4
                sp.dma_start(X[:, q * n:(q + 1) * n, :],
                             x_dram.rearrange("b (t p) f -> p (b t) f", p=P)[:, q * n:(q + 1) * n, :])\
                  .then_inc(x_in, 16)
            sp.wait_ge(x_in, 16 * 4)
            sp.nop()

        @block.gpsimd
        def _(pool):
            pool.memset(ident_f[:, :], 0.0).then_inc(set_, 1)
            pool.memset(ident_b[:, :], 0.0).then_inc(set_, 1)
            pool.memset(ones_row[:, :], 1.0).then_inc(set_, 1)
            pool.memset(fold[:, :], 0.0).then_inc(set_, 1)
            pool.wait_ge(set_, 4)
            for m in (ident_f, ident_b):
                pool.affine_select(out=m[:, :], in_=m[:, :], compare_op=ALU.not_equal, fill=1.0, base=0,
                                   pattern=[[-1, P]], channel_multiplier=1).then_inc(set_, 1)
            for q in range(4):
                pool.wait_ge(set_, 6 + q)
                pool.affine_select(out=fold[:, :], in_=fold[:, :], compare_op=ALU.not_equal, fill=1.0,
                                   base=-32 * q, pattern=[[-1, DH + 1]], channel_multiplier=1).then_inc(set_, 1)


def store(nc, ctx, X, out):
    stored = ctx.enter_context(nc.semaphore("stored"))
    with nc.Block() as block:
        @block.sync
        def _(sp):
            sp.dma_start(out.rearrange("b (t p) f -> p (b t) f", p=P), X[:, :, :]).then_inc(stored, 16)
            sp.wait_ge(stored, 16)


T = B * S
BLK = 512
BT = BLK // P
NBLK = T // BLK
NE, NGRP, TOPK, TOPG = 32, 8, 6, 4
MI, SI = 64, 256
ROUTED_SCALE = 2.5
SCALING = 2.0


def tiles(x, i):
    return x[:, i * BT:(i + 1) * BT, :] if isinstance(i, int) else x[:, bass.ds(i * BT, BT), :]


def experts(nc, top, X, ident_f, ident_b, a):
    NC = NE * MI // P
    NCH = NC + SI // P
    with ExitStack() as ctx:
        def sb(name, shape, dt):
            return ctx.enter_context(nc.sbuf_tensor(f"moe_{name}", shape, dt))

        def sem(name):
            return top.enter_context(nc.semaphore(f"moe_{name}"))

        raw_up = sb("raw_up", [P, NCH, D], F32)
        raw_down = sb("raw_down", [D, NCH, P], F32)
        raw_gate = sb("raw_gate", [NE, D], F32)
        up = sb("up", [D, NCH, P], F32)
        down = sb("down", [P, NCH, D], F32)
        gate = sb("gate", [D, NE], F32)
        ebias = sb("ebias", [P, NE], F32)
        xT = sb("xT", [D, T], F32)
        sel = sb("sel", [PARTS * NE, NC, P], BF16)
        cT = sb("cT", [PARTS * NE, T], BF16)
        s0 = sb("s0", [P, NT, NE], F32)
        sc = sb("sc", [P, NT, NE], F32)
        pair = sb("pair", [P, 4, NT, NGRP], F32)
        gsum = sb("gsum", [P, NT, NGRP], F32)
        top8 = sb("top8", [P, NT, 8], F32)
        gt = sb("gt", [P, NT, NE], F32)
        eq = sb("eq", [P, NT, NE], F32)
        cum = sb("cum", [P, NT, NE], F32)
        left = sb("left", [P, NT], F32)
        restart_g = sb("restart_g", [P, NT, NGRP], F32)
        restart_e = sb("restart_e", [P, NT, NE], F32)
        cparts = sb("cparts", [P, NT, PARTS * NE], BF16)
        r = sb("r", [P, 3, BLK], F32)
        rc = sb("rc", [P, 3, BLK], F32)
        hh = sb("hh", [P, 3, BLK], F32)
        y = sb("y", [P, BT, D], F32)
        stats = sb("stats", [P, BT, 6], F32)
        mv = sb("mv", [P, BT, 2], F32)
        rstd = sb("rstd", [P, BT], F32)
        half_neg = sb("half_neg", [P, BT], F32)
        eps = sb("eps", [P, BT], F32)
        seen = sb("seen", [P, 1], F32)

        bank = ctx.enter_context(nc.psum_tensor("moe_bank", [P, 8, 512], F32))
        ROUTE = 44
        NW = 2 * NCH // 4
        turned_units = NW + 1 + NBLK

        loaded = sem("loaded")
        turned = sem("turned")
        took_act = sem("took_act")
        took_dve = sem("took_dve")
        logits = sem("logits")
        sig = sem("sig")
        chain = sem("chain")
        consts = sem("consts")
        c_turned = sem("c_turned")
        c_took = sem("c_took")
        up_done = sem("up_done")
        spread = sem("spread")
        relu = sem("relu")
        scaled = sem("scaled")
        hidden = sem("hidden")
        summed = sem("summed")
        ln_dve = sem("ln_dve")
        ln_pool = sem("ln_pool")
        block = ctx.enter_context(nc.Block())

        def weight_tile(j):
            return (raw_up[:, j, :], up[:, j, :]) if j < NCH else (raw_down[:, j - NCH, :], down[:, j - NCH, :])

        def took(n, eng):
            if n >= 4:
                eng.wait_ge(took_act if n % 2 == 0 else took_dve, (n - 4) // 2 + 1)

        def half(eng, j, n):
            copy = (lambda o, s: eng.activation(o, s, ACT.Copy)) if n % 2 == 0 else eng.tensor_copy
            sm = took_act if n % 2 == 0 else took_dve
            flat_up = up[:, :, :].rearrange("p m n -> p (m n)")
            flat_down = down[:, :, :].rearrange("p m n -> p (m n)")
            a_n = max(0, min(4, NCH - j))
            ins = None
            if a_n:
                ins = copy(flat_up[:, j * P:(j + a_n) * P], bank[:, n % 4, 0:a_n * P])
            if a_n < 4:
                k = j + a_n - NCH
                ins = copy(flat_down[:, k * P:(k + 4 - a_n) * P], bank[:, n % 4, a_n * P:512])
            ins.then_inc(sm, 1)

        @block.sync
        def _(sp):
            sp.dma_start(raw_gate[:, :], a["L0_ffn_gate_w"]).then_inc(loaded, 16)
            sp.dma_start(ebias[:, :], a["L0_ffn_e_bias"].partition_broadcast(P)).then_inc(loaded, 16)
            sp.dma_start(raw_up[:, 0:NC, :], a["L0_ffn_up_w"].rearrange("(m e) i h -> (e i) m h", e=P // MI))\
              .then_inc(loaded, 16)
            sp.dma_start(raw_up[:, NC:NCH, :], a["L0_ffn_shared_up_w"].rearrange("(m p) h -> p m h", p=P))\
              .then_inc(loaded, 16)
            sp.dma_start(raw_down[:, 0:NC, :].rearrange("h m (e i) -> h (m e) i", e=P // MI),
                         a["L0_ffn_down_w"].rearrange("e h i -> h e i")).then_inc(loaded, 16)
            sp.dma_start(raw_down[:, NC:NCH, :].rearrange("h m i -> h (m i)"), a["L0_ffn_shared_down_w"])\
              .then_inc(loaded, 16)

        @block.gpsimd
        def _(pool):
            pool.memset(sel[:, :, :], 0.0).then_inc(consts, 1)
            pool.memset(half_neg[:, :], -0.5).then_inc(consts, 1)
            pool.memset(eps[:, :], EPS).then_inc(consts, 1)
            n = 3
            for part in range(PARTS):
                for e in range(P // MI):
                    v = sel[:, :, e * MI:(e + 1) * MI]
                    pool.wait_ge(consts, n)
                    pool.affine_select(out=v, in_=v, compare_op=ALU.not_equal, fill=1.0,
                                       base=-(part * NE + e), pattern=[[-(P // MI), NC], [0, MI]],
                                       channel_multiplier=1).then_inc(consts, 1)
                    n += 1

            with pool.Fori(0, NBLK) as i:
                for m in range(NCH):
                    q = m % 3
                    if m < NC:
                        pool.wait_ge(scaled, i * NC + m + 1)
                        pool.tensor_tensor(hh[:, q, :], r[:, q, :], rc[:, q, :], ALU.mult).then_inc(hidden, 1)
                    else:
                        pool.wait_ge(relu, i * NCH + m + 1)
                        pool.tensor_tensor(hh[:, q, :], r[:, q, :], r[:, q, :], ALU.mult).then_inc(hidden, 1)
                pool.wait_ge(ln_dve, i * (1 + 3 * BT) + 1 + 2 * BT)
                pool.tensor_tensor(rstd[:, :], mv[:, :, 1], eps[:, :], ALU.add).then_inc(ln_pool, 1)
                pool.wait_ge(ln_pool, 2 * i + 1)
                pool.tensor_tensor(rstd[:, :], rstd[:, :], half_neg[:, :], ALU.pow).then_inc(ln_pool, 1)

        @block.tensor
        def _(pe):
            pe.wait_ge(loaded, 16 * 6)
            n = 0
            pe.transpose(bank[:, 0, 0:NE], raw_gate[:, :], ident_f[0:NE, 0:NE]).then_inc(turned, 1)
            n += 1
            for b in range(NBLK):
                took(n, pe)
                for t in range(BT):
                    mm = pe.transpose(bank[:, n % 4, t * P:(t + 1) * P], X[:, b * BT + t, :], ident_f[:, :])
                mm.then_inc(turned, 1)
                n += 1
            pe.wait_ge(took_act, (NBLK // 2) + 1)
            pe.wait_ge(took_dve, NBLK // 2)
            for t in range(NT):
                mm = pe.matmul(bank[:, 4 + t // 16, (t % 16) * NE:(t % 16 + 1) * NE], xT[:, t * P:(t + 1) * P],
                               gate[:, :], start=True, stop=True)
            mm.then_inc(logits, 1)
            for w in range(NW):
                took(n, pe)
                for t in range(4):
                    mm = pe.transpose(bank[:, n % 4, t * P:(t + 1) * P], weight_tile(4 * w + t)[0], ident_f[:, :])
                mm.then_inc(turned, 1)
                n += 1
            assert n == turned_units
            pe.wait_ge(took_act, (n + 1) // 2)
            pe.wait_ge(took_dve, n // 2)
            pe.wait_ge(chain, ROUTE)
            for u in range(4):
                ct = bank[:, u, :].bitcast(BF16)
                for t in range(8):
                    mm = pe.transpose(ct[0:PARTS * NE, t * P:(t + 1) * P], cparts[:, u * 8 + t, :], ident_b[:, :])
                mm.then_inc(c_turned, 1)
            pe.wait_ge(c_took, 4)
            pe.wait_ge(consts, 3 + PARTS * P // MI)

            def output(i, m):
                pe.wait_ge(hidden, i * NCH + m + 1)
                for t in range(BT):
                    mm = pe.matmul(bank[:, 4, t * D:(t + 1) * D], hh[:, m % 3, t * P:(t + 1) * P], down[:, m, :],
                                   start=(m == 0 and t == 0), stop=(m == NCH - 1), skip_group_check=True)
                if m == NCH - 1:
                    mm.then_inc(summed, 1)

            with pe.Fori(0, NBLK) as i:
                xb = xT[:, bass.ds(i * BLK, BLK)]
                cb = cT[:, bass.ds(i * BLK, BLK)]
                for m in range(NCH):
                    if m >= 2:
                        pe.wait_ge(relu, i * NCH + m - 1)
                    pe.matmul(bank[:, m % 2, :], up[:, m, :], xb, start=True, stop=True).then_inc(up_done, 1)
                    if m < NC:
                        if m >= 2:
                            pe.wait_ge(scaled, i * NC + m - 1)
                        pe.matmul(bank[:, 2 + m % 2, :], sel[:, m, :], cb, start=True, stop=True)\
                          .then_inc(spread, 1)
                    if m >= 2:
                        output(i, m - 2)
                output(i, NCH - 2)
                output(i, NCH - 1)
                pe.wait_ge(ln_dve, i * (1 + 3 * BT) + 1)

        @block.scalar
        def _(act):
            n = 0
            for n in range(0, turned_units, 2):
                act.wait_ge(turned, n + 1)
                if n == 0:
                    ins = act.activation(gate[:, :], bank[:, 0, 0:NE], ACT.Copy)
                elif n <= NBLK:
                    ins = act.activation(xT[:, (n - 1) * BLK:n * BLK], bank[:, n % 4, :], ACT.Copy)
                else:
                    j = 4 * (n - 1 - NBLK)
                    half(act, j, n)
                    ins = None
                if ins is not None:
                    ins.then_inc(took_act, 1)
                if n == NBLK:
                    act.wait_ge(logits, 1)
                    act.activation(s0[:, :, :].rearrange("p t e -> p (t e)"),
                                   bank[:, 4:6, :].rearrange("p a n -> p (a n)"), ACT.Sigmoid).then_inc(sig, 1)
            for u in range(4):
                act.wait_ge(c_turned, u + 1)
                act.activation(cT[:, u * 1024:(u + 1) * 1024], bank[0:PARTS * NE, u, :].bitcast(BF16),
                               ACT.Copy).then_inc(c_took, 1)
            with act.Fori(0, NBLK) as i:
                for m in range(NCH):
                    act.wait_ge(up_done, i * NCH + m + 1)
                    if m >= 3:
                        act.wait_ge(hidden, i * NCH + m - 2)
                    act.activation(r[:, m % 3, :], bank[:, m % 2, :], ACT.Relu).then_inc(relu, 1)

        steps = [0]

        @block.vector
        def _(dve):
            def link(ins):
                steps[0] += 1
                ins.then_inc(chain, 1)
                dve.wait_ge(chain, steps[0])

            def take(n):
                dve.wait_ge(turned, n + 1)
                if n <= NBLK:
                    dve.tensor_copy(xT[:, (n - 1) * BLK:n * BLK], bank[:, n % 4, :]).then_inc(took_dve, 1)
                else:
                    half(dve, 4 * (n - 1 - NBLK), n)

            for n in range(1, NBLK + 1, 2):
                take(n)
            for x, w in ((restart_g, NGRP), (restart_e, NE)):
                link(dve.memset(x[:, :, :], 1.0))
                link(dve.memset(x[:, :, 0:1], 0.0))
            for n in range(NBLK + 1, turned_units, 2):
                take(n)
            dve.wait_ge(sig, 1)
            dve.wait_ge(loaded, 16 * 6)
            link(dve.tensor_tensor(sc[:, :, :], s0[:, :, :], ebias[:, :].unsqueeze(1).broadcast_to([P, NT, NE]),
                                   ALU.add))
            four = sc[:, :, :].rearrange("p t (g k) -> p k t g", k=NE // NGRP)
            w = [pair[:, j, :, :] for j in range(4)]
            link(dve.tensor_tensor(w[0], four[:, 0], four[:, 1], ALU.max))
            link(dve.tensor_tensor(w[1], four[:, 0], four[:, 1], ALU.min))
            link(dve.tensor_tensor(w[2], four[:, 2], four[:, 3], ALU.max))
            link(dve.tensor_tensor(w[3], four[:, 2], four[:, 3], ALU.min))
            link(dve.tensor_tensor(w[1], w[1], w[3], ALU.max))
            link(dve.tensor_tensor(w[3], w[0], w[2], ALU.min))
            link(dve.tensor_tensor(w[0], w[0], w[2], ALU.max))
            link(dve.tensor_tensor(w[1], w[1], w[3], ALU.max))
            link(dve.tensor_tensor(gsum[:, :, :], w[0], w[1], ALU.add))

            def choose(v, n, k, restart):
                g, e, c = (x[:, :, 0:n] for x in (gt, eq, cum))
                for t in range(NT):
                    ins = dve.max(top8[:, t, :], v[:, t, :])
                link(ins)
                kth = top8[:, :, k - 1:k].broadcast_to([P, NT, n])
                link(dve.tensor_tensor(g, v, kth, ALU.is_gt))
                link(dve.tensor_tensor(e, v, kth, ALU.is_equal))
                link(dve.tensor_reduce(left[:, :], g, AX.X, ALU.add))
                link(dve.tensor_scalar(left[:, :], left[:, :], -1.0, float(k), ALU.mult, ALU.add))
                if n == NE:
                    flat = lambda x: x[:, :, :].rearrange("p t e -> p (t e)")
                    link(dve.tensor_tensor_scan(flat(cum), flat(restart), flat(eq), 0.0, ALU.mult, ALU.add))
                else:
                    flat = lambda x: x[:, 0:2, 0:1]
                    e2 = pair[:, 2, :, :]
                    link(dve.tensor_copy(e2, e))
                    c2 = pair[:, 3, :, :]
                    link(dve.tensor_tensor_scan(c2.rearrange("p t e -> p (t e)"),
                                                restart[:, :, :].rearrange("p t e -> p (t e)"),
                                                e2.rearrange("p t e -> p (t e)"), 0.0, ALU.mult, ALU.add))
                    c = c2
                link(dve.tensor_tensor(c, c, left[:, :].unsqueeze(2).broadcast_to([P, NT, n]), ALU.is_le))
                link(dve.tensor_tensor(e, e, c, ALU.mult))
                link(dve.tensor_tensor(g, g, e, ALU.add))

            choose(gsum[:, :, :], NGRP, TOPG, restart_g)
            link(dve.tensor_tensor(sc[:, :, :].rearrange("p t (g k) -> p t g k", k=NE // NGRP),
                                   sc[:, :, :].rearrange("p t (g k) -> p t g k", k=NE // NGRP),
                                   gt[:, :, 0:NGRP].unsqueeze(3).broadcast_to([P, NT, NGRP, NE // NGRP]), ALU.mult))
            choose(sc[:, :, :], NE, TOPK, restart_e)
            link(dve.tensor_tensor(gt[:, :, :], gt[:, :, :], s0[:, :, :], ALU.mult))
            link(dve.tensor_reduce(left[:, :], gt[:, :, :], AX.X, ALU.add))
            link(dve.tensor_scalar(left[:, :], left[:, :], 1e-20, None, ALU.add))
            link(dve.reciprocal(left[:, :], left[:, :]))
            link(dve.tensor_scalar(left[:, :], left[:, :], ROUTED_SCALE, None, ALU.mult))
            link(dve.tensor_tensor(gt[:, :, :], gt[:, :, :], left[:, :].unsqueeze(2).broadcast_to([P, NT, NE]),
                                   ALU.mult))
            cp = [cparts[:, :, j * NE:(j + 1) * NE] for j in range(PARTS)]
            link(dve.tensor_copy(cp[0], gt[:, :, :]))
            link(dve.tensor_tensor(eq[:, :, :], gt[:, :, :], cp[0], ALU.subtract))
            link(dve.tensor_copy(cp[1], eq[:, :, :]))
            link(dve.tensor_tensor(cp[2], eq[:, :, :], cp[1], ALU.subtract))

            assert steps[0] == ROUTE

            with dve.Fori(0, NBLK) as i:
                for m in range(NC):
                    dve.wait_ge(spread, i * NC + m + 1)
                    dve.wait_ge(relu, i * NCH + m + 1)
                    dve.tensor_tensor(rc[:, m % 3, :], r[:, m % 3, :], bank[:, 2 + m % 2, :], ALU.mult)\
                       .then_inc(scaled, 1)
                per = 1 + 3 * BT
                dve.wait_ge(summed, i + 1)
                dve.tensor_tensor(y[:, :, :], bank[:, 4, :].rearrange("p (t f) -> p t f", t=BT), tiles(X, i),
                                  ALU.add).then_inc(ln_dve, 1)
                layernorm(dve, y, X, i, stats, mv, rstd, ln_dve, i * per + 1, ln_pool, 2 * i + 2, seen)



def layernorm(dve, y, X, i, stats, mv, rstd, ln_dve, at, ln_pool, pool_at, seen):
    dve.wait_ge(ln_dve, at)
    for t in range(BT):
        dve.bn_stats(stats[:, t, :], y[:, t, :]).then_inc(ln_dve, 1)
    dve.wait_ge(ln_dve, at + BT)
    dve.tensor_copy(seen[:, :], stats[:, 0, 0:1])
    for t in range(BT):
        dve.bn_aggr(mv[:, t, :], stats[:, t, :]).then_inc(ln_dve, 1)
    dve.wait_ge(ln_pool, pool_at)
    for t in range(BT):
        xo = X[:, i * BT + t:i * BT + t + 1, :] if isinstance(i, int) else X[:, bass.ds(i * BT + t, 1), :]
        dve.tensor_scalar(xo, y[:, t:t + 1, :], mv[:, t, 0:1], rstd[:, t:t + 1], ALU.subtract, ALU.mult)\
           .then_inc(ln_dve, 1)


def state_space(nc, top, X, ident_f, A_log, B_mat, C_mat, D_vec, W_dt, b_dt):
    with ExitStack() as ctx:
        def sb(name, shape, dt):
            return ctx.enter_context(nc.sbuf_tensor(f"ssm_{name}", shape, dt))

        def sem(name):
            return top.enter_context(nc.semaphore(f"ssm_{name}"))

        N = A_log.shape[1]
        HALF = T // 2
        HT = HALF // P
        QTR = T // 4
        raw_w = sb("raw_w", [D, D], F32)
        w = sb("w", [D, D], F32)
        bias = sb("bias", [D, 1], F32)
        a_log = sb("a_log", [D, N], F32)
        neg_a = sb("neg_a", [D, N + 2], F32)
        rate = sb("rate", [D, 2], F32)
        bmat = sb("bmat", [D, N], F32)
        cmat = sb("cmat", [D, N + 1], F32)
        diag = sb("diag", [D, N + 1, D], F32)
        u = sb("u", [D, T], F32)
        dt = sb("dt", [D, T], F32)
        dtu = sb("dtu", [D, T], F32)
        decay = sb("decay", [D, 2, HALF], F32)
        state = sb("state", [D, 2, HALF], F32)
        y = sb("y", [P, BT, D], F32)
        stats = sb("stats", [P, BT, 6], F32)
        mv = sb("mv", [P, BT, 2], F32)
        rstd = sb("rstd", [P, BT], F32)
        eps = sb("eps", [P, BT], F32)
        seen = sb("seen", [P, 1], F32)
        half_neg = sb("half_neg", [P, BT], F32)
        bank = ctx.enter_context(nc.psum_tensor("ssm_bank", [P, 8, 512], F32))

        loaded = sem("loaded")
        consts = sem("consts")
        turned = sem("turned")
        u_ready = sem("u_ready")
        w_ready = sem("w_ready")
        proj = sem("proj")
        z_ready = sem("z_ready")
        acts = sem("acts")
        softs = sem("softs")
        diags = sem("diags")
        rated = sem("rated")
        decayed = sem("decayed")
        scanned = sem("scanned")
        added = sem("added")
        ln_dve = sem("ln_dve")
        ln_pool = sem("ln_pool")
        block = ctx.enter_context(nc.Block())

        def scratch(c, k):
            buf = (decay, state)[k // 2]
            return buf[:, c % 2, (k % 2) * QTR:(k % 2 + 1) * QTR]

        @block.sync
        def _(sp):
            for dst, src in ((raw_w[:, :], W_dt), (a_log[:, :], A_log), (bmat[:, :], B_mat),
                             (cmat[:, 0:N], C_mat), (cmat[:, N:N + 1], D_vec.rearrange("(p o) -> p o", o=1)),
                             (bias[:, :], b_dt.rearrange("(p o) -> p o", o=1))):
                sp.dma_start(dst, src, allow_slow_non_contiguous=True).then_inc(loaded, 16)

        @block.gpsimd
        def _(pool):
            pool.memset(eps[:, :], EPS).then_inc(consts, 1)
            pool.memset(half_neg[:, :], -0.5).then_inc(consts, 1)
            pool.wait_ge(consts, 2)
            with pool.Fori(0, NBLK) as i:
                pool.wait_ge(ln_dve, i * (1 + 3 * BT) + 1 + 2 * BT)
                pool.tensor_tensor(rstd[:, :], mv[:, :, 1], eps[:, :], ALU.add).then_inc(ln_pool, 1)
                pool.wait_ge(ln_pool, 2 * i + 1)
                pool.tensor_tensor(rstd[:, :], rstd[:, :], half_neg[:, :], ALU.pow).then_inc(ln_pool, 1)

        @block.tensor
        def _(pe):
            for b in range(NBLK):
                for t in range(BT):
                    mm = pe.transpose(bank[:, b, t * P:(t + 1) * P], X[:, b * BT + t, :], ident_f[:, :])
                mm.then_inc(turned, 1)
            pe.wait_ge(loaded, 16 * 6)
            pe.wait_ge(u_ready, 1)
            pe.transpose(bank[:, 0, 0:D], raw_w[:, :], ident_f[:, :]).then_inc(turned, 1)
            pe.wait_ge(w_ready, 1)
            for b in range(NBLK):
                pe.wait_ge(u_ready, b + 1)
                pe.matmul(bank[:, b, :], w[:, :], u[:, b * BLK:(b + 1) * BLK], start=True, stop=True)\
                  .then_inc(proj, 1)
            pe.wait_ge(z_ready, 4)
            pe.wait_ge(diags, 2)

            def weigh(lhs, tile, rhs, first):
                return pe.matmul(bank[:, tile // BT, (tile % BT) * D:(tile % BT + 1) * D], lhs, rhs,
                                 start=first and tile % BT == 0, stop=True, skip_group_check=True)

            for h in range(2):
                for t in range(HT):
                    k = h * HT + t
                    mm = weigh(u[:, k * P:(k + 1) * P], k, diag[:, N, :], True)
                mm.then_inc(added, 1)
            with pe.Fori(0, N) as n:
                for h in range(2):
                    pe.wait_ge(scanned, 2 * n + h + 3)
                    for t in range(HT):
                        mm = weigh(state[:, h, t * P:(t + 1) * P], h * HT + t, diag[:, bass.ds(n, 1), :], False)
                    mm.then_inc(added, 1)

        @block.scalar
        def _(act):
            act.wait_ge(turned, NBLK + 1)
            act.activation(w[:, :], bank[:, 0, 0:D], ACT.Copy).then_inc(w_ready, 1)
            act.wait_ge(loaded, 16 * 6)
            act.activation(neg_a[:, 0:N], a_log[:, :], ACT.Exp).then_inc(w_ready, 1)
            for c in range(4):
                zs = dt[:, c * QTR:(c + 1) * QTR]
                act.wait_ge(z_ready, c + 1)
                if c >= 2:
                    act.wait_ge(softs, 5 * (c - 1))
                act.activation(scratch(c, 0), zs, ACT.Abs).then_inc(acts, 1)
                act.wait_ge(acts, 4 * c + 1)
                act.activation(scratch(c, 0), scratch(c, 0), ACT.Exp, scale=-1.0).then_inc(acts, 1)
                act.wait_ge(softs, 5 * c + 1)
                act.activation(scratch(c, 2), scratch(c, 1), ACT.Ln).then_inc(acts, 1)
                act.wait_ge(acts, 4 * c + 3)
                act.activation(scratch(c, 3), scratch(c, 2), ACT.Exp, scale=-1.0).then_inc(acts, 1)
            with act.Fori(0, N // 2) as i:
                for k in range(2):
                    n = 2 * i + k
                    act.wait_ge(rated, n + 1)
                    for h in range(2):
                        act.wait_ge(scanned, 2 * n + h + 1)
                        act.activation(decay[:, h, :].rearrange("p (b s) -> p b s", s=S)[:, :, 1:S],
                                       dt[:, h * HALF:(h + 1) * HALF].rearrange("p (b s) -> p b s", s=S)[:, :, 1:S],
                                       ACT.Exp, scale=rate[:, k:k + 1]).then_inc(decayed, 1)

        @block.vector
        def _(dve):
            for b in range(NBLK):
                dve.wait_ge(turned, b + 1)
                dve.tensor_copy(u[:, b * BLK:(b + 1) * BLK], bank[:, b, :]).then_inc(u_ready, 1)
            dve.wait_ge(loaded, 16 * 6)
            dve.tensor_tensor(cmat[:, 0:N], cmat[:, 0:N], bmat[:, :], ALU.mult).then_inc(diags, 1)

            def z(c):
                dve.wait_ge(proj, 2 * c + 2)
                dve.tensor_scalar(dt[:, c * QTR:(c + 1) * QTR].rearrange("p (a n) -> p a n", a=2),
                                  bank[:, 2 * c:2 * c + 2, :], bias[:, 0:1], None, ALU.add).then_inc(z_ready, 1)

            z(0)
            z(1)
            dve.wait_ge(diags, 1)
            dve.tensor_tensor(diag[:, :, :], ident_f[:, :].unsqueeze(1).broadcast_to([D, N + 1, D]),
                              cmat[:, :].unsqueeze(2).broadcast_to([D, N + 1, D]), ALU.mult).then_inc(diags, 1)
            dve.wait_ge(w_ready, 2)
            dve.tensor_scalar(neg_a[:, 0:N], neg_a[:, 0:N], -1.0, None, ALU.mult).then_inc(diags, 1)
            dve.memset(neg_a[:, N:N + 2], 0.0).then_inc(diags, 1)
            dve.wait_ge(diags, 4)
            for k in range(2):
                dve.tensor_copy(rate[:, k:k + 1], neg_a[:, k:k + 1]).then_inc(rated, 1)
            z(2)
            z(3)
            dve.wait_ge(u_ready, NBLK)
            for c in range(4):
                cols = slice(c * QTR, (c + 1) * QTR)
                e, one_e, ln, inv = (scratch(c, k) for k in range(4))
                dve.wait_ge(acts, 4 * c + 2)
                dve.tensor_scalar(one_e, e, 1.0, None, ALU.add).then_inc(softs, 1)
                dve.wait_ge(acts, 4 * c + 4)
                dve.wait_ge(softs, 5 * c + 1)
                dve.scalar_tensor_tensor(e, one_e, -1.0, e, ALU.add, ALU.subtract).then_inc(softs, 1)
                dve.scalar_tensor_tensor(dt[:, cols], dt[:, cols], 0.0, ln, ALU.max, ALU.add).then_inc(softs, 1)
                dve.wait_ge(softs, 5 * c + 2)
                dve.tensor_tensor(e, e, inv, ALU.mult).then_inc(softs, 1)
                dve.wait_ge(softs, 5 * c + 4)
                dve.tensor_tensor(dt[:, cols], dt[:, cols], e, ALU.subtract).then_inc(softs, 1)
                dve.wait_ge(softs, 5 * c + 5)
                dve.tensor_tensor(dtu[:, cols], dt[:, cols], u[:, cols], ALU.mult)
            for h in range(2):
                dve.memset(decay[:, h, :].rearrange("p (b s) -> p b s", s=S)[:, :, 0:1], 0.0).then_inc(scanned, 1)
            dve.wait_ge(scanned, 2)
            dve.wait_ge(rated, 2)
            with dve.Fori(0, N // 2) as i:
                for k in range(2):
                    n = 2 * i + k
                    for h in range(2):
                        dve.wait_ge(decayed, 2 * n + h + 1)
                        dve.wait_ge(added, 2 * n + h + 1)
                        dve.tensor_tensor_scan(state[:, h, :], decay[:, h, :], dtu[:, h * HALF:(h + 1) * HALF], 0.0,
                                               ALU.mult, ALU.add).then_inc(scanned, 1)
                    dve.tensor_copy(rate[:, k:k + 1], neg_a[:, bass.ds(n + 2, 1)]).then_inc(rated, 1)
            per = 1 + 3 * BT
            dve.wait_ge(added, 2 * N + 2)
            for i in range(NBLK):
                if i > 0:
                    dve.wait_ge(ln_dve, i * per)
                dve.tensor_tensor(y[:, :, :], bank[:, i, :].rearrange("p (t f) -> p t f", t=BT), tiles(X, i),
                                  ALU.add).then_inc(ln_dve, 1)
                layernorm(dve, y, X, i, stats, mv, rstd, ln_dve, i * per + 1, ln_pool, 2 * i + 2, seen)


def feed_forward(nc, top, X, ident_f, ones_row, W_fc, b_fc, A_fc, B_fc, W_proj, b_proj, A_proj, B_proj):
    with ExitStack() as ctx:
        def sb(name, shape, dt):
            return ctx.enter_context(nc.sbuf_tensor(f"ffn_{name}", shape, dt))

        def sem(name):
            return top.enter_context(nc.semaphore(f"ffn_{name}"))

        F = W_fc.shape[0]
        FC = F // P
        R = A_fc.shape[0]
        QMAX = 127.0
        ROUND = 1.5 * 2.0 ** 23
        raw = sb("raw", [P, 2, FC, P], F32)
        quant = sb("quant", [P, 2, FC, P], F32)
        tmp = sb("tmp", [P, 2, FC, P], F32)
        peak = sb("peak", [P, 2], F32)
        peaks = sb("peaks", [P, 2], F32)
        scale = sb("scale", [P, 2], F32)
        a_fc = sb("a_fc", [R, D], F32)
        b_fc_raw = sb("b_fc_raw", [P, FC, R], F32)
        a_proj = sb("a_proj", [R, F], F32)
        b_proj_raw = sb("b_proj_raw", [D, R], F32)
        bT = sb("bT", [R, F + D], F32)
        bias1 = sb("bias1", [P, FC], F32)
        bias2 = sb("bias2", [1, D], F32)
        w1 = sb("w1", [D, F], F32)
        w2 = sb("w2", [P, FC, D], F32)
        xT = sb("xT", [D, T], F32)
        g = sb("g", [P, 4, BLK], F32)
        y = sb("y", [P, BT, D], F32)
        stats = sb("stats", [P, BT, 6], F32)
        mv = sb("mv", [P, BT, 2], F32)
        rstd = sb("rstd", [P, BT], F32)
        eps = sb("eps", [P, BT], F32)
        seen = sb("seen", [P, 1], F32)
        half_neg = sb("half_neg", [P, BT], F32)
        bank = ctx.enter_context(nc.psum_tensor("ffn_bank", [P, 8, 512], F32))

        loaded = sem("loaded")
        consts = sem("consts")
        q_steps = sem("q_steps")
        peaked = sem("peaked")
        turned = sem("turned")
        took = sem("took")
        hidden = sem("hidden")
        gelus = sem("gelus")
        summed = sem("summed")
        ln_dve = sem("ln_dve")
        ln_pool = sem("ln_pool")
        block = ctx.enter_context(nc.Block())
        LOADS = 8
        QSTEPS = 9

        @block.sync
        def _(sp):
            for dst, src in ((raw[:, 0, :, :], W_fc.rearrange("(c p) i -> p c i", p=P)),
                             (raw[:, 1, :, :].rearrange("p c j -> p (c j)"), W_proj),
                             (a_fc[:, :], A_fc), (b_fc_raw[:, :, :], B_fc.rearrange("(c p) r -> p c r", p=P)),
                             (a_proj[:, :], A_proj), (b_proj_raw[:, :], B_proj),
                             (bias1[:, :], b_fc.rearrange("(c p) -> p c", p=P)),
                             (bias2[:, :], b_proj.rearrange("(o n) -> o n", o=1))):
                sp.dma_start(dst, src, allow_slow_non_contiguous=True).then_inc(loaded, 16)

        @block.gpsimd
        def _(pool):
            pool.memset(eps[:, :], EPS).then_inc(consts, 1)
            pool.memset(half_neg[:, :], -0.5).then_inc(consts, 1)
            pool.wait_ge(q_steps, 1)
            pool.partition_all_reduce(peaks[:, :], peak[:, :], P, bass.bass_isa.ReduceOp.max).then_inc(peaked, 1)
            pool.wait_ge(consts, 2)
            with pool.Fori(0, NBLK) as i:
                pool.wait_ge(ln_dve, i * (1 + 3 * BT) + 1 + 2 * BT)
                pool.tensor_tensor(rstd[:, :], mv[:, :, 1], eps[:, :], ALU.add).then_inc(ln_pool, 1)
                pool.wait_ge(ln_pool, 2 * i + 1)
                pool.tensor_tensor(rstd[:, :], rstd[:, :], half_neg[:, :], ALU.pow).then_inc(ln_pool, 1)

        @block.tensor
        def _(pe):
            for b in range(NBLK):
                for t in range(BT):
                    mm = pe.transpose(bank[:, b, t * P:(t + 1) * P], X[:, b * BT + t, :], ident_f[:, :])
                mm.then_inc(turned, 1)
            pe.wait_ge(loaded, 16 * LOADS)
            pe.wait_ge(took, 2)
            for c in range(FC):
                mm = pe.transpose(bank[0:R, 0, c * P:(c + 1) * P], b_fc_raw[:, c, :], ident_f[:, :])
            mm = pe.transpose(bank[0:R, 1, 0:D], b_proj_raw[:, :], ident_f[:, :])
            mm.then_inc(turned, 1)
            pe.wait_ge(took, NBLK + 2)
            pe.wait_ge(q_steps, QSTEPS)
            for c in range(FC):
                o = bank[:, 2, c * P:(c + 1) * P]
                pe.matmul(o, quant[:, 0, c, :], ident_f[:, :], start=(c == 0), stop=False, skip_group_check=True)
                mm = pe.matmul(o, a_fc[:, :], bT[:, c * P:(c + 1) * P], start=False, stop=True,
                               skip_group_check=True)
            mm.then_inc(turned, 1)
            for c in range(FC):
                o = bank[:, 3, c * D:(c + 1) * D]
                pe.matmul(o, quant[:, 1, c, :], ident_f[:, :], start=(c == 0), stop=False, skip_group_check=True)
                mm = pe.matmul(o, a_proj[:, c * P:(c + 1) * P], bT[:, F:F + D], start=False, stop=True,
                               skip_group_check=True)
            mm.then_inc(turned, 1)
            pe.wait_ge(took, NBLK + 4)
            with pe.Fori(0, NBLK) as i:
                xb = xT[:, bass.ds(i * BLK, BLK)]
                for m in range(FC):
                    pe.matmul(bank[:, m, :], w1[:, m * P:(m + 1) * P], xb, start=True, stop=True)\
                      .then_inc(hidden, 1)
                for t in range(BT):
                    pe.matmul(bank[:, 4, t * D:(t + 1) * D], ones_row[:, :], bias2[:, :],
                              start=(t == 0), stop=False, skip_group_check=True)
                for m in range(FC):
                    pe.wait_ge(gelus, i * FC + m + 1)
                    for t in range(BT):
                        mm = pe.matmul(bank[:, 4, t * D:(t + 1) * D], g[:, m, t * P:(t + 1) * P], w2[:, m, :],
                                       start=False, stop=(m == FC - 1), skip_group_check=True)
                mm.then_inc(summed, 1)
                pe.wait_ge(ln_dve, i * (1 + 3 * BT) + 1)

        @block.scalar
        def _(act):
            for b in range(NBLK):
                act.wait_ge(turned, b + 1)
                act.activation(xT[:, b * BLK:(b + 1) * BLK], bank[:, b, :], ACT.Copy).then_inc(took, 1)
            act.wait_ge(turned, NBLK + 1)
            act.activation(bT[:, 0:F], bank[0:R, 0, :], ACT.Copy, scale=SCALING).then_inc(took, 1)
            act.activation(bT[:, F:F + D], bank[0:R, 1, 0:D], ACT.Copy, scale=SCALING).then_inc(took, 1)
            act.wait_ge(turned, NBLK + 2)
            act.activation(w1[:, :], bank[:, 2, :], ACT.Copy).then_inc(took, 1)
            act.wait_ge(turned, NBLK + 3)
            act.activation(w2[:, :, :].rearrange("p c n -> p (c n)"), bank[:, 3, :], ACT.Copy).then_inc(took, 1)
            act.wait_ge(loaded, 16 * LOADS)
            with act.Fori(0, NBLK) as i:
                for m in range(FC):
                    act.wait_ge(hidden, i * FC + m + 1)
                    act.activation(g[:, m, :], bank[:, m, :], ACT.Gelu, bias=bias1[:, m:m + 1]).then_inc(gelus, 1)

        @block.vector
        def _(dve):
            steps = [0]

            def link(ins):
                steps[0] += 1
                ins.then_inc(q_steps, 1)
                dve.wait_ge(q_steps, steps[0])

            dve.wait_ge(loaded, 16 * LOADS)
            flat = lambda x: x[:, :, :, :].rearrange("p w c j -> p w (c j)")
            both = lambda x: x[:, :].unsqueeze(2).broadcast_to([P, 2, F])
            link(dve.tensor_reduce(peak[:, :], flat(raw), AX.X, ALU.max, apply_absolute_value=True))
            dve.wait_ge(peaked, 1)
            link(dve.tensor_scalar(scale[:, :], peaks[:, :], 1.0 / QMAX, None, ALU.mult))
            link(dve.reciprocal(peak[:, :], scale[:, :]))
            link(dve.tensor_tensor(flat(quant), flat(raw), both(peak), ALU.mult))
            link(dve.tensor_scalar(quant[:, :, :, :], quant[:, :, :, :], ROUND, -ROUND, ALU.add, ALU.add))
            link(dve.tensor_scalar(quant[:, :, :, :], quant[:, :, :, :], QMAX, -QMAX - 1.0, ALU.min, ALU.max))
            link(dve.tensor_tensor(flat(quant), flat(quant), both(scale), ALU.mult))
            link(dve.tensor_tensor(flat(tmp), flat(quant), flat(raw), ALU.subtract))
            link(dve.tensor_tensor(flat(quant), flat(tmp), flat(raw), ALU.add))
            assert steps[0] == QSTEPS
            per = 1 + 3 * BT
            with dve.Fori(0, NBLK) as i:
                dve.wait_ge(summed, i + 1)
                dve.tensor_tensor(y[:, :, :], bank[:, 4, :].rearrange("p (t f) -> p t f", t=BT), tiles(X, i),
                                  ALU.add).then_inc(ln_dve, 1)
                layernorm(dve, y, X, i, stats, mv, rstd, ln_dve, i * per + 1, ln_pool, 2 * i + 2, seen)
                dve.wait_ge(ln_dve, i * per + per)


def build(nc, a, out):
    with ExitStack() as ctx:
        def sb(name, shape, dt):
            return ctx.enter_context(nc.sbuf_tensor(name, shape, dt))

        X = sb("X", [P, NT, D], F32)
        ident_f = sb("ident_f", [P, P], F32)
        ident_b = sb("ident_b", [P, P], BF16)
        ones_row = sb("ones_row", [1, P], F32)
        fold = sb("fold", [P, DH + 1], F32)
        constants(nc, ctx, a["x"], X, ident_f, ident_b, ones_row, fold)
        common = (X, ident_f, ident_b, ones_row, fold)
        attention(nc, ctx, Attention("self", S), *common, None,
                  SelfWeights(a["L0_attn_qkv_w"], a["L0_attn_out_w"], a["L0_attn_out_b"]))
        attention(nc, ctx, Attention("cross0", NKV), *common, a["ctx_768"],
              CrossWeightsIn(*(a["L0_xattn_" + k] for k in
                               ("w_q", "b_q", "w_k", "b_k", "w_v", "b_v", "w_o", "b_o"))))
        experts(nc, ctx, X, ident_f, ident_b, a)
        state_space(nc, ctx, X, ident_f, *(a["L1_attn_" + k] for k in
                                           ("A_log", "B_mat", "C_mat", "D_vec", "W_dt", "b_dt")))
        attention(nc, ctx, Attention("cross1", NKV), *common, a["ctx_768"],
              CrossWeightsOut(*(a["L1_xattn_" + k] for k in ("Wq", "bq", "Wkv", "bkv", "Wo", "bo"))))
        feed_forward(nc, ctx, X, ident_f, ones_row, *(a["L1_ffn_" + k] for k in
                     ("W_fc", "b_fc", "A_fc", "B_fc", "W_proj", "b_proj", "A_proj", "B_proj")))
        store(nc, ctx, X, out)



_INS = ["x", "ctx_768", "L0_attn_qkv_w", "L0_attn_out_w", "L0_attn_out_b", "L0_xattn_w_q", "L0_xattn_b_q",
        "L0_xattn_w_k", "L0_xattn_b_k", "L0_xattn_w_v", "L0_xattn_b_v", "L0_xattn_w_o", "L0_xattn_b_o",
        "L0_ffn_gate_w", "L0_ffn_e_bias", "L0_ffn_up_w", "L0_ffn_down_w", "L0_ffn_shared_up_w",
        "L0_ffn_shared_down_w", "L1_attn_A_log", "L1_attn_B_mat", "L1_attn_C_mat", "L1_attn_D_vec",
        "L1_attn_W_dt", "L1_attn_b_dt", "L1_xattn_Wq", "L1_xattn_bq", "L1_xattn_Wkv", "L1_xattn_bkv",
        "L1_xattn_Wo", "L1_xattn_bo", "L1_ffn_W_fc", "L1_ffn_b_fc", "L1_ffn_A_fc", "L1_ffn_B_fc",
        "L1_ffn_W_proj", "L1_ffn_b_proj", "L1_ffn_A_proj", "L1_ffn_B_proj"]


def kernel(**inputs):
    import numpy as _np
    import concourse.bacc as _bacc
    from concourse import mybir as _mybir
    from concourse.bass_utils import run_bass_kernel_spmd as _run

    nc = _bacc.Bacc("TRN2", target_bir_lowering=False, num_devices=1)
    arrays, args = {}, {}
    for name in _INS:
        a = _np.ascontiguousarray(inputs[name])
        arrays[f"in_{name}_dram"] = a
        args[name] = nc.dram_tensor(f"in_{name}_dram", a.shape, _mybir.dt.from_np(a.dtype),
                                    kind="ExternalInput").ap()
    out = nc.dram_tensor("out_dram", arrays["in_x_dram"].shape, _mybir.dt.float32, kind="ExternalOutput").ap()
    build(nc, args, out)
    r = _run(nc, [arrays], core_ids=[0])
    return r.results[0]["out_dram"]
```

```python
from contextlib import ExitStack

import numpy as np

import concourse.bass as bass
from concourse import mybir

F32 = mybir.dt.float32
BF16 = mybir.dt.bfloat16
ALU = mybir.AluOpType
ACT = mybir.ActivationFunctionType
AX = mybir.AxisListType

P = 128
B, S, D = 16, 256, 128
H, DH = 16, 8
NKV, DC = 1601, 96
QT = S // P
NT = B * QT
EPS = 1e-5
SCALE = 1.0 / float(np.sqrt(np.float32(DH)))
PARTS = 3
STACK = PARTS * PARTS * DH
MROW = 96
KROWS = MROW + PARTS
TWO_ONES = 0x3F803F80
PAIR = 2
VR = DH + 1


def heads_to_groups(ap, groups):
    return ap.rearrange("p (g l d) -> p g d l", g=groups, d=DH)


def as_groups(ap, groups):
    return ap.rearrange("p (g d l) -> p g d l", g=groups, d=DH)


class Attention:

    def __init__(self, name, keys):
        self.name = name
        self.keys = keys
        self.cross = keys != S
        self.groups, self.bufs = (2, 1) if self.cross else (1, 2)
        self.gh = H // self.groups
        self.gp = self.gh * DH
        self.chunks = [(s, min(P, keys - s)) for s in range(0, keys, P)]
        self.nch = len(self.chunks)
        self.units = (self.nch + 1) // 2
        self.nb = H * self.units
        self.quads = min(4, self.nch)
        self.pvs = (self.units + 1) // 2
        self.nw = H * self.pvs
        self.npr = 8
        self.fold_lag = 4 if self.cross else 3
        self.keep = 4
        assert self.nb % self.npr == 0
        if self.cross:
            self.block = (keys + 3) // 4
            self.block_step = (keys - 1) // 4
            self.max_units = QT * 2
            self.ahead, self.ahead_rows = 2, 1
            assert 3 * self.block_step + self.block == keys
            self.ksplit = [(s, min(256, keys - s)) for s in range(0, keys, 256)]
        else:
            self.block = keys
            self.max_units = 1
            self.ahead, self.ahead_rows = 4, 2
            self.ksplit = [(0, keys)]
        self.prep = ["XT"] + (["CT0", "CT1"] if self.cross else []) + ["Q", "K0"] + (["K1"] if self.cross else [])
        self.values = ["V0", "V1"] if self.cross else ["V0"]
        self.reader = {"A": "dve", "XT": "act", "CT0": "dve", "CT1": "dve", "Q": "dve", "K0": "dve",
                       "K1": "dve", "V0": "dve", "V1": "dve", "ONT": "act", "OUT": "dve"}
        self.pro = self._prologue()
        self.plans = {"pro": self.pro, "first": self._iteration(False, True), "loop": self._iteration(True, True),
                      "last": self._iteration(True, False)}
        self.ring = {p: [e for slot in plan for e in slot if e[0] in self.reader]
                     for p, plan in self.plans.items()}
        self.n_pro = len(self.ring["pro"])
        self.n_first = len(self.ring["first"])
        self.n_loop = len(self.ring["loop"])
        assert self.n_loop % 2 == 0

    def _prologue(self):
        slots = [[(k, 0)] for k in self.prep[:-1] if k not in ("K0", "K1")]
        slots += [[("SPLIT_Q", 0)]]
        slots += [[(k, 0)] for k in self.prep if k in ("K0", "K1")]
        slots += [[("SPLIT_K", 0, j)] for j in range(len(self.ksplit))]
        slots += [[(k, 0)] for k in self.values]
        slots += [[("VX", h, 0)] for h in range(2)]
        slots += [[("A", h, k, 0)] for h in range(self.ahead) for k in range(self.max_units)]
        slots += [[("MT", h, 0)] for h in range(self.ahead_rows)]
        return slots

    def _iteration(self, has_before, has_next):
        n, u = self.nb, self.units
        slots = [[] for _ in range(n + 12)]
        for g in range(n):
            slots[g].append(("B", g))
        if has_before:
            for step, at in self._end():
                slots[at].append((*step, -1))
        for h in range(1, H, PAIR):
            if (h + 1) * u + self.fold_lag < n:
                slots[(h + 1) * u + self.fold_lag].append(("FOLD", h, 0))
        for h in range(H - 2):
            slots[h * u + (4 if self.cross else 0)].append(("VX", h + 2, 0))
        if has_next:
            nxt = 1
            if self.cross:
                at = {"XT": 1, "CT0": u + 1, "CT1": 2 * u + 1, "Q": u + 5, "K0": 3 * u + 1, "K1": 4 * u + 3,
                      "V0": 13 * u + 3, "V1": 14 * u + 3}
                slots[3 * u + 2].append(("SPLIT_Q", nxt))
                for j in range(len(self.ksplit)):
                    slots[4 * u + 6 * j + 1].append(("SPLIT_K", nxt, j))
            else:
                at = {"XT": 0, "Q": 1, "K0": 2, "V0": 14}
                slots[2].append(("SPLIT_Q", nxt))
                slots[3].append(("SPLIT_K", nxt, 0))
            for k, s in at.items():
                slots[s].append((k, nxt))
            for h in range(2):
                slots[15 * u + 3 * h + 1 if self.cross else n - 1].append(("VX", h, 1))
        for h in range(H):
            ha, hm = h + self.ahead, h + self.ahead_rows
            for k in range(self.max_units):
                if has_next or ha < H:
                    slots[h * u + 2 * k].append(("A", ha % H, k, ha // H))
            if has_next or hm < H:
                at = h * u + (5 if h in (0, H - 1) else 4) if self.cross else (4 if h == 3 else h)
                slots[at].append(("MT", hm % H, hm // H))
        for h in range(H):
            for j in range(self.pvs):
                at = h * u + min(2 * j + 1, u - 1) + 2
                if at < n:
                    slots[at].append(("PV", h, j, 0))
            if h % PAIR == PAIR - 1 and (h + 1) * u + 1 < n:
                slots[(h + 1) * u + 1].append(("EV", h, 0))
        if not has_next:
            for step, at in self._end():
                slots[n + at].append((*step, 0))
        assert has_next is False or not any(slots[n:])
        return slots if not has_next else slots[:n]

    def _end(self):
        n, u = self.nb, self.units
        steps = []
        for at in range(n, n + 5):
            steps += [(("FOLD", h), at - n) for h in range(1, H, PAIR) if (h + 1) * u + self.fold_lag == at]
            steps += [(("PV", h, j), at - n) for h in range(H) for j in range(self.pvs)
                      if h * u + min(2 * j + 1, u - 1) + 2 == at]
            steps += [(("EV", h), at - n) for h in range(1, H, PAIR) if (h + 1) * u + 1 == at]
        last = 5 if self.cross else 4
        return steps + [(("ON",), self.fold_lag), (("ONT",), last + 1), (("OUT",), last + 3), (("LN",), last + 6)]

    def splitter(self, part):
        return "pool" if self.cross and part != "pro" else "dve"

    def ring_slot(self, part, k):
        return {"pro": k, "first": self.n_pro + k}.get(part, self.n_pro + self.n_first + k) % 2

    def ring_at(self, part, k, i):
        return {"pro": k, "first": self.n_pro + k}.get(
            part, self.n_pro + self.n_first + self.n_loop * (i - 1) + k)

    def released(self, part, k, i, who):
        count = lambda units: sum(self.reader[e[0]] == who for e in units)
        here = count(self.ring[part][:k])
        if part == "pro":
            return here
        if part == "first":
            return count(self.ring["pro"]) + here
        return count(self.ring["pro"]) + count(self.ring["first"]) + (i - 1) * count(self.ring["loop"]) + here


def attention(nc, top, cfg, X, ident_f, ident_b, ones_row, fold, ctx_dram, wts):
    n = cfg.name
    with ExitStack() as ctx:
        def sb(name, shape, dt):
            return ctx.enter_context(nc.sbuf_tensor(f"{n}_{name}", shape, dt))

        def pb(name, shape, dt):
            return ctx.enter_context(nc.psum_tensor(f"{n}_{name}", shape, dt))

        def sem(name):
            return top.enter_context(nc.semaphore(f"{n}_{name}"))

        NK, U, NB = cfg.keys, cfg.units, cfg.nb
        NKP = NK + NK % 2
        GROUPS, GH, GP = cfg.groups, cfg.gh, cfg.gp
        KD = DC + 1 if cfg.cross else D
        wq = sb("wq", [D, D], F32)
        wk = sb("wk", [KD, D], F32)
        wv = sb("wv", [KD, D], F32)
        wo = sb("wo", [D, D], F32)
        bq = sb("bq", [D, 1], F32)
        bo = sb("bo", [1, D], F32)
        raw = sb("raw", [P, 4, D], F32)
        raw_k = sb("raw_k", [P, 2, DC + 1], F32)
        xs = sb("xs", [P, QT, D], F32)
        xT = sb("xT", [D, S], F32)
        C = sb("C", [P, cfg.nch, DC], F32) if cfg.cross else None
        cT = sb("cT", [DC + 1, NK], F32) if cfg.cross else xT
        qf = sb("qf", [D, S], F32)
        kf = sb("kf", [D, NK], F32)
        res = sb("res", [D, 512], F32)
        qparts = sb("qparts", [D, PARTS, S], BF16)
        kparts = sb("kparts", [D, PARTS, NKP], BF16)
        Qs = [sb(f"Q{j}", [KROWS, H, S], BF16) for j in range(cfg.bufs)]
        Ks = [sb(f"K{j}", [KROWS, H, NKP], BF16) for j in range(cfg.bufs)]
        Vf = sb("Vf", [P, cfg.nch, H, DH], F32)
        V32 = sb("V32", [P, cfg.keep, cfg.nch, 32], F32)
        nm4 = sb("nm4", [P, cfg.keep, QT, 2], F32)
        nm = sb("nm", [P, cfg.keep, QT], F32)
        mres = sb("mres", [P, cfg.keep, QT], F32)
        mp = sb("mp", [P, cfg.keep, QT, PARTS + 1], BF16)
        Pr = sb("Pr", [P, cfg.npr, 2 * S], F32)
        OTs = sb("OTs", [32 * cfg.quads, 2, S], F32)
        rden = sb("rden", [P, QT * H], F32)
        On = sb("On", [P, QT, D], F32)
        OnT = sb("OnT", [D, S], F32)
        y = sb("y", [P, QT, D], F32)
        stats = sb("stats", [P, QT, 6], F32)
        mv = sb("mv", [P, QT, 2], F32)
        rstd = sb("rstd", [P, QT], F32)
        half_neg = sb("half_neg", [P, QT], F32)
        eps = sb("eps", [P, QT], F32)
        one = sb("one", [P, 1], F32)
        seen = sb("seen", [P, 1], F32)

        ring = pb("ring", [P, 2, 1024], F32)
        sT = pb("sT", [P, 2, 512], F32)
        oT = pb("oT", [P, S], F32)
        pm = pb("pm", [P, 512], F32)
        om = pm[:, 0:QT * H * (DH + 1)].rearrange("p (t h r) -> p t h r", t=QT, h=H)
        mrow = pm[:, 384:512].bitcast(BF16)

        w_loaded = sem("w_loaded")
        w_turned = sem("w_turned")
        w_ready = sem("w_ready")
        rows_set = sem("rows_set")
        ctx_in = sem("ctx_in")
        xs_ready = sem("xs_ready")
        filled = sem("filled")
        by = {"dve": sem("ring_dve"), "act": sem("ring_act")}
        split_q = sem("split_q")
        split_k = sem("split_k")
        stacked = [sem(f"stacked{g}") for g in range(GROUPS)]
        max_done = sem("max_done")
        max_split = sem("max_split")
        max_turned = sem("max_turned")
        max_rows = sem("max_rows")
        scored = sem("scored")
        exped = sem("exped")
        v_zero = sem("v_zero")
        v_ready = sem("v_ready")
        weighed = sem("weighed")
        o_out = sem("o_out")
        folded = sem("folded")
        recips = sem("recips")
        on_ready = sem("on_ready")
        ln_dve = sem("ln_dve")
        ln_pool = sem("ln_pool")

        tensors = dict(wq=wq, wk=wk, wv=wv, wo=wo, bq=bq, bo=bo, raw=raw, raw_k=raw_k)
        NPV = cfg.nw
        PV = cfg.pvs
        READY = wts.n_ready + (5 if cfg.cross else 3) + cfg.keep
        SQ = 4 * 1
        SK = 4 * len(cfg.ksplit)
        STK = 16 * 18

        def fill_wait(pe, part, k, i):
            if k >= 2:
                who = cfg.reader[cfg.ring[part][k - 2][0]]
                pe.wait_ge(by[who], cfg.released(part, k - 1, i, who))
            elif part != "pro":
                two = [cfg.reader[e[0]] for e in cfg.ring["pro" if part == "first" else "first"][-2:]]
                who = two[k]
                pe.wait_ge(by[who], cfg.released(part, 0, i, who) - (1 if k == 0 and two[1] == who else 0))

        def parts_of(eng, body):
            body("pro", cfg.plans["pro"], 0, 0)
            body("first", cfg.plans["first"], 0, 0)
            assert (B - 2) % cfg.bufs == 0
            with eng.Fori(0, (B - 2) // cfg.bufs) as j:
                for k in range(cfg.bufs):
                    body("loop", cfg.plans["loop"], cfg.bufs * j + k + 1, (k + 1) % cfg.bufs)
            body("last", cfg.plans["last"], B - 1, (B - 1) % cfg.bufs)

        def rows(c):
            return cfg.chunks[c][1]

        def split(eng, src, dst, sm, at):
            r = res[:, 0:src.shape[1]]
            ones = one[:, :].broadcast_to([P, src.shape[1]])
            eng.tensor_tensor(dst[0], src, ones, ALU.mult).then_inc(sm, 1)
            eng.wait_ge(sm, at + 1)
            eng.tensor_tensor(r, src, dst[0], ALU.subtract).then_inc(sm, 1)
            eng.wait_ge(sm, at + 2)
            eng.tensor_tensor(dst[1], r, ones, ALU.mult).then_inc(sm, 1)
            eng.wait_ge(sm, at + 3)
            eng.tensor_tensor(dst[2], r, dst[1], ALU.subtract).then_inc(sm, 1)

        def split_step(eng, e, part, i):
            nb = i if part == "pro" else i + 1
            if e[0] == "SPLIT_Q":
                qn = [j for j, x in enumerate(cfg.ring[part]) if x[0] == "Q"][0]
                eng.wait_ge(by["dve"], cfg.released(part, qn + 1, i, "dve"))
                if part != "pro":
                    for g in range(GROUPS):
                        eng.wait_ge(stacked[g], STK * (i + 1))
                    eng.wait_ge(split_k, SK * nb)
                split(eng, qf[:, :], [qparts[:, a, :] for a in range(PARTS)], split_q, SQ * nb)
            if e[0] == "SPLIT_K":
                j = e[2]
                unit = "K0" if cfg.ksplit[j][0] + cfg.ksplit[j][1] <= 1024 else "K1"
                kn = [x[0] for x in cfg.ring[part]].index(unit)
                eng.wait_ge(by["dve"], cfg.released(part, kn + 1, i, "dve"))
                if j == 0:
                    eng.wait_ge(split_q, SQ * (nb + 1))
                else:
                    eng.wait_ge(split_k, SK * nb + 4 * j)
                s, w = cfg.ksplit[j]
                split(eng, kf[:, s:s + w], [kparts[:, a, s:s + w] for a in range(PARTS)],
                      split_k, SK * nb + 4 * j)

        block = ctx.enter_context(nc.Block())

        @block.sync
        def _(sp):
            loads = wts.loads(tensors)
            for dst, src in loads:
                sp.dma_start(dst, src, allow_slow_non_contiguous=True).then_inc(w_loaded, 16)

            def load_x(b):
                src = X[:, QT * b:QT * (b + 1), :] if isinstance(b, int) else X[:, bass.ds(b * QT, QT), :]
                sp.dma_start(xs[:, :, :], src).then_inc(xs_ready, 16)

            def load_ctx(b):
                full = (NK // P) * P
                if isinstance(b, int):
                    src = ctx_dram[b:b + 1]
                else:
                    src = ctx_dram[bass.ds(b, 1)]
                sp.dma_start(C[:, 0:NK // P, :],
                             src[:, 0:full, :].rearrange("o (c p) f -> p (o c) f", p=P)).then_inc(ctx_in, 16)
                sp.dma_start(C[0:NK - full, NK // P, :],
                             src[:, full:NK, :].rearrange("o p f -> (o p) f")).then_inc(ctx_in, 16)

            def stack(g, buf=0):
                for parts, dst, side, w in ((qparts, Qs[buf], 0, S), (kparts, Ks[buf], 1, NK)):
                    for a in range(PARTS):
                        for b in range(PARTS):
                            r = (a * PARTS + b) * DH
                            sp.dma_start(dst[r:r + DH, g * GH:(g + 1) * GH, 0:w],
                                         parts[g * GP:(g + 1) * GP, a if side else b, 0:w])\
                              .then_inc(stacked[g], 16)

            load_x(0)
            if cfg.cross:
                load_ctx(0)
            sp.wait_ge(rows_set, 2 * cfg.bufs)
            sp.wait_ge(split_q, SQ)
            sp.wait_ge(split_k, SK)
            stack(0)
            load_x(1)
            if cfg.cross:
                load_ctx(1)
                stack(1)

            def body(i, buf, has_next):
                sp.wait_ge(split_k, SK * (i + 2))
                if has_next and cfg.cross:
                    load_x(i + 2)
                    load_ctx(i + 2)
                if cfg.cross:
                    sp.wait_ge(scored, NB * i + NB // 2)
                    stack(0)
                    sp.wait_ge(scored, NB * i + NB)
                    stack(1)
                else:
                    if not (isinstance(i, int) and i == 0):
                        sp.wait_ge(scored, NB * i)
                    stack(0, buf)
                    if has_next:
                        load_x(i + 2)

            if cfg.cross:
                with sp.Fori(0, B - 2) as i:
                    body(i, 0, True)
            else:
                body(0, 1, True)
                with sp.Fori(0, (B - 4) // 2) as j:
                    for k in range(2):
                        body(2 * j + k + 1, k % 2, True)
                body(B - 3, B % 2, True)
            body(B - 2, (B - 1) % cfg.bufs, False)

        @block.gpsimd
        def _(pool):
            pool.memset(half_neg[:, :], -0.5).then_inc(w_ready, 1)
            pool.memset(eps[:, :], EPS).then_inc(w_ready, 1)
            pool.memset(one[:, :], 1.0).then_inc(w_ready, 1)
            if cfg.cross:
                pool.memset(Vf[:, cfg.nch - 1, :, :], 0.0).then_inc(w_ready, 1)
            pool.memset(V32[:, :, :, :], 0.0).then_inc(v_zero, 1)
            pool.wait_ge(v_zero, 1)
            for k in range(cfg.keep):
                end = (k % PAIR + 1) * VR
                pool.memset(V32[:, k, :, end - 1:end], 1.0).then_inc(w_ready, 1)

            pool.wait_ge(w_ready, READY)
            rows_above = [(T[64:MROW, :, :], 0) for T in Qs + Ks] + [(T[MROW:KROWS, :, :], TWO_ONES) for T in Ks]
            for k, (r, v) in enumerate(rows_above):
                pool.memset(r.rearrange("p h n -> p (h n)").bitcast(mybir.dt.uint32), v).then_inc(rows_set, 1)
                pool.wait_ge(rows_set, k + 1)

            def body(part, plan, i, buf):
                k_ring = 0
                for slot in plan:
                    for e in slot:
                        ring_now = k_ring
                        if e[0] in cfg.reader:
                            k_ring += 1
                        nb = i if part == "pro" else i + 1
                        if e[0] in ("SPLIT_Q", "SPLIT_K") and cfg.splitter(part) == "pool":
                            split_step(pool, e, part, i)
                        if e[0] == "VX":
                            _, h, nxt = e
                            gh = (i + nxt) * H + h
                            if nxt or part == "pro":
                                vn = max(m for m, x in enumerate(cfg.ring[part]) if x[0] in ("V0", "V1"))
                                pool.wait_ge(by["dve"], cfg.released(part, vn + 1, i, "dve"))
                            if part == "pro":
                                pool.wait_ge(w_ready, READY)
                            if part != "pro" and not (part == "first" and not nxt and h < cfg.keep):
                                pool.wait_ge(weighed, (gh - cfg.keep + 1) * PV)
                            pool.tensor_tensor(V32[:, h % cfg.keep, :, (h % 2) * VR:(h % 2) * VR + DH], Vf[:, :, h, :],
                                               one[:, :].unsqueeze(2).broadcast_to([P, cfg.nch, DH]), ALU.mult).then_inc(v_ready, 1)
                        if e[0] == "A" and e[2] == cfg.max_units - 1:
                            h = e[1]
                            gh = (i + e[3]) * H + h
                            sl = h % cfg.keep
                            ones = one[:, :].broadcast_to([P, QT])
                            if cfg.cross:
                                pool.wait_ge(max_done, gh + 1)
                            else:
                                pool.wait_ge(by["dve"], cfg.released(part, ring_now + 1, i, "dve"))
                            if not ((part == "pro" or part == "first" and not e[3]) and h < cfg.keep):
                                pool.wait_ge(max_turned, gh - cfg.keep + 1)
                            pool.tensor_tensor(mp[:, sl, :, 0], nm[:, sl, :], ones, ALU.mult).then_inc(max_split, 1)
                            pool.wait_ge(max_split, 4 * gh + 1)
                            pool.tensor_tensor(mres[:, sl, :], nm[:, sl, :], mp[:, sl, :, 0],
                                               ALU.subtract).then_inc(max_split, 1)
                            pool.wait_ge(max_split, 4 * gh + 2)
                            pool.tensor_tensor(mp[:, sl, :, 1], mres[:, sl, :], ones,
                                               ALU.mult).then_inc(max_split, 1)
                            pool.wait_ge(max_split, 4 * gh + 3)
                            pool.tensor_tensor(mp[:, sl, :, 2], mres[:, sl, :], mp[:, sl, :, 1],
                                               ALU.subtract).then_inc(max_split, 1)
                        if e[0] == "OUT":
                            b = i + e[1]
                            pool.wait_ge(ln_dve, 6 * b + 4)
                            pool.tensor_tensor(rstd[:, :], mv[:, :, 1], eps[:, :], ALU.add).then_inc(ln_pool, 1)
                            pool.wait_ge(ln_pool, 2 * b + 1)
                            pool.tensor_tensor(rstd[:, :], rstd[:, :], half_neg[:, :], ALU.pow)\
                                .then_inc(ln_pool, 1)

            parts_of(pool, body)

        @block.tensor
        def _(pe):
            wts.turn(pe, tensors, ring, w_loaded, w_turned, ident_f)
            pe.wait_ge(w_ready, READY)

            def body(part, plan, i, buf):
                k = 0
                turned = 0
                normalized = None
                for slot in plan:
                    for e in slot:
                        op = e[0]
                        if op in cfg.reader:
                            fill_wait(pe, part, k, i)
                            R = ring[:, cfg.ring_slot(part, k), :]
                            k += 1
                        nb = i if part == "pro" else i + 1
                        if op == "XT":
                            pe.wait_ge(xs_ready, 16 * (nb + 1))
                            for t in range(QT):
                                mm = pe.transpose(R[:, t * P:(t + 1) * P], xs[:, t, :], ident_f[:, :])
                            mm.then_inc(filled, 1)
                        elif op in ("CT0", "CT1"):
                            if op == "CT0":
                                pe.wait_ge(ctx_in, 32 * (nb + 1))
                            lo, hi = (0, 8) if op == "CT0" else (8, cfg.nch)
                            for c in range(lo, hi):
                                r = rows(c)
                                mm = pe.transpose(R[0:DC, (c - lo) * P:(c - lo) * P + r], C[0:r, c, :],
                                                  ident_f[0:r, 0:r])
                            mm.then_inc(filled, 1)
                        elif op == "Q":
                            pe.wait_ge(by["act"], cfg.released(part, 1 + [x[0] for x in cfg.ring[part]].index("XT"),
                                                               i, "act"))
                            pe.matmul(R[:, 0:S], wq[:, :], xT[:, :], start=True, stop=True).then_inc(filled, 1)
                        elif op in ("K0", "K1"):
                            names = [x[0] for x in cfg.ring[part]]
                            if op == "K0" and cfg.cross:
                                pe.wait_ge(by["dve"], cfg.released(part, 1 + names.index("CT1"), i, "dve"))
                            lo, hi = (0, min(1024, NK)) if op == "K0" else (1024, NK)
                            for s in range(lo, hi, 512):
                                w = min(512, hi - s)
                                mm = pe.matmul(R[:, s - lo:s - lo + w], wk[:, :], cT[0:KD, s:s + w],
                                               start=True, stop=True)
                            mm.then_inc(filled, 1)
                        elif op in ("V0", "V1"):
                            lo, hi = (0, min(8, cfg.nch)) if op == "V0" else (8, cfg.nch)
                            for c in range(lo, hi):
                                s, r = cfg.chunks[c]
                                mm = pe.matmul(R[0:r, (c - lo) * D:(c - lo + 1) * D], cT[0:KD, s:s + r], wv[:, :],
                                               start=True, stop=True)
                            mm.then_inc(filled, 1)
                        elif op == "A":
                            _, h, m, nxt = e
                            b = i + nxt
                            Q, K = Qs[(buf + nxt) % cfg.bufs], Ks[(buf + nxt) % cfg.bufs]
                            if m == 0 and h % GH == 0:
                                pe.wait_ge(stacked[h // GH], STK * (b + 1))
                            if cfg.cross:
                                t, half = m // 2, m % 2
                                for j in range(2):
                                    s = (2 * half + j) * cfg.block_step
                                    mm = pe.matmul(R[:, 512 * j:512 * j + cfg.block],
                                                   Q[0:STACK, h, t * P:(t + 1) * P],
                                                   K[0:STACK, h, s:s + cfg.block], start=True, stop=True)
                            else:
                                for t in range(QT):
                                    mm = pe.matmul(R[:, 512 * t:512 * t + NK], Q[0:STACK, h, t * P:(t + 1) * P],
                                                   K[0:STACK, h, 0:NK], start=True, stop=True)
                            mm.then_inc(filled, 1)
                        elif op == "MT":
                            _, h, nxt = e
                            gh = (i + nxt) * H + h
                            pe.wait_ge(max_split, 4 * (gh + 1))
                            if normalized is not None:
                                pe.wait_ge(on_ready, normalized + 1)
                                normalized = None
                            if not (part == "pro" and h == 0):
                                pe.wait_ge(max_rows, gh)
                            for t in range(QT):
                                mm = pe.transpose(mrow[0:PARTS, t * P:(t + 1) * P], mp[:, h % cfg.keep, t, 0:PARTS],
                                                  ident_b[:, :])
                            mm.then_inc(max_turned, 1)
                            turned += 1
                        elif op == "B":
                            Q, K = Qs[buf], Ks[buf]
                            h, u = divmod(e[1], U)
                            if u == 0:
                                pe.wait_ge(max_rows, i * H + h + 1)
                            if e[1] >= 2 or part != "first":
                                pe.wait_ge(exped, i * NB + e[1] - 1)
                            for c in range(2 * u, min(2 * u + 2, cfg.nch)):
                                s, r = cfg.chunks[c]
                                mm = pe.matmul(sT[0:r, e[1] % 2, (c % 2) * S:(c % 2 + 1) * S],
                                               K[0:KROWS, h, s:s + r], Q[0:KROWS, h, :], start=True, stop=True)
                            mm.then_inc(scored, 1)
                        elif op == "PV":
                            _, h, j, d = e
                            b = i + d
                            first, end = 2 * j, min(2 * j + 2, U)
                            pe.wait_ge(exped, b * NB + h * U + end)
                            if j == 0:
                                pe.wait_ge(v_ready, b * H + h + 1)
                                if h % PAIR == 0 and (h > 0 or part != "first"):
                                    pe.wait_ge(o_out, b * (H // PAIR) + h // PAIR)
                            for c in range(2 * first, min(2 * end, cfg.nch)):
                                r = rows(c)
                                slot = (h * U + c // 2) % cfg.npr
                                alone = cfg.cross and c == cfg.nch - 1
                                for q, s, w in ([(q, q * S // 4, S // 4) for q in range(4)] if alone else
                                                [(c % 4, 0, S)]):
                                    mm = pe.matmul(oT[32 * q:32 * q + 32, s:s + w], V32[0:r, h % cfg.keep, c, :],
                                                   Pr[0:r, slot, (c % 2) * S + s:(c % 2) * S + s + w],
                                                   start=(c < 4 and h % PAIR == 0), stop=(c + 4 >= cfg.nch or alone),
                                                   tile_position=(0, 32 * q), skip_group_check=True)
                            mm.then_inc(weighed, 1)
                        elif op == "ON":
                            normalized = i + e[1]
                        elif op == "FOLD":
                            _, h, d = e
                            b = i + d
                            pe.wait_ge(o_out, b * (H // PAIR) + h // PAIR + 1)
                            if normalized is not None:
                                pe.wait_ge(on_ready, normalized + 1)
                                normalized = None
                            pe.wait_ge(max_rows, cfg.ahead_rows + i * H + turned)
                            for t in range(QT):
                                mm = pe.matmul(om[:, t, h - 1:h + 1, :], OTs[:, h // PAIR % 2, t * P:(t + 1) * P],
                                               fold[0:32 * cfg.quads, :], start=True, stop=True)
                            mm.then_inc(folded, 1)
                        elif op == "ONT":
                            pe.wait_ge(on_ready, i + e[1] + 1)
                            for t in range(QT):
                                mm = pe.transpose(R[:, t * P:(t + 1) * P], On[:, t, :], ident_f[:, :])
                            mm.then_inc(filled, 1)
                        elif op == "OUT":
                            pe.wait_ge(by["act"], cfg.released(part, k - 1, i, "act"))
                            for t in range(QT):
                                pe.matmul(R[:, t * D:(t + 1) * D], OnT[:, t * P:(t + 1) * P], wo[:, :],
                                          start=(t == 0), stop=False, skip_group_check=True)
                                mm = pe.matmul(R[:, t * D:(t + 1) * D], ones_row[:, :], bo[:, :],
                                               start=False, stop=(t == QT - 1), skip_group_check=True)
                            mm.then_inc(filled, 1)

            parts_of(pe, body)

        @block.scalar
        def _(act):
            def body(part, plan, i, buf):
                k = 0
                for slot in plan:
                    for e in slot:
                        op = e[0]
                        if op in cfg.reader:
                            R = ring[:, cfg.ring_slot(part, k), :]
                            if cfg.reader[op] == "act":
                                act.wait_ge(filled, cfg.ring_at(part, k, i) + 1)
                            k += 1
                        if op == "XT":
                            act.activation(xT[:, :], R[:, 0:S], ACT.Copy).then_inc(by["act"], 1)
                        elif op == "MT":
                            _, h, nxt = e
                            gh = (i + nxt) * H + h
                            act.wait_ge(max_turned, gh + 1)
                            Q = Qs[(buf + nxt) % cfg.bufs]
                            if part == "pro":
                                act.wait_ge(rows_set, 3 * cfg.bufs)
                            act.activation(Q[MROW:KROWS, h, :], mrow[0:PARTS, :], ACT.Copy).then_inc(max_rows, 1)
                        elif op == "B":
                            g = e[1]
                            u = g % U
                            act.wait_ge(scored, i * NB + g + 1)
                            if g >= cfg.npr:
                                ho, uo = divmod(g - cfg.npr, U)
                                act.wait_ge(weighed, i * NPV + ho * PV + uo // 2 + 1)
                            elif part != "first":
                                ho, uo = divmod(NB + g - cfg.npr, U)
                                act.wait_ge(weighed, (i - 1) * NPV + ho * PV + uo // 2 + 1)
                            nchunk = min(2, cfg.nch - 2 * u)
                            r = rows(2 * u)
                            act.activation(Pr[0:r, g % cfg.npr, 0:nchunk * S], sT[0:r, g % 2, 0:nchunk * S],
                                           ACT.Exp).then_inc(exped, 1)
                        elif op == "EV":
                            _, h, d = e
                            gh = (i + d) * H + h
                            act.wait_ge(weighed, (gh + 1) * PV)
                            gp = (i + d) * (H // PAIR) + h // PAIR
                            if h >= 2 * PAIR or part != "first":
                                act.wait_ge(folded, gp - 1)
                            act.activation(OTs[:, h // PAIR % 2, :], oT[0:32 * cfg.quads, :],
                                           ACT.Copy).then_inc(o_out, 1)
                        elif op == "ONT":
                            act.activation(OnT[:, :], R[:, 0:S], ACT.Copy).then_inc(by["act"], 1)

            parts_of(act, body)

        @block.vector
        def _(dve):
            wts.place(dve, tensors, ring,
                         w_loaded, w_turned, w_ready)
            if cfg.cross:
                dve.memset(cT[DC:DC + 1, :], 1.0).then_inc(w_ready, 1)
            def body(part, plan, i, buf):
                k = 0
                for slot in plan:
                    for e in slot:
                        op = e[0]
                        if op in cfg.reader:
                            R = ring[:, cfg.ring_slot(part, k), :]
                            if cfg.reader[op] == "dve":
                                dve.wait_ge(filled, cfg.ring_at(part, k, i) + 1)
                            k += 1
                        nb = i if part == "pro" else i + 1
                        if op in ("SPLIT_Q", "SPLIT_K") and cfg.splitter(part) == "dve":
                            split_step(dve, e, part, i)
                        if op in ("CT0", "CT1"):
                            lo, hi = (0, 1024) if op == "CT0" else (1024, NK)
                            dve.tensor_copy(cT[0:DC, lo:hi], R[0:DC, 0:hi - lo]).then_inc(by["dve"], 1)
                        elif op in ("K0", "K1"):
                            if op == "K0" and part != "pro":
                                dve.wait_ge(split_k, SK * nb)
                            lo, hi = (0, min(1024, NK)) if op == "K0" else (1024, NK)
                            dve.tensor_copy(kf[:, lo:hi], R[:, 0:hi - lo]).then_inc(by["dve"], 1)
                        elif op == "Q":
                            if part != "pro":
                                dve.wait_ge(split_q, SQ * nb)
                            if part == "pro":
                                dve.wait_ge(w_ready, READY)
                            dve.tensor_scalar(qf[:, :], R[:, 0:S], bq[:, 0:1], SCALE, ALU.add, ALU.mult)\
                               .then_inc(by["dve"], 1)
                        elif op in ("V0", "V1"):
                            lo, hi = (0, min(8, cfg.nch)) if op == "V0" else (8, cfg.nch)
                            if part == "pro":
                                dve.wait_ge(w_ready, READY)
                            else:
                                dve.wait_ge(v_ready, (i + 1) * H)
                            full = hi if rows(hi - 1) == P else hi - 1
                            last = dve.tensor_copy(
                                Vf[:, lo:full, :, :],
                                R[:, 0:(full - lo) * D].rearrange("p (c h d) -> p c h d", h=H, d=DH))
                            if full < hi:
                                r = rows(full)
                                last = dve.tensor_copy(
                                    Vf[0:r, full, :, :],
                                    R[0:r, (full - lo) * D:(full - lo + 1) * D].rearrange("p (h d) -> p h d", d=DH))
                            last.then_inc(by["dve"], 1)
                        elif op == "A":
                            _, h, m, nxt = e
                            gh = (i + nxt) * H + h
                            sl = h % cfg.keep
                            if m == 0 and not ((part == "pro" or part == "first" and not nxt) and h < cfg.keep):
                                dve.wait_ge(max_split, 4 * (gh - cfg.keep + 1))
                            if cfg.cross:
                                t, half = m // 2, m % 2
                                dve.tensor_reduce(
                                    nm4[:, sl, t, half:half + 1],
                                    R.rearrange("p (j n) -> p j n", j=2)[:, :, 0:cfg.block],
                                    AX.XY, ALU.max, negate=True).then_inc(by["dve"], 1)
                                if m == cfg.max_units - 1:
                                    dve.wait_ge(by["dve"], cfg.released(part, k, i, "dve"))
                                    dve.tensor_tensor(nm[:, sl, :], nm4[:, sl, :, 0], nm4[:, sl, :, 1],
                                                      ALU.min).then_inc(max_done, 1)
                            else:
                                dve.tensor_reduce(
                                    nm[:, sl, :], R.rearrange("p (t n) -> p t n", t=2)[:, :, 0:NK],
                                    AX.X, ALU.max, negate=True).then_inc(by["dve"], 1)
                        elif op == "ON":
                            b = i + e[1]
                            dve.wait_ge(folded, (b + 1) * (H // PAIR))
                            dve.reciprocal(rden[:, :].rearrange("p (t h) -> p t h", t=QT),
                                           om[:, :, :, DH]).then_inc(recips, 1)
                            dve.wait_ge(recips, b + 1)
                            dve.tensor_tensor(
                                On[:, :, :].rearrange("p t (h d) -> p (t h) d", d=DH),
                                om[:, :, :, 0:DH].rearrange("p t h d -> p (t h) d"),
                                rden[:, :].unsqueeze(2).broadcast_to([P, QT * H, DH]),
                                ALU.mult).then_inc(on_ready, 1)
                        elif op == "OUT":
                            b = i + e[1]
                            xb = X[:, 2 * b:2 * b + 2, :] if isinstance(b, int) else X[:, bass.ds(b * 2, 2), :]
                            dve.tensor_tensor(y[:, :, :], R[:, 0:QT * D].rearrange("p (t f) -> p t f", t=QT),
                                              xb, ALU.add).then_inc(by["dve"], 1)
                            dve.wait_ge(by["dve"], cfg.released(part, k, i, "dve"))
                            for t in range(QT):
                                dve.bn_stats(stats[:, t, :], y[:, t, :]).then_inc(ln_dve, 1)
                            dve.wait_ge(ln_dve, 6 * b + 2)
                            dve.tensor_copy(seen[:, :], stats[:, 0, 0:1])
                            for t in range(QT):
                                dve.bn_aggr(mv[:, t, :], stats[:, t, :]).then_inc(ln_dve, 1)
                        elif op == "LN":
                            b = i + e[1]
                            dve.wait_ge(ln_pool, 2 * b + 2)
                            for t in range(QT):
                                xo = X[:, 2 * b + t, :] if isinstance(b, int) else X[:, bass.ds(b * 2 + t, 1), :]
                                dve.tensor_scalar(xo, y[:, t, :] if isinstance(b, int) else y[:, t:t + 1, :],
                                                  mv[:, t, 0:1], rstd[:, t:t + 1],
                                                  ALU.subtract, ALU.mult).then_inc(ln_dve, 1)

            parts_of(dve, body)


class SelfWeights:
    n_ready = 5

    def __init__(self, qkv_w, out_w, out_b):
        self.qkv_w, self.out_w, self.out_b = qkv_w, out_w, out_b

    def loads(self, t):
        return [(t["raw"][:, 0:3, :], self.qkv_w.rearrange("(j p) c -> p j c", p=P)),
                (t["raw"][:, 3, :], self.out_w),
                (t["bo"][:, :], self.out_b.rearrange("(o n) -> o n", o=1))]

    def turn(self, pe, t, ring, w_loaded, w_turned, ident_f):
        pe.wait_ge(w_loaded, 16 * 3)
        for j in range(4):
            mm = pe.transpose(ring[:, 0, j * D:(j + 1) * D], t["raw"][:, j, :], ident_f[:, :])
        mm.then_inc(w_turned, 1)

    def place(self, dve, t, ring, w_loaded, w_turned, w_ready):
        dve.wait_ge(w_turned, 1)
        for j, w in enumerate((t["wq"], t["wk"])):
            dve.tensor_copy(as_groups(w[:, :], 1), heads_to_groups(ring[:, 0, j * D:(j + 1) * D], 1)).then_inc(w_ready, 1)
        for j, w in ((2, t["wv"]), (3, t["wo"])):
            dve.tensor_copy(w[:, :], ring[:, 0, j * D:(j + 1) * D]).then_inc(w_ready, 1)
        dve.memset(t["bq"][:, :], 0.0).then_inc(w_ready, 1)


GROUPS = 2


class CrossWeightsIn:
    n_ready = 3

    def __init__(self, w_q, b_q, w_k, b_k, w_v, b_v, w_o, b_o):
        self.w_q, self.b_q, self.w_k, self.b_k = w_q, b_q, w_k, b_k
        self.w_v, self.b_v, self.w_o, self.b_o = w_v, b_v, w_o, b_o

    def loads(self, t):
        row = lambda v: v.rearrange("(o n) -> o n", o=1)
        return [(t["raw"][:, 0, :], self.w_q),
                (t["raw"][0:DC, 1, :], self.w_k), (t["raw"][DC:DC + 1, 1, :], row(self.b_k)),
                (t["raw"][0:DC, 2, :], self.w_v), (t["raw"][DC:DC + 1, 2, :], row(self.b_v)),
                (t["wo"][:, :], self.w_o), (t["bo"][:, :], row(self.b_o))] + bias_in_groups(t["bq"], self.b_q)

    def turn(self, pe, t, ring, w_loaded, w_turned, ident_f):
        pe.wait_ge(w_loaded, 16 * (7 + GROUPS))

    def place(self, dve, t, ring, w_loaded, w_turned, w_ready):
        dve.wait_ge(w_loaded, 16 * (7 + GROUPS))
        raw = t["raw"]
        dve.tensor_copy(as_groups(t["wq"][:, :], GROUPS), heads_to_groups(raw[:, 0, :], GROUPS)).then_inc(w_ready, 1)
        dve.tensor_copy(as_groups(t["wk"][:, :], GROUPS), heads_to_groups(raw[0:DC + 1, 1, :], GROUPS)).then_inc(w_ready, 1)
        dve.tensor_copy(t["wv"][:, :], raw[0:DC + 1, 2, :]).then_inc(w_ready, 1)


class CrossWeightsOut:
    n_ready = 4

    def __init__(self, Wq, bq, Wkv, bkv, Wo, bo):
        self.Wq, self.bq, self.Wkv, self.bkv, self.Wo, self.bo = Wq, bq, Wkv, bkv, Wo, bo

    def loads(self, t):
        return [(t["raw"][:, 0, :], self.Wq), (t["raw"][:, 1, :], self.Wo),
                (t["raw_k"][:, :, 0:DC], self.Wkv.rearrange("(j p) c -> p j c", p=P)),
                (t["raw_k"][:, :, DC], self.bkv.rearrange("(j p) -> p j", p=P)),
                (t["bo"][:, :], self.bo.rearrange("(o n) -> o n", o=1))] + bias_in_groups(t["bq"], self.bq)

    def turn(self, pe, t, ring, w_loaded, w_turned, ident_f):
        pe.wait_ge(w_loaded, 16 * (5 + GROUPS))
        for j in range(2):
            pe.transpose(ring[:, 0, j * D:(j + 1) * D], t["raw"][:, j, :], ident_f[:, :])
        for j in range(2):
            mm = pe.transpose(ring[0:DC + 1, 0, 512 + j * P:512 + (j + 1) * P], t["raw_k"][:, j, :], ident_f[:, :])
        mm.then_inc(w_turned, 1)

    def place(self, dve, t, ring, w_loaded, w_turned, w_ready):
        dve.wait_ge(w_turned, 1)
        dve.tensor_copy(as_groups(t["wq"][:, :], GROUPS), heads_to_groups(ring[:, 0, 0:D], GROUPS)).then_inc(w_ready, 1)
        dve.tensor_copy(t["wo"][:, :], ring[:, 0, D:2 * D]).then_inc(w_ready, 1)
        kv = ring[0:DC + 1, 0, 512:512 + 2 * D].rearrange("p (g l s d) -> p s g d l", g=GROUPS, s=2, d=DH)
        dve.tensor_copy(as_groups(t["wk"][:, :], GROUPS), kv[:, 0]).then_inc(w_ready, 1)
        v = ring[0:DC + 1, 0, 512:512 + 2 * D].rearrange("p (h s d) -> p s h d", h=H, s=2)
        dve.tensor_copy(t["wv"][:, :].rearrange("p (h d) -> p h d", h=H), v[:, 1]).then_inc(w_ready, 1)


def bias_in_groups(dst, src):
    v = src.rearrange("(g l d o) -> g d l o", g=GROUPS, d=DH, o=1)
    return [(dst[g * (D // GROUPS):(g + 1) * (D // GROUPS), :], v[g]) for g in range(GROUPS)]


def constants(nc, ctx, x_dram, X, ident_f, ident_b, ones_row, fold):
    x_in = ctx.enter_context(nc.semaphore("x_in"))
    set_ = ctx.enter_context(nc.semaphore("constants_set"))
    block = nc.Block()
    with block:
        @block.sync
        def _(sp):
            for q in range(4):
                n = NT // 4
                sp.dma_start(X[:, q * n:(q + 1) * n, :],
                             x_dram.rearrange("b (t p) f -> p (b t) f", p=P)[:, q * n:(q + 1) * n, :])\
                  .then_inc(x_in, 16)
            sp.wait_ge(x_in, 16 * 4)
            sp.nop()

        @block.gpsimd
        def _(pool):
            pool.memset(ident_f[:, :], 0.0).then_inc(set_, 1)
            pool.memset(ident_b[:, :], 0.0).then_inc(set_, 1)
            pool.memset(ones_row[:, :], 1.0).then_inc(set_, 1)
            pool.memset(fold[:, :], 0.0).then_inc(set_, 1)
            pool.wait_ge(set_, 4)
            for m in (ident_f, ident_b):
                pool.affine_select(out=m[:, :], in_=m[:, :], compare_op=ALU.not_equal, fill=1.0, base=0,
                                   pattern=[[-1, P]], channel_multiplier=1).then_inc(set_, 1)
            for q in range(4):
                pool.wait_ge(set_, 6 + q)
                pool.affine_select(out=fold[:, :], in_=fold[:, :], compare_op=ALU.not_equal, fill=1.0,
                                   base=-32 * q, pattern=[[-1, PAIR * VR]], channel_multiplier=1).then_inc(set_, 1)


def store(nc, ctx, X, out):
    stored = ctx.enter_context(nc.semaphore("stored"))
    with nc.Block() as block:
        @block.sync
        def _(sp):
            sp.dma_start(out.rearrange("b (t p) f -> p (b t) f", p=P), X[:, :, :]).then_inc(stored, 16)
            sp.wait_ge(stored, 16)


T = B * S
BLK = 512
BT = BLK // P
NBLK = T // BLK
NE, NGRP, TOPK, TOPG = 32, 8, 6, 4
MI, SI = 64, 256
ROUTED_SCALE = 2.5
SCALING = 2.0


def tiles(x, i):
    return x[:, i * BT:(i + 1) * BT, :] if isinstance(i, int) else x[:, bass.ds(i * BT, BT), :]


def experts(nc, top, X, ident_f, ident_b, a):
    NC = NE * MI // P
    NCH = NC + SI // P
    with ExitStack() as ctx:
        def sb(name, shape, dt):
            return ctx.enter_context(nc.sbuf_tensor(f"moe_{name}", shape, dt))

        def sem(name):
            return top.enter_context(nc.semaphore(f"moe_{name}"))

        raw_up = sb("raw_up", [P, NCH, D], F32)
        raw_down = sb("raw_down", [D, NCH, P], F32)
        raw_gate = sb("raw_gate", [NE, D], F32)
        up = sb("up", [D, NCH, P], F32)
        down = sb("down", [P, NCH, D], F32)
        gate = sb("gate", [D, NE], F32)
        ebias = sb("ebias", [P, NE], F32)
        xT = sb("xT", [D, T], F32)
        sel = sb("sel", [PARTS * NE, NC, P], BF16)
        cT = sb("cT", [PARTS * NE, T], BF16)
        s0 = sb("s0", [P, NT, NE], F32)
        sc = sb("sc", [P, NT, NE], F32)
        pair = sb("pair", [P, 4, NT, NGRP], F32)
        gsum = sb("gsum", [P, NT, NGRP], F32)
        top8 = sb("top8", [P, NT, 8], F32)
        gt = sb("gt", [P, NT, NE], F32)
        eq = sb("eq", [P, NT, NE], F32)
        cum = sb("cum", [P, NT, NE], F32)
        left = sb("left", [P, NT], F32)
        restart_g = sb("restart_g", [P, NT, NGRP], F32)
        restart_e = sb("restart_e", [P, NT, NE], F32)
        cparts = sb("cparts", [P, NT, PARTS * NE], BF16)
        r = sb("r", [P, 3, BLK], F32)
        rc = sb("rc", [P, 3, BLK], F32)
        hh = sb("hh", [P, 3, BLK], F32)
        y = sb("y", [P, BT, D], F32)
        stats = sb("stats", [P, BT, 6], F32)
        mv = sb("mv", [P, BT, 2], F32)
        rstd = sb("rstd", [P, BT], F32)
        half_neg = sb("half_neg", [P, BT], F32)
        eps = sb("eps", [P, BT], F32)
        seen = sb("seen", [P, 1], F32)

        bank = ctx.enter_context(nc.psum_tensor("moe_bank", [P, 8, 512], F32))
        ROUTE = 44
        NW = 2 * NCH // 4
        turned_units = NW + 1 + NBLK

        loaded = sem("loaded")
        turned = sem("turned")
        took_act = sem("took_act")
        took_dve = sem("took_dve")
        logits = sem("logits")
        sig = sem("sig")
        chain = sem("chain")
        consts = sem("consts")
        c_turned = sem("c_turned")
        c_took = sem("c_took")
        up_done = sem("up_done")
        spread = sem("spread")
        relu = sem("relu")
        scaled = sem("scaled")
        hidden = sem("hidden")
        summed = sem("summed")
        ln_dve = sem("ln_dve")
        ln_pool = sem("ln_pool")
        block = ctx.enter_context(nc.Block())

        def weight_tile(j):
            return (raw_up[:, j, :], up[:, j, :]) if j < NCH else (raw_down[:, j - NCH, :], down[:, j - NCH, :])

        def took(n, eng):
            if n >= 4:
                eng.wait_ge(took_act if n % 2 == 0 else took_dve, (n - 4) // 2 + 1)

        def half(eng, j, n):
            copy = (lambda o, s: eng.activation(o, s, ACT.Copy)) if n % 2 == 0 else eng.tensor_copy
            sm = took_act if n % 2 == 0 else took_dve
            flat_up = up[:, :, :].rearrange("p m n -> p (m n)")
            flat_down = down[:, :, :].rearrange("p m n -> p (m n)")
            a_n = max(0, min(4, NCH - j))
            ins = None
            if a_n:
                ins = copy(flat_up[:, j * P:(j + a_n) * P], bank[:, n % 4, 0:a_n * P])
            if a_n < 4:
                k = j + a_n - NCH
                ins = copy(flat_down[:, k * P:(k + 4 - a_n) * P], bank[:, n % 4, a_n * P:512])
            ins.then_inc(sm, 1)

        @block.sync
        def _(sp):
            sp.dma_start(raw_gate[:, :], a["L0_ffn_gate_w"]).then_inc(loaded, 16)
            sp.dma_start(ebias[:, :], a["L0_ffn_e_bias"].partition_broadcast(P)).then_inc(loaded, 16)
            sp.dma_start(raw_up[:, 0:NC, :], a["L0_ffn_up_w"].rearrange("(m e) i h -> (e i) m h", e=P // MI))\
              .then_inc(loaded, 16)
            sp.dma_start(raw_up[:, NC:NCH, :], a["L0_ffn_shared_up_w"].rearrange("(m p) h -> p m h", p=P))\
              .then_inc(loaded, 16)
            sp.dma_start(raw_down[:, 0:NC, :].rearrange("h m (e i) -> h (m e) i", e=P // MI),
                         a["L0_ffn_down_w"].rearrange("e h i -> h e i")).then_inc(loaded, 16)
            sp.dma_start(raw_down[:, NC:NCH, :].rearrange("h m i -> h (m i)"), a["L0_ffn_shared_down_w"])\
              .then_inc(loaded, 16)

        @block.gpsimd
        def _(pool):
            pool.memset(sel[:, :, :], 0.0).then_inc(consts, 1)
            pool.memset(half_neg[:, :], -0.5).then_inc(consts, 1)
            pool.memset(eps[:, :], EPS).then_inc(consts, 1)
            n = 3
            for part in range(PARTS):
                for e in range(P // MI):
                    v = sel[:, :, e * MI:(e + 1) * MI]
                    pool.wait_ge(consts, n)
                    pool.affine_select(out=v, in_=v, compare_op=ALU.not_equal, fill=1.0,
                                       base=-(part * NE + e), pattern=[[-(P // MI), NC], [0, MI]],
                                       channel_multiplier=1).then_inc(consts, 1)
                    n += 1

            def roots(i):
                pool.wait_ge(ln_dve, i * (1 + 3 * BT) + 1 + 2 * BT)
                pool.tensor_tensor(rstd[:, :], mv[:, :, 1], eps[:, :], ALU.add).then_inc(ln_pool, 1)
                pool.wait_ge(ln_pool, 2 * i + 1)
                pool.tensor_tensor(rstd[:, :], rstd[:, :], half_neg[:, :], ALU.pow).then_inc(ln_pool, 1)

            def square(i, has_before):
                for m in range(NCH):
                    q = m % 3
                    if m < NC:
                        pool.wait_ge(scaled, i * NC + m + 1)
                        pool.tensor_tensor(hh[:, q, :], r[:, q, :], rc[:, q, :], ALU.mult).then_inc(hidden, 1)
                    else:
                        pool.wait_ge(relu, i * NCH + m + 1)
                        pool.tensor_tensor(hh[:, q, :], r[:, q, :], r[:, q, :], ALU.mult).then_inc(hidden, 1)
                    if has_before and m == 3:
                        roots(i - 1)

            square(0, False)
            with pool.Fori(1, NBLK) as i:
                square(i, True)
            roots(NBLK - 1)

        @block.tensor
        def _(pe):
            pe.wait_ge(loaded, 16 * 6)
            n = 0
            pe.transpose(bank[:, 0, 0:NE], raw_gate[:, :], ident_f[0:NE, 0:NE]).then_inc(turned, 1)
            n += 1
            for b in range(NBLK):
                took(n, pe)
                for t in range(BT):
                    mm = pe.transpose(bank[:, n % 4, t * P:(t + 1) * P], X[:, b * BT + t, :], ident_f[:, :])
                mm.then_inc(turned, 1)
                n += 1
            pe.wait_ge(took_act, (NBLK // 2) + 1)
            pe.wait_ge(took_dve, NBLK // 2)
            for t in range(NT):
                mm = pe.matmul(bank[:, 4 + t // 16, (t % 16) * NE:(t % 16 + 1) * NE], xT[:, t * P:(t + 1) * P],
                               gate[:, :], start=True, stop=True)
            mm.then_inc(logits, 1)
            for w in range(NW):
                took(n, pe)
                for t in range(4):
                    mm = pe.transpose(bank[:, n % 4, t * P:(t + 1) * P], weight_tile(4 * w + t)[0], ident_f[:, :])
                mm.then_inc(turned, 1)
                n += 1
            assert n == turned_units
            pe.wait_ge(took_act, (n + 1) // 2)
            pe.wait_ge(took_dve, n // 2)
            pe.wait_ge(chain, ROUTE)
            for u in range(4):
                ct = bank[:, u, :].bitcast(BF16)
                for t in range(8):
                    mm = pe.transpose(ct[0:PARTS * NE, t * P:(t + 1) * P], cparts[:, u * 8 + t, :], ident_b[:, :])
                mm.then_inc(c_turned, 1)
            pe.wait_ge(c_took, 4)
            pe.wait_ge(consts, 3 + PARTS * P // MI)

            def up_and_spread(i, m):
                first = isinstance(i, int) and i == 0 and m < 2
                xb, cb = ((x[:, i * BLK:(i + 1) * BLK] if isinstance(i, int) else x[:, bass.ds(i * BLK, BLK)])
                          for x in (xT, cT))
                if not first:
                    pe.wait_ge(relu, i * NCH + m - 1)
                pe.matmul(bank[:, m % 2, :], up[:, m, :], xb, start=True, stop=True).then_inc(up_done, 1)
                if m < NC:
                    if not first:
                        pe.wait_ge(scaled, i * NC + m - 1)
                    pe.matmul(bank[:, 2 + m % 2, :], sel[:, m, :], cb, start=True, stop=True)\
                      .then_inc(spread, 1)

            def output(i, m):
                pe.wait_ge(hidden, i * NCH + m + 1)
                if m == 0 and not (isinstance(i, int) and i == 0):
                    pe.wait_ge(ln_dve, (i - 1) * (1 + 3 * BT) + 1)
                for t in range(BT):
                    mm = pe.matmul(bank[:, 4, t * D:(t + 1) * D], hh[:, m % 3, t * P:(t + 1) * P], down[:, m, :],
                                   start=(m == 0 and t == 0), stop=(m == NCH - 1), skip_group_check=True)
                if m == NCH - 1:
                    mm.then_inc(summed, 1)

            def block_of(i, has_next):
                for m in range(NCH):
                    if m + 2 < NCH:
                        up_and_spread(i, m + 2)
                    elif has_next:
                        up_and_spread(i + 1, m + 2 - NCH)
                    output(i, m)

            up_and_spread(0, 0)
            up_and_spread(0, 1)
            block_of(0, True)
            with pe.Fori(1, NBLK - 1) as i:
                block_of(i, True)
            block_of(NBLK - 1, False)

        @block.scalar
        def _(act):
            n = 0
            for n in range(0, turned_units, 2):
                act.wait_ge(turned, n + 1)
                if n == 0:
                    ins = act.activation(gate[:, :], bank[:, 0, 0:NE], ACT.Copy)
                elif n <= NBLK:
                    ins = act.activation(xT[:, (n - 1) * BLK:n * BLK], bank[:, n % 4, :], ACT.Copy)
                else:
                    j = 4 * (n - 1 - NBLK)
                    half(act, j, n)
                    ins = None
                if ins is not None:
                    ins.then_inc(took_act, 1)
                if n == NBLK:
                    act.wait_ge(logits, 1)
                    act.activation(s0[:, :, :].rearrange("p t e -> p (t e)"),
                                   bank[:, 4:6, :].rearrange("p a n -> p (a n)"), ACT.Sigmoid).then_inc(sig, 1)
            for u in range(4):
                act.wait_ge(c_turned, u + 1)
                act.activation(cT[:, u * 1024:(u + 1) * 1024], bank[0:PARTS * NE, u, :].bitcast(BF16),
                               ACT.Copy).then_inc(c_took, 1)
            def rectify(i):
                for m in range(NCH):
                    act.wait_ge(up_done, i * NCH + m + 1)
                    if m >= 3 or not isinstance(i, int):
                        act.wait_ge(hidden, i * NCH + m - 2)
                    act.activation(r[:, m % 3, :], bank[:, m % 2, :], ACT.Relu).then_inc(relu, 1)

            rectify(0)
            with act.Fori(1, NBLK) as i:
                rectify(i)

        steps = [0]

        @block.vector
        def _(dve):
            def link(ins):
                steps[0] += 1
                ins.then_inc(chain, 1)
                dve.wait_ge(chain, steps[0])

            def take(n):
                dve.wait_ge(turned, n + 1)
                if n <= NBLK:
                    dve.tensor_copy(xT[:, (n - 1) * BLK:n * BLK], bank[:, n % 4, :]).then_inc(took_dve, 1)
                else:
                    half(dve, 4 * (n - 1 - NBLK), n)

            for n in range(1, NBLK + 1, 2):
                take(n)
            for x, w in ((restart_g, NGRP), (restart_e, NE)):
                link(dve.memset(x[:, :, :], 1.0))
                link(dve.memset(x[:, :, 0:1], 0.0))
            for n in range(NBLK + 1, turned_units, 2):
                take(n)
            dve.wait_ge(sig, 1)
            dve.wait_ge(loaded, 16 * 6)
            link(dve.tensor_tensor(sc[:, :, :], s0[:, :, :], ebias[:, :].unsqueeze(1).broadcast_to([P, NT, NE]),
                                   ALU.add))
            four = sc[:, :, :].rearrange("p t (g k) -> p k t g", k=NE // NGRP)
            w = [pair[:, j, :, :] for j in range(4)]
            link(dve.tensor_tensor(w[0], four[:, 0], four[:, 1], ALU.max))
            link(dve.tensor_tensor(w[1], four[:, 0], four[:, 1], ALU.min))
            link(dve.tensor_tensor(w[2], four[:, 2], four[:, 3], ALU.max))
            link(dve.tensor_tensor(w[3], four[:, 2], four[:, 3], ALU.min))
            link(dve.tensor_tensor(w[1], w[1], w[3], ALU.max))
            link(dve.tensor_tensor(w[3], w[0], w[2], ALU.min))
            link(dve.tensor_tensor(w[0], w[0], w[2], ALU.max))
            link(dve.tensor_tensor(w[1], w[1], w[3], ALU.max))
            link(dve.tensor_tensor(gsum[:, :, :], w[0], w[1], ALU.add))

            def choose(v, n, k, restart):
                g, e, c = (x[:, :, 0:n] for x in (gt, eq, cum))
                for t in range(NT):
                    ins = dve.max(top8[:, t, :], v[:, t, :])
                link(ins)
                kth = top8[:, :, k - 1:k].broadcast_to([P, NT, n])
                link(dve.tensor_tensor(g, v, kth, ALU.is_gt))
                link(dve.tensor_tensor(e, v, kth, ALU.is_equal))
                link(dve.tensor_reduce(left[:, :], g, AX.X, ALU.add))
                link(dve.tensor_scalar(left[:, :], left[:, :], -1.0, float(k), ALU.mult, ALU.add))
                if n == NE:
                    flat = lambda x: x[:, :, :].rearrange("p t e -> p (t e)")
                    link(dve.tensor_tensor_scan(flat(cum), flat(restart), flat(eq), 0.0, ALU.mult, ALU.add))
                else:
                    flat = lambda x: x[:, 0:2, 0:1]
                    e2 = pair[:, 2, :, :]
                    link(dve.tensor_copy(e2, e))
                    c2 = pair[:, 3, :, :]
                    link(dve.tensor_tensor_scan(c2.rearrange("p t e -> p (t e)"),
                                                restart[:, :, :].rearrange("p t e -> p (t e)"),
                                                e2.rearrange("p t e -> p (t e)"), 0.0, ALU.mult, ALU.add))
                    c = c2
                link(dve.tensor_tensor(c, c, left[:, :].unsqueeze(2).broadcast_to([P, NT, n]), ALU.is_le))
                link(dve.tensor_tensor(e, e, c, ALU.mult))
                link(dve.tensor_tensor(g, g, e, ALU.add))

            choose(gsum[:, :, :], NGRP, TOPG, restart_g)
            link(dve.tensor_tensor(sc[:, :, :].rearrange("p t (g k) -> p t g k", k=NE // NGRP),
                                   sc[:, :, :].rearrange("p t (g k) -> p t g k", k=NE // NGRP),
                                   gt[:, :, 0:NGRP].unsqueeze(3).broadcast_to([P, NT, NGRP, NE // NGRP]), ALU.mult))
            choose(sc[:, :, :], NE, TOPK, restart_e)
            link(dve.tensor_tensor(gt[:, :, :], gt[:, :, :], s0[:, :, :], ALU.mult))
            link(dve.tensor_reduce(left[:, :], gt[:, :, :], AX.X, ALU.add))
            link(dve.tensor_scalar(left[:, :], left[:, :], 1e-20, None, ALU.add))
            link(dve.reciprocal(left[:, :], left[:, :]))
            link(dve.tensor_scalar(left[:, :], left[:, :], ROUTED_SCALE, None, ALU.mult))
            link(dve.tensor_tensor(gt[:, :, :], gt[:, :, :], left[:, :].unsqueeze(2).broadcast_to([P, NT, NE]),
                                   ALU.mult))
            cp = [cparts[:, :, j * NE:(j + 1) * NE] for j in range(PARTS)]
            link(dve.tensor_copy(cp[0], gt[:, :, :]))
            link(dve.tensor_tensor(eq[:, :, :], gt[:, :, :], cp[0], ALU.subtract))
            link(dve.tensor_copy(cp[1], eq[:, :, :]))
            link(dve.tensor_tensor(cp[2], eq[:, :, :], cp[1], ALU.subtract))

            assert steps[0] == ROUTE

            per = 1 + 3 * BT

            def residual(i):
                dve.wait_ge(summed, i + 1)
                dve.tensor_tensor(y[:, :, :], bank[:, 4, :].rearrange("p (t f) -> p t f", t=BT), tiles(X, i),
                                  ALU.add).then_inc(ln_dve, 1)

            def scale(i, has_before):
                for m in range(NC):
                    dve.wait_ge(spread, i * NC + m + 1)
                    dve.wait_ge(relu, i * NCH + m + 1)
                    dve.tensor_tensor(rc[:, m % 3, :], r[:, m % 3, :], bank[:, 2 + m % 2, :], ALU.mult)\
                       .then_inc(scaled, 1)
                    if has_before and m == 1:
                        if not (isinstance(i, int) and i == 1):
                            dve.wait_ge(ln_dve, (i - 1) * per)
                        residual(i - 1)
                    if has_before and m in (2, 3, 5):
                        layernorm_step(m, i - 1)

            def layernorm_step(m, i):
                layernorm(dve, y, X, i, stats, mv, rstd, ln_dve, i * per + 1, ln_pool, 2 * i + 2, seen,
                          steps={2: (0,), 3: (1,), 5: (2,)}[m])

            scale(0, False)
            scale(1, True)
            with dve.Fori(2, NBLK) as i:
                scale(i, True)
            dve.wait_ge(ln_dve, (NBLK - 1) * per)
            residual(NBLK - 1)
            layernorm(dve, y, X, NBLK - 1, stats, mv, rstd, ln_dve, (NBLK - 1) * per + 1, ln_pool,
                      2 * NBLK, seen)


def layernorm(dve, y, X, i, stats, mv, rstd, ln_dve, at, ln_pool, pool_at, seen, steps=(0, 1, 2)):
    if 0 in steps:
        dve.wait_ge(ln_dve, at)
        for t in range(BT):
            dve.bn_stats(stats[:, t, :], y[:, t, :]).then_inc(ln_dve, 1)
    if 1 in steps:
        dve.wait_ge(ln_dve, at + BT)
        dve.tensor_copy(seen[:, :], stats[:, 0, 0:1])
        for t in range(BT):
            dve.bn_aggr(mv[:, t, :], stats[:, t, :]).then_inc(ln_dve, 1)
    if 2 in steps:
        dve.wait_ge(ln_pool, pool_at)
        for t in range(BT):
            xo = X[:, i * BT + t:i * BT + t + 1, :] if isinstance(i, int) else X[:, bass.ds(i * BT + t, 1), :]
            dve.tensor_scalar(xo, y[:, t:t + 1, :], mv[:, t, 0:1], rstd[:, t:t + 1], ALU.subtract, ALU.mult)\
               .then_inc(ln_dve, 1)


def state_space(nc, top, X, ident_f, A_log, B_mat, C_mat, D_vec, W_dt, b_dt):
    with ExitStack() as ctx:
        def sb(name, shape, dt):
            return ctx.enter_context(nc.sbuf_tensor(f"ssm_{name}", shape, dt))

        def sem(name):
            return top.enter_context(nc.semaphore(f"ssm_{name}"))

        N = A_log.shape[1]
        HALF = T // 2
        HT = HALF // P
        QTR = T // 4
        raw_w = sb("raw_w", [D, D], F32)
        w = sb("w", [D, D], F32)
        bias = sb("bias", [D, 1], F32)
        a_log = sb("a_log", [D, N], F32)
        neg_a = sb("neg_a", [D, N + 2], F32)
        rate = sb("rate", [D, 2], F32)
        bmat = sb("bmat", [D, N], F32)
        cmat = sb("cmat", [D, N + 1], F32)
        diag = sb("diag", [D, N + 1, D], F32)
        u = sb("u", [D, T], F32)
        dt = sb("dt", [D, T], F32)
        dtu = sb("dtu", [D, T], F32)
        decay = sb("decay", [D, 2, HALF], F32)
        state = sb("state", [D, 2, HALF], F32)
        y = sb("y", [P, BT, D], F32)
        stats = sb("stats", [P, BT, 6], F32)
        mv = sb("mv", [P, BT, 2], F32)
        rstd = sb("rstd", [P, BT], F32)
        eps = sb("eps", [P, BT], F32)
        seen = sb("seen", [P, 1], F32)
        half_neg = sb("half_neg", [P, BT], F32)
        bank = ctx.enter_context(nc.psum_tensor("ssm_bank", [P, 8, 512], F32))

        loaded = sem("loaded")
        consts = sem("consts")
        turned = sem("turned")
        u_ready = sem("u_ready")
        w_ready = sem("w_ready")
        proj = sem("proj")
        z_ready = sem("z_ready")
        acts = sem("acts")
        softs = sem("softs")
        diags = sem("diags")
        rated = sem("rated")
        decayed = sem("decayed")
        scanned = sem("scanned")
        added = sem("added")
        ln_dve = sem("ln_dve")
        ln_pool = sem("ln_pool")
        block = ctx.enter_context(nc.Block())

        def scratch(c, k):
            buf = (decay, state)[k // 2]
            return buf[:, c % 2, (k % 2) * QTR:(k % 2 + 1) * QTR]

        @block.sync
        def _(sp):
            for dst, src in ((raw_w[:, :], W_dt), (a_log[:, :], A_log), (bmat[:, :], B_mat),
                             (cmat[:, 0:N], C_mat), (cmat[:, N:N + 1], D_vec.rearrange("(p o) -> p o", o=1)),
                             (bias[:, :], b_dt.rearrange("(p o) -> p o", o=1))):
                sp.dma_start(dst, src, allow_slow_non_contiguous=True).then_inc(loaded, 16)

        @block.gpsimd
        def _(pool):
            pool.memset(eps[:, :], EPS).then_inc(consts, 1)
            pool.memset(half_neg[:, :], -0.5).then_inc(consts, 1)
            pool.wait_ge(consts, 2)
            with pool.Fori(0, NBLK) as i:
                pool.wait_ge(ln_dve, i * (1 + 3 * BT) + 1 + 2 * BT)
                pool.tensor_tensor(rstd[:, :], mv[:, :, 1], eps[:, :], ALU.add).then_inc(ln_pool, 1)
                pool.wait_ge(ln_pool, 2 * i + 1)
                pool.tensor_tensor(rstd[:, :], rstd[:, :], half_neg[:, :], ALU.pow).then_inc(ln_pool, 1)

        @block.tensor
        def _(pe):
            for b in range(NBLK):
                for t in range(BT):
                    mm = pe.transpose(bank[:, b, t * P:(t + 1) * P], X[:, b * BT + t, :], ident_f[:, :])
                mm.then_inc(turned, 1)
            pe.wait_ge(loaded, 16 * 6)
            pe.wait_ge(u_ready, 1)
            pe.transpose(bank[:, 0, 0:D], raw_w[:, :], ident_f[:, :]).then_inc(turned, 1)
            pe.wait_ge(w_ready, 1)
            for b in range(NBLK):
                pe.wait_ge(u_ready, b + 1)
                pe.matmul(bank[:, b, :], w[:, :], u[:, b * BLK:(b + 1) * BLK], start=True, stop=True)\
                  .then_inc(proj, 1)
            pe.wait_ge(z_ready, 4)
            pe.wait_ge(diags, 2)

            def weigh(lhs, tile, rhs, first):
                return pe.matmul(bank[:, tile // BT, (tile % BT) * D:(tile % BT + 1) * D], lhs, rhs,
                                 start=first and tile % BT == 0, stop=True, skip_group_check=True)

            for h in range(2):
                for t in range(HT):
                    k = h * HT + t
                    mm = weigh(u[:, k * P:(k + 1) * P], k, diag[:, N, :], True)
                mm.then_inc(added, 1)
            with pe.Fori(0, N) as n:
                for h in range(2):
                    pe.wait_ge(scanned, 2 * n + h + 3)
                    for t in range(HT):
                        mm = weigh(state[:, h, t * P:(t + 1) * P], h * HT + t, diag[:, bass.ds(n, 1), :], False)
                    mm.then_inc(added, 1)

        @block.scalar
        def _(act):
            act.wait_ge(turned, NBLK + 1)
            act.activation(w[:, :], bank[:, 0, 0:D], ACT.Copy).then_inc(w_ready, 1)
            act.wait_ge(loaded, 16 * 6)
            act.activation(neg_a[:, 0:N], a_log[:, :], ACT.Exp).then_inc(w_ready, 1)
            for c in range(4):
                zs = dt[:, c * QTR:(c + 1) * QTR]
                act.wait_ge(z_ready, c + 1)
                if c >= 2:
                    act.wait_ge(softs, 5 * (c - 1))
                act.activation(scratch(c, 0), zs, ACT.Abs).then_inc(acts, 1)
                act.wait_ge(acts, 4 * c + 1)
                act.activation(scratch(c, 0), scratch(c, 0), ACT.Exp, scale=-1.0).then_inc(acts, 1)
                act.wait_ge(softs, 5 * c + 1)
                act.activation(scratch(c, 2), scratch(c, 1), ACT.Ln).then_inc(acts, 1)
                act.wait_ge(acts, 4 * c + 3)
                act.activation(scratch(c, 3), scratch(c, 2), ACT.Exp, scale=-1.0).then_inc(acts, 1)
            with act.Fori(0, N // 2) as i:
                for k in range(2):
                    n = 2 * i + k
                    act.wait_ge(rated, n + 1)
                    for h in range(2):
                        act.wait_ge(scanned, 2 * n + h + 1)
                        act.activation(decay[:, h, :].rearrange("p (b s) -> p b s", s=S)[:, :, 1:S],
                                       dt[:, h * HALF:(h + 1) * HALF].rearrange("p (b s) -> p b s", s=S)[:, :, 1:S],
                                       ACT.Exp, scale=rate[:, k:k + 1]).then_inc(decayed, 1)

        @block.vector
        def _(dve):
            for b in range(NBLK):
                dve.wait_ge(turned, b + 1)
                dve.tensor_copy(u[:, b * BLK:(b + 1) * BLK], bank[:, b, :]).then_inc(u_ready, 1)
            dve.wait_ge(loaded, 16 * 6)
            dve.tensor_tensor(cmat[:, 0:N], cmat[:, 0:N], bmat[:, :], ALU.mult).then_inc(diags, 1)

            def z(c):
                dve.wait_ge(proj, 2 * c + 2)
                dve.tensor_scalar(dt[:, c * QTR:(c + 1) * QTR].rearrange("p (a n) -> p a n", a=2),
                                  bank[:, 2 * c:2 * c + 2, :], bias[:, 0:1], None, ALU.add).then_inc(z_ready, 1)

            z(0)
            z(1)
            dve.wait_ge(diags, 1)
            dve.tensor_tensor(diag[:, :, :], ident_f[:, :].unsqueeze(1).broadcast_to([D, N + 1, D]),
                              cmat[:, :].unsqueeze(2).broadcast_to([D, N + 1, D]), ALU.mult).then_inc(diags, 1)
            dve.wait_ge(w_ready, 2)
            dve.tensor_scalar(neg_a[:, 0:N], neg_a[:, 0:N], -1.0, None, ALU.mult).then_inc(diags, 1)
            dve.memset(neg_a[:, N:N + 2], 0.0).then_inc(diags, 1)
            dve.wait_ge(diags, 4)
            for k in range(2):
                dve.tensor_copy(rate[:, k:k + 1], neg_a[:, k:k + 1]).then_inc(rated, 1)
            z(2)
            z(3)
            dve.wait_ge(u_ready, NBLK)
            for c in range(4):
                cols = slice(c * QTR, (c + 1) * QTR)
                e, one_e, ln, inv = (scratch(c, k) for k in range(4))
                dve.wait_ge(acts, 4 * c + 2)
                dve.tensor_scalar(one_e, e, 1.0, None, ALU.add).then_inc(softs, 1)
                dve.wait_ge(acts, 4 * c + 4)
                dve.wait_ge(softs, 5 * c + 1)
                dve.scalar_tensor_tensor(e, one_e, -1.0, e, ALU.add, ALU.subtract).then_inc(softs, 1)
                dve.scalar_tensor_tensor(dt[:, cols], dt[:, cols], 0.0, ln, ALU.max, ALU.add).then_inc(softs, 1)
                dve.wait_ge(softs, 5 * c + 2)
                dve.tensor_tensor(e, e, inv, ALU.mult).then_inc(softs, 1)
                dve.wait_ge(softs, 5 * c + 4)
                dve.tensor_tensor(dt[:, cols], dt[:, cols], e, ALU.subtract).then_inc(softs, 1)
                dve.wait_ge(softs, 5 * c + 5)
                dve.tensor_tensor(dtu[:, cols], dt[:, cols], u[:, cols], ALU.mult)
            for h in range(2):
                dve.memset(decay[:, h, :].rearrange("p (b s) -> p b s", s=S)[:, :, 0:1], 0.0).then_inc(scanned, 1)
            dve.wait_ge(scanned, 2)
            dve.wait_ge(rated, 2)
            with dve.Fori(0, N // 2) as i:
                for k in range(2):
                    n = 2 * i + k
                    for h in range(2):
                        dve.wait_ge(decayed, 2 * n + h + 1)
                        dve.wait_ge(added, 2 * n + h + 1)
                        dve.tensor_tensor_scan(state[:, h, :], decay[:, h, :], dtu[:, h * HALF:(h + 1) * HALF], 0.0,
                                               ALU.mult, ALU.add).then_inc(scanned, 1)
                    dve.tensor_copy(rate[:, k:k + 1], neg_a[:, bass.ds(n + 2, 1)]).then_inc(rated, 1)
            per = 1 + 3 * BT
            dve.wait_ge(added, 2 * N + 2)
            for i in range(NBLK):
                if i > 0:
                    dve.wait_ge(ln_dve, i * per)
                dve.tensor_tensor(y[:, :, :], bank[:, i, :].rearrange("p (t f) -> p t f", t=BT), tiles(X, i),
                                  ALU.add).then_inc(ln_dve, 1)
                layernorm(dve, y, X, i, stats, mv, rstd, ln_dve, i * per + 1, ln_pool, 2 * i + 2, seen)


def feed_forward(nc, top, X, ident_f, ones_row, W_fc, b_fc, A_fc, B_fc, W_proj, b_proj, A_proj, B_proj):
    with ExitStack() as ctx:
        def sb(name, shape, dt):
            return ctx.enter_context(nc.sbuf_tensor(f"ffn_{name}", shape, dt))

        def sem(name):
            return top.enter_context(nc.semaphore(f"ffn_{name}"))

        F = W_fc.shape[0]
        FC = F // P
        R = A_fc.shape[0]
        QMAX = 127.0
        ROUND = 1.5 * 2.0 ** 23
        raw = sb("raw", [P, 2, FC, P], F32)
        quant = sb("quant", [P, 2, FC, P], F32)
        tmp = sb("tmp", [P, 2, FC, P], F32)
        peak = sb("peak", [P, 2], F32)
        peaks = sb("peaks", [P, 2], F32)
        scale = sb("scale", [P, 2], F32)
        a_fc = sb("a_fc", [R, D], F32)
        b_fc_raw = sb("b_fc_raw", [P, FC, R], F32)
        a_proj = sb("a_proj", [R, F], F32)
        b_proj_raw = sb("b_proj_raw", [D, R], F32)
        bT = sb("bT", [R, F + D], F32)
        bias1 = sb("bias1", [P, FC], F32)
        bias2 = sb("bias2", [1, D], F32)
        w1 = sb("w1", [D, F], F32)
        w2 = sb("w2", [P, FC, D], F32)
        xT = sb("xT", [D, T], F32)
        g = sb("g", [P, 4, BLK], F32)
        y = sb("y", [P, BT, D], F32)
        stats = sb("stats", [P, BT, 6], F32)
        mv = sb("mv", [P, BT, 2], F32)
        rstd = sb("rstd", [P, BT], F32)
        eps = sb("eps", [P, BT], F32)
        seen = sb("seen", [P, 1], F32)
        half_neg = sb("half_neg", [P, BT], F32)
        bank = ctx.enter_context(nc.psum_tensor("ffn_bank", [P, 8, 512], F32))

        loaded = sem("loaded")
        consts = sem("consts")
        q_steps = sem("q_steps")
        peaked = sem("peaked")
        turned = sem("turned")
        took = sem("took")
        hidden = sem("hidden")
        gelus = sem("gelus")
        summed = sem("summed")
        ln_dve = sem("ln_dve")
        ln_pool = sem("ln_pool")
        block = ctx.enter_context(nc.Block())
        LOADS = 8
        QSTEPS = 9

        @block.sync
        def _(sp):
            for dst, src in ((raw[:, 0, :, :], W_fc.rearrange("(c p) i -> p c i", p=P)),
                             (raw[:, 1, :, :].rearrange("p c j -> p (c j)"), W_proj),
                             (a_fc[:, :], A_fc), (b_fc_raw[:, :, :], B_fc.rearrange("(c p) r -> p c r", p=P)),
                             (a_proj[:, :], A_proj), (b_proj_raw[:, :], B_proj),
                             (bias1[:, :], b_fc.rearrange("(c p) -> p c", p=P)),
                             (bias2[:, :], b_proj.rearrange("(o n) -> o n", o=1))):
                sp.dma_start(dst, src, allow_slow_non_contiguous=True).then_inc(loaded, 16)

        @block.gpsimd
        def _(pool):
            pool.memset(eps[:, :], EPS).then_inc(consts, 1)
            pool.memset(half_neg[:, :], -0.5).then_inc(consts, 1)
            pool.wait_ge(q_steps, 1)
            pool.partition_all_reduce(peaks[:, :], peak[:, :], P, bass.bass_isa.ReduceOp.max).then_inc(peaked, 1)
            pool.wait_ge(consts, 2)
            with pool.Fori(0, NBLK) as i:
                pool.wait_ge(ln_dve, i * (1 + 3 * BT) + 1 + 2 * BT)
                pool.tensor_tensor(rstd[:, :], mv[:, :, 1], eps[:, :], ALU.add).then_inc(ln_pool, 1)
                pool.wait_ge(ln_pool, 2 * i + 1)
                pool.tensor_tensor(rstd[:, :], rstd[:, :], half_neg[:, :], ALU.pow).then_inc(ln_pool, 1)

        @block.tensor
        def _(pe):
            for b in range(NBLK):
                for t in range(BT):
                    mm = pe.transpose(bank[:, b, t * P:(t + 1) * P], X[:, b * BT + t, :], ident_f[:, :])
                mm.then_inc(turned, 1)
            pe.wait_ge(loaded, 16 * LOADS)
            pe.wait_ge(took, 2)
            for c in range(FC):
                mm = pe.transpose(bank[0:R, 0, c * P:(c + 1) * P], b_fc_raw[:, c, :], ident_f[:, :])
            mm = pe.transpose(bank[0:R, 1, 0:D], b_proj_raw[:, :], ident_f[:, :])
            mm.then_inc(turned, 1)
            pe.wait_ge(took, NBLK + 2)
            pe.wait_ge(q_steps, QSTEPS)
            for c in range(FC):
                o = bank[:, 2, c * P:(c + 1) * P]
                pe.matmul(o, quant[:, 0, c, :], ident_f[:, :], start=(c == 0), stop=False, skip_group_check=True)
                mm = pe.matmul(o, a_fc[:, :], bT[:, c * P:(c + 1) * P], start=False, stop=True,
                               skip_group_check=True)
            mm.then_inc(turned, 1)
            for c in range(FC):
                o = bank[:, 3, c * D:(c + 1) * D]
                pe.matmul(o, quant[:, 1, c, :], ident_f[:, :], start=(c == 0), stop=False, skip_group_check=True)
                mm = pe.matmul(o, a_proj[:, c * P:(c + 1) * P], bT[:, F:F + D], start=False, stop=True,
                               skip_group_check=True)
            mm.then_inc(turned, 1)
            pe.wait_ge(took, NBLK + 4)

            def block_of(i):
                xb = xT[:, 0:BLK] if isinstance(i, int) else xT[:, bass.ds(i * BLK, BLK)]
                for m in range(FC):
                    pe.matmul(bank[:, m, :], w1[:, m * P:(m + 1) * P], xb, start=True, stop=True)\
                      .then_inc(hidden, 1)
                if not isinstance(i, int):
                    pe.wait_ge(ln_dve, (i - 1) * (1 + 3 * BT) + 1)
                for t in range(BT):
                    pe.matmul(bank[:, 4, t * D:(t + 1) * D], ones_row[:, :], bias2[:, :],
                              start=(t == 0), stop=False, skip_group_check=True)
                for m in range(FC):
                    pe.wait_ge(gelus, i * FC + m + 1)
                    for t in range(BT):
                        mm = pe.matmul(bank[:, 4, t * D:(t + 1) * D], g[:, m, t * P:(t + 1) * P], w2[:, m, :],
                                       start=False, stop=(m == FC - 1), skip_group_check=True)
                mm.then_inc(summed, 1)

            block_of(0)
            with pe.Fori(1, NBLK) as i:
                block_of(i)

        @block.scalar
        def _(act):
            for b in range(NBLK):
                act.wait_ge(turned, b + 1)
                act.activation(xT[:, b * BLK:(b + 1) * BLK], bank[:, b, :], ACT.Copy).then_inc(took, 1)
            act.wait_ge(turned, NBLK + 1)
            act.activation(bT[:, 0:F], bank[0:R, 0, :], ACT.Copy, scale=SCALING).then_inc(took, 1)
            act.activation(bT[:, F:F + D], bank[0:R, 1, 0:D], ACT.Copy, scale=SCALING).then_inc(took, 1)
            act.wait_ge(turned, NBLK + 2)
            act.activation(w1[:, :], bank[:, 2, :], ACT.Copy).then_inc(took, 1)
            act.wait_ge(turned, NBLK + 3)
            act.activation(w2[:, :, :].rearrange("p c n -> p (c n)"), bank[:, 3, :], ACT.Copy).then_inc(took, 1)
            act.wait_ge(loaded, 16 * LOADS)
            with act.Fori(0, NBLK) as i:
                for m in range(FC):
                    act.wait_ge(hidden, i * FC + m + 1)
                    act.activation(g[:, m, :], bank[:, m, :], ACT.Gelu, bias=bias1[:, m:m + 1]).then_inc(gelus, 1)

        @block.vector
        def _(dve):
            steps = [0]

            def link(ins):
                steps[0] += 1
                ins.then_inc(q_steps, 1)
                dve.wait_ge(q_steps, steps[0])

            dve.wait_ge(loaded, 16 * LOADS)
            flat = lambda x: x[:, :, :, :].rearrange("p w c j -> p w (c j)")
            both = lambda x: x[:, :].unsqueeze(2).broadcast_to([P, 2, F])
            link(dve.tensor_reduce(peak[:, :], flat(raw), AX.X, ALU.max, apply_absolute_value=True))
            dve.wait_ge(peaked, 1)
            link(dve.tensor_scalar(scale[:, :], peaks[:, :], 1.0 / QMAX, None, ALU.mult))
            link(dve.reciprocal(peak[:, :], scale[:, :]))
            link(dve.tensor_tensor(flat(quant), flat(raw), both(peak), ALU.mult))
            link(dve.tensor_scalar(quant[:, :, :, :], quant[:, :, :, :], ROUND, -ROUND, ALU.add, ALU.add))
            link(dve.tensor_scalar(quant[:, :, :, :], quant[:, :, :, :], QMAX, -QMAX - 1.0, ALU.min, ALU.max))
            link(dve.tensor_tensor(flat(quant), flat(quant), both(scale), ALU.mult))
            link(dve.tensor_tensor(flat(tmp), flat(quant), flat(raw), ALU.subtract))
            link(dve.tensor_tensor(flat(quant), flat(tmp), flat(raw), ALU.add))
            assert steps[0] == QSTEPS
            per = 1 + 3 * BT
            with dve.Fori(0, NBLK) as i:
                dve.wait_ge(summed, i + 1)
                dve.tensor_tensor(y[:, :, :], bank[:, 4, :].rearrange("p (t f) -> p t f", t=BT), tiles(X, i),
                                  ALU.add).then_inc(ln_dve, 1)
                layernorm(dve, y, X, i, stats, mv, rstd, ln_dve, i * per + 1, ln_pool, 2 * i + 2, seen)
                dve.wait_ge(ln_dve, i * per + per)


def build(nc, a, out):
    with ExitStack() as ctx:
        def sb(name, shape, dt):
            return ctx.enter_context(nc.sbuf_tensor(name, shape, dt))

        X = sb("X", [P, NT, D], F32)
        ident_f = sb("ident_f", [P, P], F32)
        ident_b = sb("ident_b", [P, P], BF16)
        ones_row = sb("ones_row", [1, P], F32)
        fold = sb("fold", [P, PAIR * VR], F32)
        constants(nc, ctx, a["x"], X, ident_f, ident_b, ones_row, fold)
        common = (X, ident_f, ident_b, ones_row, fold)
        attention(nc, ctx, Attention("self", S), *common, None,
                  SelfWeights(a["L0_attn_qkv_w"], a["L0_attn_out_w"], a["L0_attn_out_b"]))
        attention(nc, ctx, Attention("cross0", NKV), *common, a["ctx_768"],
              CrossWeightsIn(*(a["L0_xattn_" + k] for k in
                               ("w_q", "b_q", "w_k", "b_k", "w_v", "b_v", "w_o", "b_o"))))
        experts(nc, ctx, X, ident_f, ident_b, a)
        state_space(nc, ctx, X, ident_f, *(a["L1_attn_" + k] for k in
                                           ("A_log", "B_mat", "C_mat", "D_vec", "W_dt", "b_dt")))
        attention(nc, ctx, Attention("cross1", NKV), *common, a["ctx_768"],
              CrossWeightsOut(*(a["L1_xattn_" + k] for k in ("Wq", "bq", "Wkv", "bkv", "Wo", "bo"))))
        feed_forward(nc, ctx, X, ident_f, ones_row, *(a["L1_ffn_" + k] for k in
                     ("W_fc", "b_fc", "A_fc", "B_fc", "W_proj", "b_proj", "A_proj", "B_proj")))
        store(nc, ctx, X, out)



_INS = ["x", "ctx_768", "L0_attn_qkv_w", "L0_attn_out_w", "L0_attn_out_b", "L0_xattn_w_q", "L0_xattn_b_q",
        "L0_xattn_w_k", "L0_xattn_b_k", "L0_xattn_w_v", "L0_xattn_b_v", "L0_xattn_w_o", "L0_xattn_b_o",
        "L0_ffn_gate_w", "L0_ffn_e_bias", "L0_ffn_up_w", "L0_ffn_down_w", "L0_ffn_shared_up_w",
        "L0_ffn_shared_down_w", "L1_attn_A_log", "L1_attn_B_mat", "L1_attn_C_mat", "L1_attn_D_vec",
        "L1_attn_W_dt", "L1_attn_b_dt", "L1_xattn_Wq", "L1_xattn_bq", "L1_xattn_Wkv", "L1_xattn_bkv",
        "L1_xattn_Wo", "L1_xattn_bo", "L1_ffn_W_fc", "L1_ffn_b_fc", "L1_ffn_A_fc", "L1_ffn_B_fc",
        "L1_ffn_W_proj", "L1_ffn_b_proj", "L1_ffn_A_proj", "L1_ffn_B_proj"]


def kernel(**inputs):
    import numpy as _np
    import concourse.bacc as _bacc
    from concourse import mybir as _mybir
    from concourse.bass_utils import run_bass_kernel_spmd as _run

    nc = _bacc.Bacc("TRN2", target_bir_lowering=False, num_devices=1)
    arrays, args = {}, {}
    for name in _INS:
        a = _np.ascontiguousarray(inputs[name])
        arrays[f"in_{name}_dram"] = a
        args[name] = nc.dram_tensor(f"in_{name}_dram", a.shape, _mybir.dt.from_np(a.dtype),
                                    kind="ExternalInput").ap()
    out = nc.dram_tensor("out_dram", arrays["in_x_dram"].shape, _mybir.dt.float32, kind="ExternalOutput").ap()
    build(nc, args, out)
    r = _run(nc, [arrays], core_ids=[0])
    return r.results[0]["out_dram"]
```
